# Optimizing a Trainium2 kernel written in Bass

```python
import numpy as np
import jax
import jax.numpy as jnp

def _softmax(x, axis=-1):
    return jax.nn.softmax(x, axis=axis)

def _gelu(x):
    return jax.nn.gelu(x, approximate=True)

def _silu(x):
    return jax.nn.silu(x)

def _sigmoid(x):
    return jax.nn.sigmoid(x)

def _layernorm(x, axis=-1, eps=1e-05):
    m = jnp.mean(x, axis=axis, keepdims=True)
    v = jnp.var(x, axis=axis, keepdims=True)
    return (x - m) / jnp.sqrt(v + eps)

def _scatter_add(tgt, idx, src, axis=0):
    return tgt.at[idx].add(src)

def _segment_sum(src, seg, n):
    return jax.ops.segment_sum(src, seg, n)
kernel_name = 'mk_gnn_resnorm_d2_gnn_r8_1f0eac'

def setup_inputs(seed: int=0):
    np.random.seed(seed)
    _w = jnp.asarray

    def _rec_inputs():
        import jax
        import jax.numpy as jnp
        _gk = jax.random.key(seed)
        x = -0.0002117 + 1 * jax.random.normal(jax.random.fold_in(_gk, 1), (6250, 256), jnp.float32)
        _s = jax.random.randint(jax.random.fold_in(_gk, 2), (100000,), 0, 6250, jnp.int32)
        _d = jax.random.randint(jax.random.fold_in(_gk, 3), (100000,), 0, 6250, jnp.int32)
        _loop = jnp.arange(6250, dtype=jnp.int32)
        src = jnp.concatenate([_s, _d, _loop])
        dst = jnp.concatenate([_d, _s, _loop])
        _o = jnp.argsort(dst, stable=True)
        src = src[_o]
        dst = dst[_o]
        return (x, src, dst)
    x, src, dst = _rec_inputs()

    def _L0_gnn_setup():
        import jax, jax.numpy as jnp
        import numpy as np
        N_NODES = 12500
        N_EDGES = 37500
        D_MODEL = 256
        N_HEADS = 8
        D_HEAD = D_MODEL // N_HEADS

        def _layernorm(x, w, b, eps=1e-05):
            mu = jnp.mean(x, axis=-1, keepdims=True)
            var = jnp.var(x, axis=-1, keepdims=True)
            return (x - mu) * jax.lax.rsqrt(var + eps) * w + b
        key = jax.random.key(seed)
        ks = jax.random.split(key, 16)
        d, h = (D_MODEL, D_MODEL)
        s = 1.0 / np.sqrt(d)
        inp = {'x': jax.random.normal(ks[0], (N_NODES, d), dtype=jnp.float32), 'edge_index': jax.random.randint(ks[1], (2, N_EDGES), 0, N_NODES, dtype=jnp.int64), 'Wq': jax.random.normal(ks[2], (d, d), dtype=jnp.float32) * s, 'Wk': jax.random.normal(ks[3], (d, d), dtype=jnp.float32) * s, 'Wv': jax.random.normal(ks[4], (d, d), dtype=jnp.float32) * s, 'O_w': jax.random.normal(ks[5], (d, d), dtype=jnp.float32) * s, 'O_b': jnp.zeros((d,), dtype=jnp.float32), 'ln1_w': jnp.ones((d,), dtype=jnp.float32), 'ln1_b': jnp.zeros((d,), dtype=jnp.float32), 'f1_w': jax.random.normal(ks[6], (d, 2 * d), dtype=jnp.float32) * s, 'f1_b': jnp.zeros((2 * d,), dtype=jnp.float32), 'f2_w': jax.random.normal(ks[7], (2 * d, d), dtype=jnp.float32) / np.sqrt(2 * d), 'f2_b': jnp.zeros((d,), dtype=jnp.float32), 'ln2_w': jnp.ones((d,), dtype=jnp.float32), 'ln2_b': jnp.zeros((d,), dtype=jnp.float32), 'gru_w_ih': jax.random.normal(ks[8], (d, 3 * h), dtype=jnp.float32) * s, 'gru_w_hh': jax.random.normal(ks[9], (h, 3 * h), dtype=jnp.float32) * s, 'gru_b_ih': jnp.zeros((3 * h,), dtype=jnp.float32), 'gru_b_hh': jnp.zeros((3 * h,), dtype=jnp.float32)}
        return inp
    _L0_gnn_all = _L0_gnn_setup()
    _L0_gnn_in = {k: v for k, v in _L0_gnn_all.items() if k in ('Wq', 'Wk', 'Wv', 'O_w', 'O_b', 'ln1_w', 'ln1_b', 'f1_w', 'f1_b', 'f2_w', 'f2_b', 'ln2_w', 'ln2_b', 'gru_w_ih', 'gru_w_hh', 'gru_b_ih', 'gru_b_hh')}
    del _L0_gnn_all

    def _L1_gnn_setup():
        import jax, jax.numpy as jnp
        import numpy as np
        N = 6250
        E_RAND = 100000
        F_IN = 256
        F_OUT = 256
        ALPHA = 0.2
        key = jax.random.key(seed)
        k1, k2, k3, k4 = jax.random.split(key, 4)
        x = jax.random.normal(k1, (N, F_IN), dtype=jnp.float32)
        edge_rand = jax.random.randint(k2, (2, E_RAND), 0, N)
        loops = jnp.arange(N)
        edge = jnp.concatenate([edge_rand, jnp.stack([loops, loops])], axis=1)
        W = jax.random.normal(k3, (F_IN, F_OUT), dtype=jnp.float32) * 0.05
        a = jax.random.normal(k4, (2 * F_OUT,), dtype=jnp.float32) * 0.05
        return {'x': x, 'edge': edge, 'W': W, 'a': a}
    _L1_gnn_all = _L1_gnn_setup()
    _L1_gnn_in = {k: v for k, v in _L1_gnn_all.items() if k in ('W', 'a')}
    del _L1_gnn_all
    return {'x': x, 'src': src, 'dst': dst, 'L0_gnn_Wq': _L0_gnn_in['Wq'], 'L0_gnn_Wk': _L0_gnn_in['Wk'], 'L0_gnn_Wv': _L0_gnn_in['Wv'], 'L0_gnn_O_w': _L0_gnn_in['O_w'], 'L0_gnn_O_b': _L0_gnn_in['O_b'], 'L0_gnn_ln1_w': _L0_gnn_in['ln1_w'], 'L0_gnn_ln1_b': _L0_gnn_in['ln1_b'], 'L0_gnn_f1_w': _L0_gnn_in['f1_w'], 'L0_gnn_f1_b': _L0_gnn_in['f1_b'], 'L0_gnn_f2_w': _L0_gnn_in['f2_w'], 'L0_gnn_f2_b': _L0_gnn_in['f2_b'], 'L0_gnn_ln2_w': _L0_gnn_in['ln2_w'], 'L0_gnn_ln2_b': _L0_gnn_in['ln2_b'], 'L0_gnn_gru_w_ih': _L0_gnn_in['gru_w_ih'], 'L0_gnn_gru_w_hh': _L0_gnn_in['gru_w_hh'], 'L0_gnn_gru_b_ih': _L0_gnn_in['gru_b_ih'], 'L0_gnn_gru_b_hh': _L0_gnn_in['gru_b_hh'], 'L1_gnn_W': _L1_gnn_in['W'], 'L1_gnn_a': _L1_gnn_in['a']}

def reference(x, src, dst, L0_gnn_Wq, L0_gnn_Wk, L0_gnn_Wv, L0_gnn_O_w, L0_gnn_O_b, L0_gnn_ln1_w, L0_gnn_ln1_b, L0_gnn_f1_w, L0_gnn_f1_b, L0_gnn_f2_w, L0_gnn_f2_b, L0_gnn_ln2_w, L0_gnn_ln2_b, L0_gnn_gru_w_ih, L0_gnn_gru_w_hh, L0_gnn_gru_b_ih, L0_gnn_gru_b_hh, L1_gnn_W, L1_gnn_a):
    import jax
    import jax.numpy as jnp

    def _L0_gnn_ref(x, edge_index, Wq, Wk, Wv, O_w, O_b, ln1_w, ln1_b, f1_w, f1_b, f2_w, f2_b, ln2_w, ln2_b, gru_w_ih, gru_w_hh, gru_b_ih, gru_b_hh):
        import jax, jax.numpy as jnp
        import numpy as np
        N_NODES = 12500
        N_EDGES = 37500
        D_MODEL = 256
        N_HEADS = 8
        D_HEAD = D_MODEL // N_HEADS

        def _layernorm(x, w, b, eps=1e-05):
            mu = jnp.mean(x, axis=-1, keepdims=True)
            var = jnp.var(x, axis=-1, keepdims=True)
            return (x - mu) * jax.lax.rsqrt(var + eps) * w + b
        N = x.shape[0]
        H, D = (N_HEADS, D_HEAD)
        Q = (x @ Wq).reshape(N, H, D)
        K = (x @ Wk).reshape(N, H, D)
        V = (x @ Wv).reshape(N, H, D)
        score = jnp.einsum('nhd,ngd->nhg', Q, K) / np.sqrt(D)
        score = jax.nn.softmax(score, axis=-1)
        x1 = jnp.einsum('nhg,ngd->nhd', score, V).reshape(N, H * D)
        src, dst = (edge_index[0], edge_index[1])
        msg = x1[dst] * x1[src]
        attn_out = jax.ops.segment_sum(msg, dst, num_segments=N)
        h = attn_out @ O_w + O_b
        h = x + h
        h = _layernorm(h, ln1_w, ln1_b)
        ffn = jax.nn.relu(h @ f1_w + f1_b) @ f2_w + f2_b
        h = _layernorm(h + ffn, ln2_w, ln2_b)
        gi = h @ gru_w_ih + gru_b_ih
        gh = h @ gru_w_hh + gru_b_hh
        gi_r, gi_z, gi_n = jnp.split(gi, 3, axis=-1)
        gh_r, gh_z, gh_n = jnp.split(gh, 3, axis=-1)
        r = jax.nn.sigmoid(gi_r + gh_r)
        z = jax.nn.sigmoid(gi_z + gh_z)
        n = jnp.tanh(gi_n + r * gh_n)
        return (1.0 - z) * n + z * h

    def _L1_gnn_ref(x, edge, W, a):
        import jax, jax.numpy as jnp
        import numpy as np
        N = 6250
        E_RAND = 100000
        F_IN = 256
        F_OUT = 256
        ALPHA = 0.2
        n = x.shape[0]
        f_out = W.shape[1]
        h = x @ W
        src, dst = (edge[0], edge[1])
        s = h @ a[:f_out]
        t = h @ a[f_out:]
        logit = s[src] + t[dst]
        e = jnp.exp(-jax.nn.leaky_relu(logit, ALPHA))
        rowsum = jax.ops.segment_sum(e, src, num_segments=n)
        msg = e[:, None] * h[dst]
        h_prime = jax.ops.segment_sum(msg, src, num_segments=n)
        h_prime = h_prime / rowsum[:, None]
        return jax.nn.relu(h_prime)
    edge_index = jnp.stack([src, dst])
    x = _layernorm(x + _L0_gnn_ref(x, edge_index, L0_gnn_Wq, L0_gnn_Wk, L0_gnn_Wv, L0_gnn_O_w, L0_gnn_O_b, L0_gnn_ln1_w, L0_gnn_ln1_b, L0_gnn_f1_w, L0_gnn_f1_b, L0_gnn_f2_w, L0_gnn_f2_b, L0_gnn_ln2_w, L0_gnn_ln2_b, L0_gnn_gru_w_ih, L0_gnn_gru_w_hh, L0_gnn_gru_b_ih, L0_gnn_gru_b_hh), axis=-1)
    x = _layernorm(x + _L1_gnn_ref(x, edge_index, L1_gnn_W, L1_gnn_a), axis=-1)
    return x

_drawn_inputs = setup_inputs


def setup_inputs(seed=0):
    import zlib

    import numpy as np

    out = dict(_drawn_inputs(seed))
    spreads = {'L0_gnn_O_b': (0.0, 0.1),
     'L0_gnn_ln1_w': (1.0, 0.2),
     'L0_gnn_ln1_b': (0.0, 0.1),
     'L0_gnn_f1_b': (0.0, 0.1),
     'L0_gnn_f2_b': (0.0, 0.1),
     'L0_gnn_ln2_w': (1.0, 0.2),
     'L0_gnn_ln2_b': (0.0, 0.1),
     'L0_gnn_gru_b_ih': (0.0, 0.1),
     'L0_gnn_gru_b_hh': (0.0, 0.338)}
    factors = {}
    for name, (base, spread) in spreads.items():
        noise = np.random.default_rng([zlib.crc32(name.encode()), seed]).standard_normal(out[name].shape)
        drawn = base * np.exp(spread * noise) if base else spread * noise
        out[name] = jnp.asarray(drawn.astype(out[name].dtype))
    for name, factor in factors.items():
        out[name] = (out[name] * factor).astype(out[name].dtype)
    return out
```

```python
from contextlib import ExitStack

import numpy as np

import concourse.bass as bass
from concourse import mybir

F32 = mybir.dt.float32
BF16 = mybir.dt.bfloat16
F16 = mybir.dt.float16
I32 = mybir.dt.int32
ALU = mybir.AluOpType
ACT = mybir.ActivationFunctionType
AX = mybir.AxisListType

P = 128
N_NODES = 6250
N_EDGES = 206250
D = 256
KC = D // P
N_HEADS = 8
D_HEAD = D // N_HEADS
D_FFN = 2 * D
FC = D_FFN // P
TILES = -(-N_NODES // P)
GROUP = 7
GROUPS = TILES // GROUP
HALF = GROUP * P // 2
ROWS = TILES * P
TRASH = ROWS
EDGE_TILES = -(-N_EDGES // P)
EDGES = EDGE_TILES * P
HT = D + 2
EPS = 1e-5
SCORE_SCALE = float(D_HEAD) ** -0.5
ALPHA = 0.2
TINY = 1.2e-38

assert TILES == GROUPS * GROUP


def before(g, n, slots):
    return GROUP * g + max(0, n - slots + 1)


def upto(g, n):
    return GROUP * g + n + 1


def tile_rows(g, n):
    return bass.ds(g * (GROUP * P) + n * P, P)


class Kit:

    def __init__(self, nc, ctx):
        self.nc, self.ctx = nc, ctx

    def sb(self, name, shape, dt=F32):
        return self.ctx.enter_context(self.nc.sbuf_tensor(name, shape, dt))

    def ps(self, name, shape, dt=F32):
        return self.ctx.enter_context(self.nc.psum_tensor(name, shape, dt))

    def sem(self, name):
        return self.ctx.enter_context(self.nc.semaphore(name))


def load_constants(nc, kit, w):
    c = {}
    c["ident"] = kit.sb("ident", [P, P])
    c["wqkv"] = kit.sb("wqkv", [P, KC, 3 * D])
    c["wo"] = kit.sb("wo", [P, KC, D])
    c["f1"] = kit.sb("f1", [P, KC, D_FFN])
    c["f2"] = kit.sb("f2", [P, FC, D])
    c["gru"] = kit.sb("gru", [P, KC, 4 * D])
    c["w1"] = kit.sb("w1", [P, KC, HT])
    c["rows"] = kit.sb("rows", [P, 6, D])
    c["f1_b"] = kit.sb("f1_bias", [P, FC])
    c["bih"] = kit.sb("bih", [P, 6])
    c["bhh"] = kit.sb("bhh", [P, 6])
    c["brz"] = kit.sb("brz", [P, 4])
    c["a"] = kit.sb("a_bc", [P, 2, D])
    c["half"] = kit.sb("minus_half", [P, 1])
    with ExitStack() as tmp:
        whh = tmp.enter_context(nc.sbuf_tensor("whh", [P, KC, 3 * D], F32))
        junk = tmp.enter_context(nc.sbuf_tensor("wa_products", [P, D], F32))
        loaded = kit.sem("weights_loaded")
        id_zero, folded = kit.sem("ident_zeroed"), kit.sem("weights_folded")
        with nc.Block() as block:

            @block.sync
            def _(sp):
                def split(ap):
                    return ap.rearrange("(k p) n -> p k n", p=P)

                n = 0
                for name, dst in (("Wq", c["wqkv"][:, :, 0:D]), ("Wk", c["wqkv"][:, :, D:2 * D]),
                                  ("Wv", c["wqkv"][:, :, 2 * D:3 * D]), ("O_w", c["wo"][:]), ("f1_w", c["f1"][:]),
                                  ("f2_w", c["f2"][:]), ("gru_w_hh", whh[:]), ("L1_W", c["w1"][:, :, 0:D])):
                    sp.dma_start(dst, split(w[name])).then_inc(loaded, 16)
                    n += 1
                sp.dma_start(c["gru"][:, :, 0:3 * D], split(w["gru_w_ih"])).then_inc(loaded, 16)
                for j, name in enumerate(("O_b", "ln1_w", "ln1_b", "f2_b", "ln2_w", "ln2_b")):
                    sp.dma_start(c["rows"][:, j, :], w[name].partition_broadcast(P)).then_inc(loaded, 16)
                sp.dma_start(c["a"][:].rearrange("p a b -> p (a b)"), w["L1_a"].partition_broadcast(P)).then_inc(loaded, 16)
                for name, m in (("f1_b", FC), ("bih", 6), ("bhh", 6)):
                    src = w[{"f1_b": "f1_b", "bih": "gru_b_ih", "bhh": "gru_b_hh"}[name]]
                    with nc.allow_non_contiguous_dma("a few hundred bias values, once"):
                        sp.dma_start(c[name][:], src.rearrange("(m p) -> p m", p=P)).then_inc(loaded, 16)
                sp.wait_ge(loaded, 16 * 19)

            @block.gpsimd
            def _(pool):
                nc.gpsimd.memset(c["ident"][:], 0.0).then_inc(id_zero, 1)
                nc.gpsimd.memset(c["half"][:], -0.5)
                pool.wait_ge(id_zero, 1)
                nc.gpsimd.affine_select(out=c["ident"][:], in_=c["ident"][:], compare_op=ALU.not_equal, fill=1.0,
                                        base=0, pattern=[[-1, P]], channel_multiplier=1)

            @block.vector
            def _(dve):
                dve.wait_ge(loaded, 16 * 19)
                g = c["gru"]
                nc.vector.tensor_copy(g[:, :, 3 * D:4 * D], whh[:, :, 2 * D:3 * D])
                nc.vector.tensor_tensor(g[:, :, 0:2 * D], g[:, :, 0:2 * D], whh[:, :, 0:2 * D], ALU.add)
                nc.vector.tensor_tensor(c["brz"][:], c["bih"][:, 0:4], c["bhh"][:, 0:4], ALU.add)
                n = 0
                for k in range(KC):
                    for j in range(2):
                        nc.vector.tensor_tensor(junk[:], c["w1"][:, k, 0:D], c["a"][:, j, :],
                                                ALU.mult).then_inc(folded, 1)
                        n += 1
                        dve.wait_ge(folded, n)
                        nc.vector.tensor_reduce(c["w1"][:, k, D + j:D + j + 1], junk[:], AX.X,
                                                ALU.add).then_inc(folded, 1)
                        n += 1
                        dve.wait_ge(folded, n)
    return c


def attention_rows(nc, kit, c, x, x1_out):
    with ExitStack() as tmp:
        def sb(name, shape, dt=F32):
            return tmp.enter_context(nc.sbuf_tensor(name, shape, dt))

        xt = sb("qx", [P, GROUP, D])
        xT = sb("qxT", [P, D])
        qk = sb("qk", [P, 2, 2 * D])
        v = sb("v", [P, GROUP, D])
        prod = sb("qk_products", [P, N_HEADS, N_HEADS, D_HEAD])
        av = sb("av_products", [P, 2, N_HEADS, D_HEAD, N_HEADS])
        sc = sb("scores", [P, 2, N_HEADS, N_HEADS])
        mx = sb("score_max", [P, N_HEADS])
        sm = sb("prob_sum", [P, N_HEADS])
        rs = sb("prob_rsum", [P, N_HEADS])
        x1 = sb("x1_tile", [P, GROUP, D])
        tp = tmp.enter_context(nc.psum_tensor("q_tp", [P, D], F32))
        pqk = tmp.enter_context(nc.psum_tensor("p_qk", [P, 2 * D], F32))
        pv = tmp.enter_context(nc.psum_tensor("p_v", [P, D], F32))

        x_loaded = [kit.sem(f"q_x_loaded{n}") for n in range(GROUP)]
        xT_in_psum, xT_ready = kit.sem("q_xT_in_psum"), kit.sem("q_xT_ready")
        qkv_in_psum, qk_ready, v_ready = kit.sem("qkv_in_psum"), kit.sem("qk_ready"), kit.sem("v_ready")
        products, reduced, maxed = kit.sem("qk_products_done"), kit.sem("scores_reduced"), kit.sem("scores_maxed")
        shifted, exped = kit.sem("scores_shifted"), kit.sem("scores_exped")
        summed, inverted, probs = kit.sem("probs_summed"), kit.sem("probs_inverted"), kit.sem("probs_ready")
        av_ready, x1_ready = kit.sem("av_products_ready"), kit.sem("x1_ready")
        x1_stored = [kit.sem(f"x1_stored{n}") for n in range(GROUP)]

        with nc.Block() as block:

            @block.sync
            def _(sp):
                with sp.Fori(0, GROUPS) as g:
                    for n in range(GROUP):
                        sp.wait_ge(xT_in_psum, before(g, n, GROUP))
                        sp.dma_start(xt[:, n, :], x[tile_rows(g, n), :]).then_inc(x_loaded[n], 16)

            @block.tensor
            def _(pe):
                with pe.Fori(0, GROUPS) as g:
                    for n in range(GROUP):
                        pe.wait_ge(x_loaded[n], 16 * g + 16)
                        for k in range(KC):
                            last = nc.tensor.transpose(tp[:, k * P:(k + 1) * P], xt[:, n, k * P:(k + 1) * P],
                                                       c["ident"][:])
                        last.then_inc(xT_in_psum, 1)
                        pe.wait_ge(xT_ready, upto(g, n))
                        pe.wait_ge(v_ready, GROUP * g + n)
                        for k in range(KC):
                            nc.tensor.matmul(pqk[:], xT[:, k * P:(k + 1) * P], c["wqkv"][:, k, 0:2 * D],
                                             start=(k == 0), stop=(k == KC - 1))
                        for k in range(KC):
                            last = nc.tensor.matmul(pv[:], xT[:, k * P:(k + 1) * P], c["wqkv"][:, k, 2 * D:3 * D],
                                                    start=(k == 0), stop=(k == KC - 1))
                        last.then_inc(qkv_in_psum, 1)

            @block.scalar
            def _(act):
                def exp_of(g, n):
                    act.wait_ge(shifted, upto(g, n))
                    nc.scalar.activation(sc[:, n % 2], sc[:, n % 2], ACT.Exp, scale=SCORE_SCALE).then_inc(exped, 1)

                def store_of(g, n):
                    act.wait_ge(x1_ready, upto(g, n))
                    act.dma_start(x1_out[tile_rows(g, n), :], x1[:, n, :]).then_inc(x1_stored[n], 16)

                with act.Fori(0, GROUPS) as g:
                    for n in range(GROUP):
                        act.wait_ge(xT_in_psum, upto(g, n))
                        act.wait_ge(qkv_in_psum, GROUP * g + n)
                        nc.scalar.copy(xT[:], tp[:]).then_inc(xT_ready, 1)
                        act.wait_ge(qkv_in_psum, upto(g, n))
                        act.wait_ge(products, before(g, n, 2))
                        nc.scalar.copy(qk[:, n % 2, :], pqk[:]).then_inc(qk_ready, 1)
                        act.wait_ge(av_ready, before(g, n, GROUP))
                        nc.scalar.copy(v[:, n, :], pv[:]).then_inc(v_ready, 1)
                        if n >= 1:
                            exp_of(g, n - 1)
                        if n >= 2:
                            store_of(g, n - 2)
                    exp_of(g, GROUP - 1)
                    store_of(g, GROUP - 2)
                    store_of(g, GROUP - 1)
                for n in range(GROUP):
                    act.wait_ge(x1_stored[n], 16 * GROUPS)

            @block.gpsimd
            def _(pool):
                with pool.Fori(0, GROUPS) as g:
                    for n in range(GROUP):
                        pool.wait_ge(v_ready, upto(g, n))
                        pool.wait_ge(probs, upto(g, n))
                        pool.wait_ge(x1_ready, before(g, n, 2))
                        p_b = sc[:, n % 2].unsqueeze(2).broadcast_to([P, N_HEADS, D_HEAD, N_HEADS])
                        v_b = v[:, n, :].rearrange("p (g d) -> p d g", g=N_HEADS).unsqueeze(1) \
                            .broadcast_to([P, N_HEADS, D_HEAD, N_HEADS])
                        nc.gpsimd.tensor_tensor(av[:, n % 2], p_b, v_b, ALU.mult).then_inc(av_ready, 1)

            @block.vector
            def _(dve):
                def sum_av(g, n):
                    dve.wait_ge(av_ready, upto(g, n))
                    dve.wait_ge(x1_stored[n], 16 * g)
                    nc.vector.tensor_reduce(x1[:, n, :], av[:, n % 2].rearrange("p h d g -> p (h d) g"), AX.X,
                                            ALU.add).then_inc(x1_ready, 1)

                with dve.Fori(0, GROUPS) as g:
                    for n in range(GROUP):
                        done = upto(g, n)
                        dve.wait_ge(qk_ready, done)
                        q_b = qk[:, n % 2, 0:D].rearrange("p (h d) -> p h d", h=N_HEADS).unsqueeze(2) \
                            .broadcast_to([P, N_HEADS, N_HEADS, D_HEAD])
                        k_b = qk[:, n % 2, D:2 * D].rearrange("p (h d) -> p h d", h=N_HEADS).unsqueeze(1) \
                            .broadcast_to([P, N_HEADS, N_HEADS, D_HEAD])
                        nc.vector.tensor_tensor(prod[:], q_b, k_b, ALU.mult).then_inc(products, 1)
                        dve.wait_ge(products, done)
                        dve.wait_ge(av_ready, before(g, n, 2))
                        nc.vector.tensor_reduce(sc[:, n % 2], prod[:], AX.X, ALU.add).then_inc(reduced, 1)
                        dve.wait_ge(reduced, done)
                        dve.wait_ge(shifted, GROUP * g + n)
                        nc.vector.tensor_reduce(mx[:], sc[:, n % 2], AX.X, ALU.max).then_inc(maxed, 1)
                        dve.wait_ge(maxed, done)
                        nc.vector.tensor_tensor(sc[:, n % 2], sc[:, n % 2],
                                                mx[:].unsqueeze(2).broadcast_to([P, N_HEADS, N_HEADS]),
                                                ALU.subtract).then_inc(shifted, 1)
                        if n >= 1:
                            sum_av(g, n - 1)
                        dve.wait_ge(exped, done)
                        dve.wait_ge(probs, GROUP * g + n)
                        nc.vector.tensor_reduce(sm[:], sc[:, n % 2], AX.X, ALU.add).then_inc(summed, 1)
                        dve.wait_ge(summed, done)
                        nc.vector.reciprocal(rs[:], sm[:]).then_inc(inverted, 1)
                        dve.wait_ge(inverted, done)
                        nc.vector.tensor_tensor(sc[:, n % 2], sc[:, n % 2],
                                                rs[:].unsqueeze(2).broadcast_to([P, N_HEADS, N_HEADS]),
                                                ALU.mult).then_inc(probs, 1)
                    sum_av(g, GROUP - 1)


def hold(eng, sem, value):
    value = eng.snap(eng.to_reg(value))
    eng.wait_ge(sem, 1)
    eng.wait_ge(sem, value)


def group_rows(g):
    return bass.ds(g * (GROUP * P), GROUP * P)


def update_rows(nc, kit, c, x, x1, agg, xmid_out, table_out):
    with ExitStack() as tmp:
        def sb(name, shape, dt=F32):
            return tmp.enter_context(nc.sbuf_tensor(name, shape, dt))

        def ps(name, shape):
            return tmp.enter_context(nc.psum_tensor(name, shape, F32))

        xt, x1t, agt = (sb(f"u_{s}", [P, GROUP, D]) for s in ("x", "x1", "agg"))
        at, xb, h, h1, hb = (sb(f"u_{s}", [P, GROUP, D]) for s in ("attn", "x_plus_bias", "h", "h1", "h1_plus_bias"))
        bk, xm = sb("u_gru_rows", [P, GROUP, D]), sb("u_xmid", [P, GROUP, D])
        ht = sb("u_table", [P, GROUP, HT])
        tT = sb("u_attnT", [P, KC, GROUP * P])
        hT = sb("u_hT", [P, KC, GROUP * P])
        gT = sb("u_hiddenT", [P, FC, GROUP * P])
        rT, zT, nT = (sb(f"u_{s}T", [P, KC, GROUP * P]) for s in "rzn")
        stats, mv = sb("u_stats", [P, nc.vector.BN_STATS_DIM]), sb("u_mean_var", [P, GROUP, 2])
        ve, rs = sb("u_var_eps", [P, GROUP]), sb("u_rstd", [P, GROUP])
        tp, mo, hf = ps("u_tp", [P, 2, 512]), ps("u_mo", [P, 2, 512]), ps("u_hf", [P, 4, 512])

        x_in, x1_in, agg_in = kit.sem("u_x_loaded"), kit.sem("u_x1_loaded"), kit.sem("u_agg_loaded")
        stored = [kit.sem("xmid_stored"), kit.sem("table_stored")]
        attn_ready, xb_ready = kit.sem("attn_ready"), kit.sem("x_plus_bias_ready")
        tp_full, tp_out = kit.sem("u_tp_full"), kit.sem("u_tp_evacuated")
        mo_full, resid = kit.sem("u_mo_full"), kit.sem("u_residual_added")
        ht_ready = kit.sem("table_row_ready")
        hf_full, relued = kit.sem("u_hf_full"), kit.sem("u_hidden_relued")
        gates, new_pre, new_ready, o_ready = (kit.sem(s) for s in ("gates_ready", "new_gate_summed", "new_gate_ready",
                                                                    "gru_out_ready"))
        var_ready, rstd_ready, normed = kit.sem("var_ready"), kit.sem("rstd_ready"), kit.sem("rows_normed")
        h1_ready, hb_ready, h2_ready, xm_ready = (kit.sem(s) for s in ("h1_ready", "h1_plus_bias_ready", "h2_ready",
                                                                       "xmid_ready"))
        stats_ready, mean_ready, y_summed = kit.sem("u_stats_ready"), kit.sem("u_mean_ready"), kit.sem("gru_plus_x_summed")
        scaled, reset_applied = kit.sem("rows_scaled"), kit.sem("reset_gate_applied")
        h_less_n, z_applied = kit.sem("h_less_n"), kit.sem("update_gate_applied")
        TP, MO, HF = 5 * GROUP, 3 * GROUP, 24
        REL, GAT, GQ = 2 * FC, 2 * 2 * KC, 2 * KC

        with nc.Block() as block:

            @block.sync
            def _(sp):
                with sp.Fori(0, GROUPS) as g:
                    for dst, src, sem, free in ((x1t, x1, x1_in, attn_ready), (agt, agg, agg_in, attn_ready),
                                                (xt, x, x_in, xm_ready)):
                        sp.wait_ge(free, GROUP * g)
                        sp.dma_start(dst[:], src[group_rows(g), 0:D].rearrange("(n p) d -> p n d", p=P)).then_inc(sem, 16)

            @block.tensor
            def _(pe):
                def turn(g, use, src):
                    pe.wait_ge(tp_out, TP * g + max(0, use - 1))
                    for k in range(KC):
                        last = nc.tensor.transpose(tp[:, use % 2, k * P:(k + 1) * P], src(k), c["ident"][:])
                    last.then_inc(tp_full, 1)

                def rows_matmul(use, lhsT, rhs, chunks, cols):
                    for k in range(chunks):
                        last = nc.tensor.matmul(mo[:, use % 2, 0:cols], lhsT(k), rhs(k), start=(k == 0),
                                                stop=(k == chunks - 1))
                    last.then_inc(mo_full, 1)

                def half_matmul(slot, w, col, src, half):
                    for k in range(KC):
                        last = nc.tensor.matmul(hf[:, slot, 0:HALF], w[:, k, col:col + P],
                                                src[:, k, half * HALF:(half + 1) * HALF],
                                                start=(k == 0), stop=(k == KC - 1))
                    last.then_inc(hf_full, 1)

                with pe.Fori(0, GROUPS) as g:
                    for n in range(GROUP):
                        pe.wait_ge(attn_ready, upto(g, n))
                        turn(g, n, lambda k: at[:, n, k * P:(k + 1) * P])
                        pe.wait_ge(tp_out, TP * g + n + 1)
                        if n < 2:
                            pe.wait_ge(ht_ready, GROUP * g)
                        else:
                            pe.wait_ge(resid, 2 * GROUP * g + n - 1)
                        rows_matmul(n, lambda k: tT[:, k, n * P:(n + 1) * P], lambda k: c["wo"][:, k, :], KC, D)
                    for n in range(GROUP):
                        pe.wait_ge(h1_ready, upto(g, n))
                        turn(g, GROUP + n, lambda k: h1[:, n, k * P:(k + 1) * P])
                    for half in range(2):
                        pe.wait_ge(tp_out, TP * g + GROUP + (4 if half == 0 else GROUP))
                        for m in range(FC):
                            use = half * FC + m
                            if use < 2:
                                pe.wait_ge(gates, GAT * g)
                            elif use < 4:
                                pe.wait_ge(new_pre, GQ * g)
                            else:
                                pe.wait_ge(relued, REL * g + use - 3)
                            half_matmul(use % 4, c["f1"], m * P, hT, half)
                    for n in range(GROUP):
                        pe.wait_ge(relued, REL * g + (FC if n < 3 else 2 * FC))
                        pe.wait_ge(resid, 2 * GROUP * g + GROUP + n - 1)
                        rows_matmul(GROUP + n, lambda m: gT[:, m, n * P:(n + 1) * P], lambda m: c["f2"][:, m, :], FC, D)
                    for n in range(GROUP):
                        pe.wait_ge(h2_ready, upto(g, n))
                        turn(g, 2 * GROUP + n, lambda k: h[:, n, k * P:(k + 1) * P])
                    for q in range(GQ):
                        half, m = q // KC, q % KC
                        pe.wait_ge(tp_out, TP * g + 2 * GROUP + (4 if half == 0 else GROUP))
                        for slot in range(4):
                            if q >= 1:
                                if slot < 2:
                                    pe.wait_ge(gates, GAT * g + 2 * (q - 1) + slot + 1)
                                else:
                                    pe.wait_ge(new_pre, GQ * g + q)
                            half_matmul(slot, c["gru"], slot * D + m * P, hT, half)
                    for n in range(GROUP):
                        pe.wait_ge(o_ready, GQ * g + (KC if n < 3 else 2 * KC))
                        turn(g, 3 * GROUP + n, lambda k: nT[:, k, n * P:(n + 1) * P])
                    for n in range(GROUP):
                        pe.wait_ge(xm_ready, upto(g, n))
                        turn(g, 4 * GROUP + n, lambda k: xm[:, n, k * P:(k + 1) * P])
                        pe.wait_ge(tp_out, TP * g + 4 * GROUP + n + 1)
                        if n < 2:
                            pe.wait_ge(resid, 2 * GROUP * g + 2 * GROUP)
                        else:
                            pe.wait_ge(ht_ready, GROUP * g + n - 1)
                        rows_matmul(2 * GROUP + n, lambda k: tT[:, k, n * P:(n + 1) * P], lambda k: c["w1"][:, k, :], KC, HT)

            @block.scalar
            def _(act):
                def evacuate(g, use, dst):
                    act.wait_ge(tp_full, TP * g + use + 1)
                    nc.scalar.copy(dst, tp[:, use % 2, 0:D].rearrange("p (k c) -> p k c", k=KC)).then_inc(tp_out, 1)

                def table_row(g, n):
                    act.wait_ge(mo_full, MO * g + 2 * GROUP + n + 1)
                    act.wait_ge(stored[1], 16 * g)
                    nc.scalar.copy(ht[:, n, :], mo[:, (2 * GROUP + n) % 2, 0:HT]).then_inc(ht_ready, 1)

                def new_gate(g, q):
                    half, m = q // KC, q % KC
                    act.wait_ge(new_pre, GQ * g + q + 1)
                    s = nT[:, m, half * HALF:(half + 1) * HALF]
                    nc.scalar.activation(s, s, ACT.Tanh, bias=c["bih"][:, 4 + m:5 + m]).then_inc(new_ready, 1)

                with act.Fori(0, GROUPS) as g:
                    for n in range(GROUP):
                        act.wait_ge(mo_full, MO * g)
                        evacuate(g, n, tT[:, :, n * P:(n + 1) * P])
                    for n in range(GROUP):
                        act.wait_ge(o_ready, GQ * g)
                        evacuate(g, GROUP + n, hT[:, :, n * P:(n + 1) * P])
                    for half in range(2):
                        for m in range(FC):
                            use = half * FC + m
                            act.wait_ge(hf_full, HF * g + use + 1)
                            nc.scalar.activation(gT[:, m, half * HALF:(half + 1) * HALF], hf[:, use % 4, 0:HALF], ACT.Relu,
                                                 bias=c["f1_b"][:, m:m + 1]).then_inc(relued, 1)
                    for n in range(GROUP):
                        evacuate(g, 2 * GROUP + n, hT[:, :, n * P:(n + 1) * P])
                    for q in range(GQ):
                        half, m = q // KC, q % KC
                        for slot, dst in ((0, rT), (1, zT)):
                            act.wait_ge(hf_full, HF * g + 2 * FC + 4 * q + slot + 1)
                            nc.scalar.activation(dst[:, m, half * HALF:(half + 1) * HALF], hf[:, slot, 0:HALF], ACT.Sigmoid,
                                                 bias=c["brz"][:, slot * KC + m:slot * KC + m + 1]).then_inc(gates, 1)
                        if q >= 1:
                            new_gate(g, q - 1)
                    new_gate(g, GQ - 1)
                    for n in range(GROUP):
                        evacuate(g, 3 * GROUP + n, bk[:, n, :].rearrange("p (k c) -> p k c", k=KC))
                    for n in range(GROUP):
                        evacuate(g, 4 * GROUP + n, tT[:, :, n * P:(n + 1) * P])
                        if n >= 1:
                            table_row(g, n - 1)
                    table_row(g, GROUP - 1)
                    act.wait_ge(xm_ready, GROUP * g + GROUP)
                    act.dma_start(xmid_out[group_rows(g), :].rearrange("(n p) d -> p n d", p=P), xm[:]).then_inc(stored[0], 16)
                    act.wait_ge(ht_ready, GROUP * g + GROUP)
                    act.dma_start(table_out[group_rows(g), :].rearrange("(n p) d -> p n d", p=P), ht[:]).then_inc(stored[1], 16)
                act.wait_ge(stored[0], 16 * GROUPS)
                act.wait_ge(stored[1], 16 * GROUPS)

            @block.gpsimd
            def _(pool):
                row = {s: c["rows"][:, j, :] for j, s in enumerate(("O_b", "ln1_w", "ln1_b", "f2_b", "ln2_w", "ln2_b"))}

                def rstd(g, which, n):
                    pool.wait_ge(var_ready, 3 * GROUP * g + which * GROUP + n + 1)
                    nc.gpsimd.tensor_tensor(rs[:, n:n + 1], ve[:, n:n + 1], c["half"][:], ALU.pow).then_inc(rstd_ready, 1)

                with pool.Fori(0, GROUPS) as g:
                    for n in range(GROUP):
                        pool.wait_ge(x_in, 16 * g + 16)
                        pool.wait_ge(resid, 2 * GROUP * g)
                        nc.gpsimd.tensor_tensor(xb[:, n, :], xt[:, n, :], row["O_b"], ALU.add).then_inc(xb_ready, 1)
                    for n in range(GROUP + 1):
                        if n < GROUP:
                            rstd(g, 0, n)
                        if n >= 1:
                            m = n - 1
                            pool.wait_ge(normed, 2 * GROUP * g + m + 1)
                            nc.gpsimd.tensor_tensor(h1[:, m, :], h[:, m, :], row["ln1_w"], ALU.mult).then_inc(scaled, 1)
                            pool.wait_ge(scaled, 2 * GROUP * g + m + 1)
                            nc.gpsimd.tensor_tensor(h1[:, m, :], h1[:, m, :], row["ln1_b"], ALU.add).then_inc(h1_ready, 1)
                            pool.wait_ge(h1_ready, upto(g, m))
                            nc.gpsimd.tensor_tensor(hb[:, m, :], h1[:, m, :], row["f2_b"], ALU.add).then_inc(hb_ready, 1)
                    for n in range(GROUP + 1):
                        if n < GROUP:
                            rstd(g, 1, n)
                        if n >= 1:
                            m = n - 1
                            pool.wait_ge(normed, 2 * GROUP * g + GROUP + m + 1)
                            nc.gpsimd.tensor_tensor(h[:, m, :], h[:, m, :], row["ln2_w"], ALU.mult).then_inc(scaled, 1)
                            pool.wait_ge(scaled, 2 * GROUP * g + GROUP + m + 1)
                            nc.gpsimd.tensor_tensor(h[:, m, :], h[:, m, :], row["ln2_b"], ALU.add).then_inc(h2_ready, 1)
                    for n in range(GROUP):
                        rstd(g, 2, n)

            @block.vector
            def _(dve):
                def sum_and_stats(g, which, n, dst, in0, in1):
                    if which < 2:
                        nc.vector.tensor_tensor(dst, in0, in1, ALU.add).then_inc(resid, 1)
                        dve.wait_ge(resid, 2 * GROUP * g + which * GROUP + n + 1)
                    else:
                        nc.vector.tensor_tensor(dst, in0, in1, ALU.add).then_inc(y_summed, 1)
                        dve.wait_ge(y_summed, upto(g, n))
                    count = 3 * GROUP * g + which * GROUP + n + 1
                    nc.vector.bn_stats(stats[:], dst).then_inc(stats_ready, 1)
                    hold(dve, stats_ready, count)
                    nc.vector.bn_aggr(mv[:, n, :], stats[:]).then_inc(mean_ready, 1)
                    dve.wait_ge(mean_ready, count)
                    nc.vector.tensor_scalar(ve[:, n:n + 1], mv[:, n, 1:2], EPS, None, ALU.add).then_inc(var_ready, 1)

                def normalise(g, which, n, dst, src):
                    dve.wait_ge(rstd_ready, 3 * GROUP * g + which * GROUP + n + 1)
                    nc.vector.tensor_scalar(dst, src, mv[:, n, 0:1], rs[:, n:n + 1], ALU.subtract,
                                            ALU.mult).then_inc(normed if which < 2 else xm_ready, 1)

                def combine(g, q):
                    half, m = q // KC, q % KC
                    cols = slice(half * HALF, (half + 1) * HALF)
                    done = GQ * g + q + 1
                    dve.wait_ge(new_ready, done)
                    nc.vector.tensor_tensor(rT[:, m, cols], hT[:, m, cols], nT[:, m, cols], ALU.subtract).then_inc(h_less_n, 1)
                    dve.wait_ge(h_less_n, done)
                    nc.vector.tensor_tensor(rT[:, m, cols], rT[:, m, cols], zT[:, m, cols], ALU.mult).then_inc(z_applied, 1)
                    dve.wait_ge(z_applied, done)
                    nc.vector.tensor_tensor(nT[:, m, cols], rT[:, m, cols], nT[:, m, cols], ALU.add).then_inc(o_ready, 1)

                with dve.Fori(0, GROUPS) as g:
                    dve.wait_ge(x1_in, 16 * g + 16)
                    dve.wait_ge(agg_in, 16 * g + 16)
                    for n in range(GROUP):
                        dve.wait_ge(tp_full, TP * g)
                        nc.vector.tensor_tensor(at[:, n, :], x1t[:, n, :], agt[:, n, :], ALU.mult).then_inc(attn_ready, 1)
                    for n in range(GROUP + 1):
                        if n < GROUP:
                            dve.wait_ge(mo_full, MO * g + n + 1)
                            dve.wait_ge(xb_ready, upto(g, n))
                            sum_and_stats(g, 0, n, h[:, n, :], mo[:, n % 2, 0:D], xb[:, n, :])
                        if n >= 1:
                            normalise(g, 0, n - 1, h[:, n - 1, :], h[:, n - 1, :])
                    for n in range(GROUP + 1):
                        if n < GROUP:
                            dve.wait_ge(mo_full, MO * g + GROUP + n + 1)
                            dve.wait_ge(hb_ready, upto(g, n))
                            sum_and_stats(g, 1, n, h[:, n, :], mo[:, (GROUP + n) % 2, 0:D], hb[:, n, :])
                        if n >= 1:
                            normalise(g, 1, n - 1, h[:, n - 1, :], h[:, n - 1, :])
                    for q in range(GQ):
                        half, m = q // KC, q % KC
                        cols = slice(half * HALF, (half + 1) * HALF)
                        dve.wait_ge(hf_full, HF * g + 2 * FC + 4 * q + 4)
                        dve.wait_ge(gates, GAT * g + 2 * q + 1)
                        dve.wait_ge(tp_full, TP * g)
                        nc.vector.scalar_tensor_tensor(out=nT[:, m, cols], in0=hf[:, 3, 0:HALF], scalar=c["bhh"][:, 4 + m:5 + m],
                                                       in1=rT[:, m, cols], op0=ALU.add, op1=ALU.mult).then_inc(reset_applied, 1)
                        dve.wait_ge(reset_applied, GQ * g + q + 1)
                        nc.vector.tensor_tensor(nT[:, m, cols], nT[:, m, cols], hf[:, 2, 0:HALF], ALU.add).then_inc(new_pre, 1)
                        if q >= 1:
                            combine(g, q - 1)
                    combine(g, GQ - 1)
                    for n in range(GROUP + 1):
                        if n < GROUP:
                            dve.wait_ge(tp_out, TP * g + 3 * GROUP + n + 1)
                            sum_and_stats(g, 2, n, bk[:, n, :], bk[:, n, :], xt[:, n, :])
                        if n >= 1:
                            dve.wait_ge(stored[0], 16 * g)
                            normalise(g, 2, n - 1, xm[:, n - 1, :], bk[:, n - 1, :])


class EdgeWalk:

    def __init__(self, kit, tmp, nc, name, weighted):
        def sb(what, shape, dt=F32):
            return tmp.enter_context(nc.sbuf_tensor(f"{name}_{what}", shape, dt))

        self.weighted, self.cols = weighted, HT if weighted else D
        self.seg, self.gat = sb("seg", [P, 1], I32), sb("gat", [P, 1], I32)
        self.seg_row = sb("seg_row", [P, P], I32)
        self.seg_f = sb("seg_f", [P, 1])
        self.rows, self.old, self.recv = sb("rows", [P, self.cols]), sb("old", [P, self.cols]), sb("recv", [P, HT])
        self.w = sb("w", [P, 4])
        self.same, self.earlier = sb("same", [P, P]), sb("earlier", [P, P])
        self.below, self.trash = sb("below", [P, P]), sb("trash", [P, 1])
        self.rank, self.first = sb("rank", [P, 1]), sb("first", [P, 1])
        self.to_f, self.to = sb("to_f", [P, 1]), sb("to", [P, 1], I32)
        self.sums = tmp.enter_context(nc.psum_tensor(f"{name}_sums", [P, 512], F32))
        self.s_zeroed = kit.sem(name + "_zeroed")
        self.s_cleared = kit.sem(name + "_cleared")
        self.s_consts = kit.sem(name + "_consts")
        self.s_below_set = kit.sem(name + "_below_set")
        self.s_idx_in = kit.sem(name + "_idx_in")
        self.s_rows_in = kit.sem(name + "_rows_in")
        self.s_recv_in = kit.sem(name + "_recv_in")
        self.s_old_in = kit.sem(name + "_old_in")
        self.s_converted = kit.sem(name + "_converted")
        self.s_same_ready = kit.sem(name + "_same_ready")
        self.s_masked = kit.sem(name + "_masked")
        self.s_ranked = kit.sem(name + "_ranked")
        self.s_first_ready = kit.sem(name + "_first_ready")
        self.s_moved = kit.sem(name + "_moved")
        self.s_blended = kit.sem(name + "_blended")
        self.s_to_ready = kit.sem(name + "_to_ready")
        self.s_summed = kit.sem(name + "_summed")
        self.s_weighted = kit.sem(name + "_weighted")
        self.s_w_added = kit.sem(name + "_w_added")
        self.s_w_scaled = kit.sem(name + "_w_scaled")
        self.s_w_leaky = kit.sem(name + "_w_leaky")
        self.s_w_ready = kit.sem(name + "_w_ready")
        self.s_w_applied = kit.sem(name + "_w_applied")
        self.s_added = kit.sem(name + "_added")
        self.s_stored = kit.sem(name + "_stored")


def edge_walk_sync(nc, sp, k, seg, gat, out):
    sp.wait_ge(k.s_zeroed, 1)
    n = (ROWS + P) // P
    with sp.Fori(0, n) as t:
        sp.dma_start(out[bass.ds(t * P, P), :], k.old[:]).then_inc(k.s_cleared, 16)
    sp.wait_ge(k.s_cleared, 16 * n)
    with sp.Fori(0, EDGE_TILES) as t:
        sp.wait_ge(k.s_stored, t * 16)
        with nc.allow_non_contiguous_dma("one index per partition"):
            sp.dma_start(k.seg[:], seg[bass.ds(t * P, P)].unsqueeze(1)).then_inc(k.s_idx_in, 16)
            sp.dma_start(k.gat[:], gat[bass.ds(t * P, P)].unsqueeze(1)).then_inc(k.s_idx_in, 16)
        sp.dma_start(k.seg_row[:], seg[bass.ds(t * P, P)].partition_broadcast(P)).then_inc(k.s_idx_in, 16)


def edge_walk_pool(nc, pool, k, table, out):
    nc.gpsimd.memset(k.old[:], 0.0).then_inc(k.s_zeroed, 1)
    nc.gpsimd.iota(k.trash[:], [[0, 1]], base=TRASH, channel_multiplier=1,
                   allow_small_or_imprecise_dtypes=True).then_inc(k.s_consts, 1)
    nc.gpsimd.memset(k.below[:], 1.0).then_inc(k.s_below_set, 1)
    pool.wait_ge(k.s_below_set, 1)
    nc.gpsimd.affine_select(out=k.below[:], in_=k.below[:], compare_op=ALU.is_gt, fill=0.0, base=0,
                            pattern=[[-1, P]], channel_multiplier=1).then_inc(k.s_consts, 1)
    pool.wait_ge(k.s_cleared, 16 * ((ROWS + P) // P))
    with pool.Fori(0, EDGE_TILES) as t:
        hold(pool, k.s_idx_in, t * 48 + 48)
        nc.gpsimd.indirect_dma_start(k.rows[:], None, table, bass.IndirectOffsetOnAxis(ap=k.gat[:, 0:1], axis=0)) \
            .then_inc(k.s_rows_in, 16)
        if k.weighted:
            nc.gpsimd.indirect_dma_start(k.recv[:], None, table, bass.IndirectOffsetOnAxis(ap=k.seg[:, 0:1], axis=0)) \
                .then_inc(k.s_recv_in, 16)
        hold(pool, k.s_to_ready, t + 1)
        nc.gpsimd.indirect_dma_start(k.old[:], None, out, bass.IndirectOffsetOnAxis(ap=k.to[:, 0:1], axis=0)) \
            .then_inc(k.s_old_in, 16)
        hold(pool, k.s_added, t + 1)
        nc.gpsimd.indirect_dma_start(out, bass.IndirectOffsetOnAxis(ap=k.to[:, 0:1], axis=0), k.old[:], None) \
            .then_inc(k.s_stored, 16)
        hold(pool, k.s_stored, t * 16 + 16)


def edge_walk_vector(nc, dve, k):
    dve.wait_ge(k.s_consts, 2)
    with dve.Fori(0, EDGE_TILES) as t:
        dve.wait_ge(k.s_idx_in, t * 48 + 48)
        nc.vector.tensor_copy(k.seg_f[:], k.seg[:]).then_inc(k.s_converted, 1)
        dve.wait_ge(k.s_converted, t + 1)
        nc.vector.tensor_scalar(k.same[:], k.seg_row[:], k.seg_f[:, 0:1], None, ALU.is_equal).then_inc(k.s_same_ready, 1)
        dve.wait_ge(k.s_same_ready, t + 1)
        nc.vector.tensor_tensor(k.earlier[:], k.same[:], k.below[:], ALU.mult).then_inc(k.s_masked, 1)
        dve.wait_ge(k.s_masked, t + 1)
        nc.vector.tensor_reduce(k.rank[:], k.earlier[:], AX.X, ALU.add).then_inc(k.s_ranked, 1)
        dve.wait_ge(k.s_ranked, t + 1)
        nc.vector.tensor_scalar(k.first[:], k.rank[:], 0.0, None, ALU.is_equal).then_inc(k.s_first_ready, 1)
        nc.vector.tensor_tensor(k.to_f[:], k.seg_f[:], k.trash[:], ALU.subtract).then_inc(k.s_moved, 1)
        dve.wait_ge(k.s_first_ready, t + 1)
        dve.wait_ge(k.s_moved, t + 1)
        nc.vector.scalar_tensor_tensor(out=k.to_f[:], in0=k.to_f[:], scalar=k.first[:, 0:1], in1=k.trash[:],
                                       op0=ALU.mult, op1=ALU.add).then_inc(k.s_blended, 1)
        dve.wait_ge(k.s_blended, t + 1)
        nc.vector.tensor_copy(k.to[:], k.to_f[:]).then_inc(k.s_to_ready, 1)
        if k.weighted:
            dve.wait_ge(k.s_rows_in, t * 16 + 16)
            dve.wait_ge(k.s_recv_in, t * 16 + 16)
            nc.vector.tensor_tensor(k.w[:, 0:1], k.recv[:, D:D + 1], k.rows[:, D + 1:D + 2], ALU.add).then_inc(k.s_w_added, 1)
            dve.wait_ge(k.s_w_added, t + 1)
            nc.vector.tensor_scalar(k.w[:, 1:2], k.w[:, 0:1], ALPHA, None, ALU.mult).then_inc(k.s_w_scaled, 1)
            dve.wait_ge(k.s_w_scaled, t + 1)
            nc.vector.tensor_tensor(k.w[:, 2:3], k.w[:, 0:1], k.w[:, 1:2], ALU.max).then_inc(k.s_w_leaky, 1)
            dve.wait_ge(k.s_w_ready, t + 1)
            nc.vector.tensor_scalar(k.rows[:], k.rows[:], k.w[:, 3:4], None, ALU.mult).then_inc(k.s_w_applied, 1)
            dve.wait_ge(k.s_w_applied, t + 1)
            nc.vector.tensor_copy(k.rows[:, D:D + 1], k.w[:, 3:4]).then_inc(k.s_weighted, 1)
        dve.wait_ge(k.s_old_in, t * 16 + 16)
        dve.wait_ge(k.s_summed, t + 1)
        nc.vector.tensor_tensor(k.old[:], k.old[:], k.sums[:, 0:k.cols], ALU.add).then_inc(k.s_added, 1)


def edge_walk_scalar(nc, act, k):
    if k.weighted:
        with act.Fori(0, EDGE_TILES) as t:
            act.wait_ge(k.s_w_leaky, t + 1)
            nc.scalar.activation(k.w[:, 3:4], k.w[:, 2:3], ACT.Exp, scale=-1.0).then_inc(k.s_w_ready, 1)


def edge_walk_tensor(nc, pe, k):
    with pe.Fori(0, EDGE_TILES) as t:
        pe.wait_ge(k.s_same_ready, t + 1)
        if k.weighted:
            pe.wait_ge(k.s_weighted, t + 1)
        else:
            pe.wait_ge(k.s_rows_in, t * 16 + 16)
        nc.tensor.matmul(k.sums[:, 0:k.cols], k.same[:], k.rows[:], start=True, stop=True).then_inc(k.s_summed, 1)


def sum_over_edges(nc, kit, name, weighted, seg, gat, table, out):
    with ExitStack() as tmp:
        k = EdgeWalk(kit, tmp, nc, name, weighted)
        with nc.Block() as block:

            @block.sync
            def _(sp):
                edge_walk_sync(nc, sp, k, seg, gat, out)

            @block.gpsimd
            def _(pool):
                edge_walk_pool(nc, pool, k, table, out)

            @block.vector
            def _(dve):
                edge_walk_vector(nc, dve, k)

            @block.scalar
            def _(act):
                edge_walk_scalar(nc, act, k)

            @block.tensor
            def _(pe):
                edge_walk_tensor(nc, pe, k)


def final_rows(nc, kit, c, xmid, sums, out):
    with ExitStack() as tmp:
        def sb(name, shape, dt=F32):
            return tmp.enter_context(nc.sbuf_tensor(name, shape, dt))

        xm, sm, y = sb("f_xmid", [P, GROUP, D]), sb("f_sums", [P, GROUP, HT]), sb("f_y", [P, GROUP, D])
        rd, rs = sb("f_rweights", [P, GROUP]), sb("f_rstd", [P, GROUP])
        stats, mv, ve = sb("f_stats", [P, nc.vector.BN_STATS_DIM]), sb("f_mv", [P, GROUP, 2]), sb("f_var_eps", [P, GROUP])
        xm_in = [kit.sem(f"f_xmid_loaded{n}") for n in range(GROUP)]
        sm_in = [kit.sem(f"f_sums_loaded{n}") for n in range(GROUP)]
        stored = [kit.sem(f"out_stored{n}") for n in range(GROUP)]
        clamped, inverted, divided, summed, stats_ready, mean_ready, var_ready, rstd_ready, ready = (
            kit.sem("f_" + s) for s in ("clamped", "inverted", "divided", "summed", "stats", "mean", "var", "rstd", "ready"))
        with nc.Block() as block:

            @block.sync
            def _(sp):
                with sp.Fori(0, GROUPS) as g:
                    for n in range(GROUP):
                        sp.wait_ge(ready, before(g, n, GROUP))
                        sp.dma_start(xm[:, n, :], xmid[tile_rows(g, n), :]).then_inc(xm_in[n], 16)
                        sp.dma_start(sm[:, n, :], sums[tile_rows(g, n), :]).then_inc(sm_in[n], 16)

            @block.scalar
            def _(act):
                with act.Fori(0, GROUPS) as g:
                    for n in range(GROUP):
                        act.wait_ge(ready, upto(g, n))
                        act.dma_start(out[tile_rows(g, n), :], y[:, n, :]).then_inc(stored[n], 16)
                for n in range(GROUP):
                    act.wait_ge(stored[n], 16 * GROUPS)

            @block.gpsimd
            def _(pool):
                with pool.Fori(0, GROUPS) as g:
                    for n in range(GROUP):
                        pool.wait_ge(var_ready, upto(g, n))
                        nc.gpsimd.tensor_tensor(rs[:, n:n + 1], ve[:, n:n + 1], c["half"][:], ALU.pow).then_inc(rstd_ready, 1)

            @block.vector
            def _(dve):
                def normalise(g, n):
                    dve.wait_ge(rstd_ready, upto(g, n))
                    nc.vector.tensor_scalar(y[:, n, :], y[:, n, :], mv[:, n, 0:1], rs[:, n:n + 1], ALU.subtract,
                                            ALU.mult).then_inc(ready, 1)

                with dve.Fori(0, GROUPS) as g:
                    for n in range(GROUP):
                        done = upto(g, n)
                        dve.wait_ge(sm_in[n], 16 * g + 16)
                        nc.vector.tensor_scalar(rd[:, n:n + 1], sm[:, n, D:D + 1], TINY, None, ALU.max).then_inc(clamped, 1)
                        dve.wait_ge(clamped, done)
                        nc.vector.reciprocal(rd[:, n:n + 1], rd[:, n:n + 1]).then_inc(inverted, 1)
                        dve.wait_ge(inverted, done)
                        dve.wait_ge(stored[n], 16 * g)
                        nc.vector.tensor_scalar(y[:, n, :], sm[:, n, 0:D], rd[:, n:n + 1], 0.0, ALU.mult,
                                                ALU.max).then_inc(divided, 1)
                        dve.wait_ge(divided, done)
                        dve.wait_ge(xm_in[n], 16 * g + 16)
                        nc.vector.tensor_tensor(y[:, n, :], y[:, n, :], xm[:, n, :], ALU.add).then_inc(summed, 1)
                        dve.wait_ge(summed, done)
                        nc.vector.bn_stats(stats[:], y[:, n, :]).then_inc(stats_ready, 1)
                        hold(dve, stats_ready, done)
                        nc.vector.bn_aggr(mv[:, n, :], stats[:]).then_inc(mean_ready, 1)
                        dve.wait_ge(mean_ready, done)
                        nc.vector.tensor_scalar(ve[:, n:n + 1], mv[:, n, 1:2], EPS, None, ALU.add).then_inc(var_ready, 1)
                        if n >= 1:
                            normalise(g, n - 1)
                    normalise(g, GROUP - 1)

_WEIGHTS = ["Wq", "Wk", "Wv", "O_w", "O_b", "ln1_w", "ln1_b", "f1_w", "f1_b", "f2_w", "f2_b", "ln2_w", "ln2_b",
            "gru_w_ih", "gru_w_hh", "gru_b_ih", "gru_b_hh"]


def build(nc, a, out):
    w = {n: a["L0_gnn_" + n] for n in _WEIGHTS}
    w["L1_W"], w["L1_a"] = a["L1_gnn_W"], a["L1_gnn_a"]

    def scratch(name, shape):
        return nc.dram_tensor(name, shape, F32, kind="Internal").ap()

    x1, xmid = scratch("x1_table", [ROWS, D]), scratch("xmid", [ROWS, D])
    table = scratch("node_table", [ROWS, HT])
    agg, sums = scratch("agg", [ROWS + P, D]), scratch("sums", [ROWS + P, HT])
    with ExitStack() as ctx:
        kit = Kit(nc, ctx)
        c = load_constants(nc, kit, w)
        attention_rows(nc, kit, c, a["x"], x1)
        sum_over_edges(nc, kit, "l0", False, a["dst"], a["src"], x1, agg)
        update_rows(nc, kit, c, a["x"], x1, agg, xmid, table)
        sum_over_edges(nc, kit, "l1", True, a["src"], a["dst"], table, sums)
        final_rows(nc, kit, c, xmid, sums, out)


def _pad(a, n, fill):
    a = np.asarray(a)
    return np.concatenate([a, np.full((n - a.shape[0],) + a.shape[1:], fill, a.dtype)])


def kernel(**inputs):
    import concourse.bacc as _bacc
    from concourse.bass_utils import run_bass_kernel_spmd as _run

    host = dict(inputs)
    host["x"] = _pad(inputs["x"], ROWS, 0)
    host["src"] = _pad(inputs["src"], EDGES, N_NODES)
    host["dst"] = _pad(inputs["dst"], EDGES, N_NODES)
    nc = _bacc.Bacc("TRN2", target_bir_lowering=False, num_devices=1)
    arrays, aps = {}, {}
    for name, a in host.items():
        a = np.ascontiguousarray(a)
        arrays[f"in_{name}"] = a
        aps[name] = nc.dram_tensor(f"in_{name}", a.shape, mybir.dt.from_np(a.dtype), kind="ExternalInput").ap()
    out = nc.dram_tensor("out_rows", [ROWS, D], F32, kind="ExternalOutput").ap()
    build(nc, aps, out)
    r = _run(nc, [arrays], core_ids=[0])
    return r.results[0]["out_rows"][:N_NODES]
```

```python
from contextlib import ExitStack, contextmanager

import numpy as np

import concourse.bass as bass
from concourse import mybir

F32 = mybir.dt.float32
BF16 = mybir.dt.bfloat16
F16 = mybir.dt.float16
I32 = mybir.dt.int32
ALU = mybir.AluOpType
ACT = mybir.ActivationFunctionType
AX = mybir.AxisListType

P = 128
N_NODES = 6250
N_EDGES = 206250
D = 256
KC = D // P
N_HEADS = 8
D_HEAD = D // N_HEADS
D_FFN = 2 * D
FC = D_FFN // P
TILES = -(-N_NODES // P)
GROUP = 7
GROUPS = TILES // GROUP
HALF = GROUP * P // 2
ROWS = TILES * P
TRASH = ROWS
EDGE_QUANTUM = 32 * P
EDGE_TILES = -(-(N_EDGES + 12 * 32) // EDGE_QUANTUM) * 32
EDGES = EDGE_TILES * P
HT = D + 2
EPS = 1e-5
SCORE_SCALE = float(D_HEAD) ** -0.5
ALPHA = 0.2
TINY = 1.2e-38

assert TILES == GROUPS * GROUP


def before(g, n, slots):
    return GROUP * g + max(0, n - slots + 1)


def upto(g, n):
    return GROUP * g + n + 1


def tile_rows(g, n):
    return bass.ds(g * (GROUP * P) + n * P, P)


class Kit:

    def __init__(self, nc, ctx):
        self.nc, self.ctx, self.sems = nc, ctx, []

    def sb(self, name, shape, dt=F32):
        return self.ctx.enter_context(self.nc.sbuf_tensor(name, shape, dt))

    def ps(self, name, shape, dt=F32):
        return self.ctx.enter_context(self.nc.psum_tensor(name, shape, dt))

    def sem(self, name):
        self.sems.append(self.ctx.enter_context(self.nc.semaphore(name)))
        return self.sems[-1]

    @contextmanager
    def stage(self):
        with ExitStack() as ctx:
            kit = Kit(self.nc, ctx)
            yield kit
            with self.nc.Block() as block:

                @block.gpsimd
                def _(pool):
                    for sem in kit.sems:
                        pool.sem_clear(sem)


def load_constants(nc, kit, w):
    c = {}
    c["ident"] = kit.sb("ident", [P, P])
    c["wqkv"] = kit.sb("wqkv", [P, KC, 3 * D])
    c["wo"] = kit.sb("wo", [P, KC, D])
    c["f1"] = kit.sb("f1", [P, KC, D_FFN])
    c["f2"] = kit.sb("f2", [P, FC, D])
    c["gru"] = kit.sb("gru", [P, KC, 4 * D])
    c["w1"] = kit.sb("w1", [P, KC, HT])
    c["rows"] = kit.sb("rows", [P, 6, D])
    c["f1_b"] = kit.sb("f1_bias", [P, FC])
    c["bih"] = kit.sb("bih", [P, 6])
    c["bhh"] = kit.sb("bhh", [P, 6])
    c["brz"] = kit.sb("brz", [P, 4])
    c["a"] = kit.sb("a_bc", [P, 2, D])
    c["half"] = kit.sb("minus_half", [P, 1])
    with ExitStack() as tmp:
        whh = tmp.enter_context(nc.sbuf_tensor("whh", [P, KC, 3 * D], F32))
        junk = tmp.enter_context(nc.sbuf_tensor("wa_products", [P, D], F32))
        loaded = kit.sem("weights_loaded")
        id_zero, folded = kit.sem("ident_zeroed"), kit.sem("weights_folded")
        with nc.Block() as block:

            @block.sync
            def _(sp):
                def split(ap):
                    return ap.rearrange("(k p) n -> p k n", p=P)

                n = 0
                for name, dst in (("Wq", c["wqkv"][:, :, 0:D]), ("Wk", c["wqkv"][:, :, D:2 * D]),
                                  ("Wv", c["wqkv"][:, :, 2 * D:3 * D]), ("O_w", c["wo"][:]), ("f1_w", c["f1"][:]),
                                  ("f2_w", c["f2"][:]), ("gru_w_hh", whh[:]), ("L1_W", c["w1"][:, :, 0:D])):
                    sp.dma_start(dst, split(w[name])).then_inc(loaded, 16)
                    n += 1
                sp.dma_start(c["gru"][:, :, 0:3 * D], split(w["gru_w_ih"])).then_inc(loaded, 16)
                for j, name in enumerate(("O_b", "ln1_w", "ln1_b", "f2_b", "ln2_w", "ln2_b")):
                    sp.dma_start(c["rows"][:, j, :], w[name].partition_broadcast(P)).then_inc(loaded, 16)
                sp.dma_start(c["a"][:].rearrange("p a b -> p (a b)"), w["L1_a"].partition_broadcast(P)).then_inc(loaded, 16)
                for name, m in (("f1_b", FC), ("bih", 6), ("bhh", 6)):
                    src = w[{"f1_b": "f1_b", "bih": "gru_b_ih", "bhh": "gru_b_hh"}[name]]
                    with nc.allow_non_contiguous_dma("a few hundred bias values, once"):
                        sp.dma_start(c[name][:], src.rearrange("(m p) -> p m", p=P)).then_inc(loaded, 16)
                sp.wait_ge(loaded, 16 * 19)

            @block.gpsimd
            def _(pool):
                nc.gpsimd.memset(c["ident"][:], 0.0).then_inc(id_zero, 1)
                nc.gpsimd.memset(c["half"][:], -0.5)
                pool.wait_ge(id_zero, 1)
                nc.gpsimd.affine_select(out=c["ident"][:], in_=c["ident"][:], compare_op=ALU.not_equal, fill=1.0,
                                        base=0, pattern=[[-1, P]], channel_multiplier=1)

            @block.vector
            def _(dve):
                dve.wait_ge(loaded, 16 * 19)
                g = c["gru"]
                nc.vector.tensor_copy(g[:, :, 3 * D:4 * D], whh[:, :, 2 * D:3 * D])
                nc.vector.tensor_tensor(g[:, :, 0:2 * D], g[:, :, 0:2 * D], whh[:, :, 0:2 * D], ALU.add)
                nc.vector.tensor_tensor(c["brz"][:], c["bih"][:, 0:4], c["bhh"][:, 0:4], ALU.add)
                n = 0
                for k in range(KC):
                    for j in range(2):
                        nc.vector.tensor_tensor(junk[:], c["w1"][:, k, 0:D], c["a"][:, j, :],
                                                ALU.mult).then_inc(folded, 1)
                        n += 1
                        dve.wait_ge(folded, n)
                        nc.vector.tensor_reduce(c["w1"][:, k, D + j:D + j + 1], junk[:], AX.X,
                                                ALU.add).then_inc(folded, 1)
                        n += 1
                        dve.wait_ge(folded, n)
    return c


def attention_rows(nc, kit, c, x, x1_out, parts):
    with ExitStack() as tmp:
        def sb(name, shape, dt=F32):
            return tmp.enter_context(nc.sbuf_tensor(name, shape, dt))

        xt = sb("qx", [P, GROUP, D])
        xT = sb("qxT", [P, D])
        qk = sb("qk", [P, 2, 2 * D])
        v = sb("v", [P, GROUP, D])
        prod = sb("qk_products", [P, N_HEADS, N_HEADS, D_HEAD])
        av = sb("av_products", [P, 2, N_HEADS, D_HEAD, N_HEADS])
        sc = sb("scores", [P, 2, N_HEADS, N_HEADS])
        mx = sb("score_max", [P, N_HEADS])
        sm = sb("prob_sum", [P, N_HEADS])
        rs = sb("prob_rsum", [P, N_HEADS])
        x1 = sb("x1_tile", [P, GROUP, D])
        rem = sb("x1_remainder", [P, GROUP, D])
        tp = tmp.enter_context(nc.psum_tensor("q_tp", [P, D], F32))
        pqk = tmp.enter_context(nc.psum_tensor("p_qk", [P, 2 * D], F32))
        pv = tmp.enter_context(nc.psum_tensor("p_v", [P, D], F32))

        x_loaded = [kit.sem(f"q_x_loaded{n}") for n in range(GROUP)]
        xT_in_psum, xT_ready = kit.sem("q_xT_in_psum"), kit.sem("q_xT_ready")
        qkv_in_psum, qk_ready, v_ready = kit.sem("qkv_in_psum"), kit.sem("qk_ready"), kit.sem("v_ready")
        products, reduced, maxed = kit.sem("qk_products_done"), kit.sem("scores_reduced"), kit.sem("scores_maxed")
        shifted, exped = kit.sem("scores_shifted"), kit.sem("scores_exped")
        summed, inverted, probs = kit.sem("probs_summed"), kit.sem("probs_inverted"), kit.sem("probs_ready")
        av_ready, x1_ready = kit.sem("av_products_ready"), kit.sem("x1_ready")
        x1_stored = [kit.sem(f"x1_stored{n}") for n in range(GROUP)]
        high, remained, mid, low = kit.sem("x1_high"), kit.sem("x1_remained"), kit.sem("x1_mid"), kit.sem("x1_low")

        def part(k, g, n):
            return parts[:, k, bass.ds(GROUP * g + n, 1), :]

        with nc.Block() as block:

            @block.sync
            def _(sp):
                with sp.Fori(0, GROUPS) as g:
                    for n in range(GROUP):
                        sp.wait_ge(xT_in_psum, before(g, n, GROUP))
                        sp.dma_start(xt[:, n, :], x[tile_rows(g, n), :]).then_inc(x_loaded[n], 16)

            @block.tensor
            def _(pe):
                with pe.Fori(0, GROUPS) as g:
                    for n in range(GROUP):
                        pe.wait_ge(x_loaded[n], 16 * g + 16)
                        for k in range(KC):
                            last = nc.tensor.transpose(tp[:, k * P:(k + 1) * P], xt[:, n, k * P:(k + 1) * P],
                                                       c["ident"][:])
                        last.then_inc(xT_in_psum, 1)
                        pe.wait_ge(xT_ready, upto(g, n))
                        pe.wait_ge(v_ready, GROUP * g + n)
                        for k in range(KC):
                            nc.tensor.matmul(pqk[:], xT[:, k * P:(k + 1) * P], c["wqkv"][:, k, 0:2 * D],
                                             start=(k == 0), stop=(k == KC - 1))
                        for k in range(KC):
                            last = nc.tensor.matmul(pv[:], xT[:, k * P:(k + 1) * P], c["wqkv"][:, k, 2 * D:3 * D],
                                                    start=(k == 0), stop=(k == KC - 1))
                        last.then_inc(qkv_in_psum, 1)

            @block.scalar
            def _(act):
                def exp_of(g, n):
                    act.wait_ge(shifted, upto(g, n))
                    nc.scalar.activation(sc[:, n % 2], sc[:, n % 2], ACT.Exp, scale=SCORE_SCALE).then_inc(exped, 1)

                def store_of(g, n):
                    act.wait_ge(x1_ready, upto(g, n))
                    act.dma_start(x1_out[tile_rows(g, n), :], x1[:, n, :]).then_inc(x1_stored[n], 16)

                def split_high(g, n):
                    nc.scalar.copy(part(0, g, n), x1[:, n:n + 1, :]).then_inc(high, 1)

                def split_mid(g, n):
                    act.wait_ge(remained, upto(g, n))
                    nc.scalar.copy(part(1, g, n), rem[:, n:n + 1, :]).then_inc(mid, 1)

                with act.Fori(0, GROUPS) as g:
                    for n in range(GROUP):
                        act.wait_ge(xT_in_psum, upto(g, n))
                        act.wait_ge(qkv_in_psum, GROUP * g + n)
                        nc.scalar.copy(xT[:], tp[:]).then_inc(xT_ready, 1)
                        act.wait_ge(qkv_in_psum, upto(g, n))
                        act.wait_ge(products, before(g, n, 2))
                        nc.scalar.copy(qk[:, n % 2, :], pqk[:]).then_inc(qk_ready, 1)
                        act.wait_ge(av_ready, before(g, n, GROUP))
                        nc.scalar.copy(v[:, n, :], pv[:]).then_inc(v_ready, 1)
                        if n >= 1:
                            exp_of(g, n - 1)
                        if n >= 2:
                            store_of(g, n - 2)
                            split_high(g, n - 2)
                        if n >= 3:
                            split_mid(g, n - 3)
                    exp_of(g, GROUP - 1)
                    for n in (GROUP - 2, GROUP - 1):
                        store_of(g, n)
                        split_high(g, n)
                    for n in (GROUP - 3, GROUP - 2, GROUP - 1):
                        split_mid(g, n)
                for n in range(GROUP):
                    act.wait_ge(x1_stored[n], 16 * GROUPS)

            @block.gpsimd
            def _(pool):
                def remain(g, n):
                    pool.wait_ge(high, upto(g, n))
                    pool.wait_ge(low, before(g, n, GROUP))
                    nc.gpsimd.tensor_tensor(rem[:, n:n + 1, :], x1[:, n:n + 1, :], part(0, g, n), ALU.subtract).then_inc(remained, 1)

                def split_low(g, n):
                    pool.wait_ge(mid, upto(g, n))
                    nc.gpsimd.tensor_tensor(part(2, g, n), rem[:, n:n + 1, :], part(1, g, n), ALU.subtract).then_inc(low, 1)

                with pool.Fori(0, GROUPS) as g:
                    for n in range(GROUP):
                        pool.wait_ge(v_ready, upto(g, n))
                        pool.wait_ge(probs, upto(g, n))
                        pool.wait_ge(x1_ready, before(g, n, 2))
                        p_b = sc[:, n % 2].unsqueeze(2).broadcast_to([P, N_HEADS, D_HEAD, N_HEADS])
                        v_b = v[:, n, :].rearrange("p (g d) -> p d g", g=N_HEADS).unsqueeze(1) \
                            .broadcast_to([P, N_HEADS, D_HEAD, N_HEADS])
                        nc.gpsimd.tensor_tensor(av[:, n % 2], p_b, v_b, ALU.mult).then_inc(av_ready, 1)
                        if n >= 2:
                            remain(g, n - 2)
                        if n >= 3:
                            split_low(g, n - 3)
                    for n in (GROUP - 2, GROUP - 1):
                        remain(g, n)
                    for n in (GROUP - 3, GROUP - 2, GROUP - 1):
                        split_low(g, n)

            @block.vector
            def _(dve):
                def sum_av(g, n):
                    dve.wait_ge(av_ready, upto(g, n))
                    dve.wait_ge(x1_stored[n], 16 * g)
                    dve.wait_ge(remained, before(g, n, GROUP))
                    nc.vector.tensor_reduce(x1[:, n, :], av[:, n % 2].rearrange("p h d g -> p (h d) g"), AX.X,
                                            ALU.add).then_inc(x1_ready, 1)

                with dve.Fori(0, GROUPS) as g:
                    for n in range(GROUP):
                        done = upto(g, n)
                        dve.wait_ge(qk_ready, done)
                        q_b = qk[:, n % 2, 0:D].rearrange("p (h d) -> p h d", h=N_HEADS).unsqueeze(2) \
                            .broadcast_to([P, N_HEADS, N_HEADS, D_HEAD])
                        k_b = qk[:, n % 2, D:2 * D].rearrange("p (h d) -> p h d", h=N_HEADS).unsqueeze(1) \
                            .broadcast_to([P, N_HEADS, N_HEADS, D_HEAD])
                        nc.vector.tensor_tensor(prod[:], q_b, k_b, ALU.mult).then_inc(products, 1)
                        dve.wait_ge(products, done)
                        dve.wait_ge(av_ready, before(g, n, 2))
                        nc.vector.tensor_reduce(sc[:, n % 2], prod[:], AX.X, ALU.add).then_inc(reduced, 1)
                        dve.wait_ge(reduced, done)
                        dve.wait_ge(shifted, GROUP * g + n)
                        nc.vector.tensor_reduce(mx[:], sc[:, n % 2], AX.X, ALU.max).then_inc(maxed, 1)
                        dve.wait_ge(maxed, done)
                        nc.vector.tensor_tensor(sc[:, n % 2], sc[:, n % 2],
                                                mx[:].unsqueeze(2).broadcast_to([P, N_HEADS, N_HEADS]),
                                                ALU.subtract).then_inc(shifted, 1)
                        if n >= 1:
                            sum_av(g, n - 1)
                        dve.wait_ge(exped, done)
                        dve.wait_ge(probs, GROUP * g + n)
                        nc.vector.tensor_reduce(sm[:], sc[:, n % 2], AX.X, ALU.add).then_inc(summed, 1)
                        dve.wait_ge(summed, done)
                        nc.vector.reciprocal(rs[:], sm[:]).then_inc(inverted, 1)
                        dve.wait_ge(inverted, done)
                        nc.vector.tensor_tensor(sc[:, n % 2], sc[:, n % 2],
                                                rs[:].unsqueeze(2).broadcast_to([P, N_HEADS, N_HEADS]),
                                                ALU.mult).then_inc(probs, 1)
                    sum_av(g, GROUP - 1)


def hold(eng, sem, value):
    value = eng.snap(eng.to_reg(value))
    eng.wait_ge(sem, 1)
    eng.wait_ge(sem, value)


def group_rows(g):
    return bass.ds(g * (GROUP * P), GROUP * P)


def update_rows(nc, kit, c, x, x1, agg, xmid_out, table_out):
    with ExitStack() as tmp:
        def sb(name, shape, dt=F32):
            return tmp.enter_context(nc.sbuf_tensor(name, shape, dt))

        def ps(name, shape):
            return tmp.enter_context(nc.psum_tensor(name, shape, F32))

        xt, x1t, agt = (sb(f"u_{s}", [P, GROUP, D]) for s in ("x", "x1", "agg"))
        at, xb, h, h1, hb = (sb(f"u_{s}", [P, GROUP, D]) for s in ("attn", "x_plus_bias", "h", "h1", "h1_plus_bias"))
        bk, xm = sb("u_gru_rows", [P, GROUP, D]), sb("u_xmid", [P, GROUP, D])
        ht = sb("u_table", [P, GROUP, HT])
        tT = sb("u_attnT", [P, KC, GROUP * P])
        hT = sb("u_hT", [P, KC, GROUP * P])
        gT = sb("u_hiddenT", [P, FC, GROUP * P])
        rT, zT, nT = (sb(f"u_{s}T", [P, KC, GROUP * P]) for s in "rzn")
        stats, mv = sb("u_stats", [P, nc.vector.BN_STATS_DIM]), sb("u_mean_var", [P, GROUP, 2])
        ve, rs = sb("u_var_eps", [P, GROUP]), sb("u_rstd", [P, GROUP])
        tp, mo, hf = ps("u_tp", [P, 2, 512]), ps("u_mo", [P, 2, 512]), ps("u_hf", [P, 4, 512])

        x_in, x1_in, agg_in = kit.sem("u_x_loaded"), kit.sem("u_x1_loaded"), kit.sem("u_agg_loaded")
        stored = [kit.sem("xmid_stored"), kit.sem("table_stored")]
        attn_ready, xb_ready = kit.sem("attn_ready"), kit.sem("x_plus_bias_ready")
        tp_full, tp_out = kit.sem("u_tp_full"), kit.sem("u_tp_evacuated")
        mo_full, resid = kit.sem("u_mo_full"), kit.sem("u_residual_added")
        ht_ready = kit.sem("table_row_ready")
        hf_full, relued = kit.sem("u_hf_full"), kit.sem("u_hidden_relued")
        gates, new_pre, new_ready, o_ready = (kit.sem(s) for s in ("gates_ready", "new_gate_summed", "new_gate_ready",
                                                                    "gru_out_ready"))
        var_ready, rstd_ready, normed = kit.sem("var_ready"), kit.sem("rstd_ready"), kit.sem("rows_normed")
        h1_ready, hb_ready, h2_ready, xm_ready = (kit.sem(s) for s in ("h1_ready", "h1_plus_bias_ready", "h2_ready",
                                                                       "xmid_ready"))
        stats_ready, mean_ready, y_summed = kit.sem("u_stats_ready"), kit.sem("u_mean_ready"), kit.sem("gru_plus_x_summed")
        scaled, reset_applied = kit.sem("rows_scaled"), kit.sem("reset_gate_applied")
        h_less_n, z_applied = kit.sem("h_less_n"), kit.sem("update_gate_applied")
        TP, MO, HF = 5 * GROUP, 3 * GROUP, 24
        REL, GAT, GQ = 2 * FC, 2 * 2 * KC, 2 * KC

        with nc.Block() as block:

            @block.sync
            def _(sp):
                with sp.Fori(0, GROUPS) as g:
                    for dst, src, sem, free in ((x1t, x1, x1_in, attn_ready), (agt, agg, agg_in, attn_ready),
                                                (xt, x, x_in, xm_ready)):
                        sp.wait_ge(free, GROUP * g)
                        sp.dma_start(dst[:], src[group_rows(g), 0:D].rearrange("(n p) d -> p n d", p=P)).then_inc(sem, 16)

            @block.tensor
            def _(pe):
                def turn(g, use, src):
                    pe.wait_ge(tp_out, TP * g + max(0, use - 1))
                    for k in range(KC):
                        last = nc.tensor.transpose(tp[:, use % 2, k * P:(k + 1) * P], src(k), c["ident"][:])
                    last.then_inc(tp_full, 1)

                def rows_matmul(use, lhsT, rhs, chunks, cols):
                    for k in range(chunks):
                        last = nc.tensor.matmul(mo[:, use % 2, 0:cols], lhsT(k), rhs(k), start=(k == 0),
                                                stop=(k == chunks - 1))
                    last.then_inc(mo_full, 1)

                def half_matmul(slot, w, col, src, half):
                    for k in range(KC):
                        last = nc.tensor.matmul(hf[:, slot, 0:HALF], w[:, k, col:col + P],
                                                src[:, k, half * HALF:(half + 1) * HALF],
                                                start=(k == 0), stop=(k == KC - 1))
                    last.then_inc(hf_full, 1)

                with pe.Fori(0, GROUPS) as g:
                    for n in range(GROUP):
                        pe.wait_ge(attn_ready, upto(g, n))
                        turn(g, n, lambda k: at[:, n, k * P:(k + 1) * P])
                        pe.wait_ge(tp_out, TP * g + n + 1)
                        if n < 2:
                            pe.wait_ge(ht_ready, GROUP * g)
                        else:
                            pe.wait_ge(resid, 2 * GROUP * g + n - 1)
                        rows_matmul(n, lambda k: tT[:, k, n * P:(n + 1) * P], lambda k: c["wo"][:, k, :], KC, D)
                    for n in range(GROUP):
                        pe.wait_ge(h1_ready, upto(g, n))
                        turn(g, GROUP + n, lambda k: h1[:, n, k * P:(k + 1) * P])
                    for half in range(2):
                        pe.wait_ge(tp_out, TP * g + GROUP + (4 if half == 0 else GROUP))
                        for m in range(FC):
                            use = half * FC + m
                            if use < 2:
                                pe.wait_ge(gates, GAT * g)
                            elif use < 4:
                                pe.wait_ge(new_pre, GQ * g)
                            else:
                                pe.wait_ge(relued, REL * g + use - 3)
                            half_matmul(use % 4, c["f1"], m * P, hT, half)
                    for n in range(GROUP):
                        pe.wait_ge(relued, REL * g + (FC if n < 3 else 2 * FC))
                        pe.wait_ge(resid, 2 * GROUP * g + GROUP + n - 1)
                        rows_matmul(GROUP + n, lambda m: gT[:, m, n * P:(n + 1) * P], lambda m: c["f2"][:, m, :], FC, D)
                    for n in range(GROUP):
                        pe.wait_ge(h2_ready, upto(g, n))
                        turn(g, 2 * GROUP + n, lambda k: h[:, n, k * P:(k + 1) * P])
                    for q in range(GQ):
                        half, m = q // KC, q % KC
                        pe.wait_ge(tp_out, TP * g + 2 * GROUP + (4 if half == 0 else GROUP))
                        for slot in range(4):
                            if q >= 1:
                                if slot < 2:
                                    pe.wait_ge(gates, GAT * g + 2 * (q - 1) + slot + 1)
                                else:
                                    pe.wait_ge(new_pre, GQ * g + q)
                            half_matmul(slot, c["gru"], slot * D + m * P, hT, half)
                    for n in range(GROUP):
                        pe.wait_ge(o_ready, GQ * g + (KC if n < 3 else 2 * KC))
                        turn(g, 3 * GROUP + n, lambda k: nT[:, k, n * P:(n + 1) * P])
                    for n in range(GROUP):
                        pe.wait_ge(xm_ready, upto(g, n))
                        turn(g, 4 * GROUP + n, lambda k: xm[:, n, k * P:(k + 1) * P])
                        pe.wait_ge(tp_out, TP * g + 4 * GROUP + n + 1)
                        if n < 2:
                            pe.wait_ge(resid, 2 * GROUP * g + 2 * GROUP)
                        else:
                            pe.wait_ge(ht_ready, GROUP * g + n - 1)
                        rows_matmul(2 * GROUP + n, lambda k: tT[:, k, n * P:(n + 1) * P], lambda k: c["w1"][:, k, :], KC, HT)

            @block.scalar
            def _(act):
                def evacuate(g, use, dst):
                    act.wait_ge(tp_full, TP * g + use + 1)
                    nc.scalar.copy(dst, tp[:, use % 2, 0:D].rearrange("p (k c) -> p k c", k=KC)).then_inc(tp_out, 1)

                def table_row(g, n):
                    act.wait_ge(mo_full, MO * g + 2 * GROUP + n + 1)
                    act.wait_ge(stored[1], 16 * g)
                    nc.scalar.copy(ht[:, n, :], mo[:, (2 * GROUP + n) % 2, 0:HT]).then_inc(ht_ready, 1)

                def new_gate(g, q):
                    half, m = q // KC, q % KC
                    act.wait_ge(new_pre, GQ * g + q + 1)
                    s = nT[:, m, half * HALF:(half + 1) * HALF]
                    nc.scalar.activation(s, s, ACT.Tanh, bias=c["bih"][:, 4 + m:5 + m]).then_inc(new_ready, 1)

                with act.Fori(0, GROUPS) as g:
                    for n in range(GROUP):
                        act.wait_ge(mo_full, MO * g)
                        evacuate(g, n, tT[:, :, n * P:(n + 1) * P])
                    for n in range(GROUP):
                        act.wait_ge(o_ready, GQ * g)
                        evacuate(g, GROUP + n, hT[:, :, n * P:(n + 1) * P])
                    for half in range(2):
                        for m in range(FC):
                            use = half * FC + m
                            act.wait_ge(hf_full, HF * g + use + 1)
                            nc.scalar.activation(gT[:, m, half * HALF:(half + 1) * HALF], hf[:, use % 4, 0:HALF], ACT.Relu,
                                                 bias=c["f1_b"][:, m:m + 1]).then_inc(relued, 1)
                    for n in range(GROUP):
                        evacuate(g, 2 * GROUP + n, hT[:, :, n * P:(n + 1) * P])
                    for q in range(GQ):
                        half, m = q // KC, q % KC
                        for slot, dst in ((0, rT), (1, zT)):
                            act.wait_ge(hf_full, HF * g + 2 * FC + 4 * q + slot + 1)
                            nc.scalar.activation(dst[:, m, half * HALF:(half + 1) * HALF], hf[:, slot, 0:HALF], ACT.Sigmoid,
                                                 bias=c["brz"][:, slot * KC + m:slot * KC + m + 1]).then_inc(gates, 1)
                        if q >= 1:
                            new_gate(g, q - 1)
                    new_gate(g, GQ - 1)
                    for n in range(GROUP):
                        evacuate(g, 3 * GROUP + n, bk[:, n, :].rearrange("p (k c) -> p k c", k=KC))
                    for n in range(GROUP):
                        evacuate(g, 4 * GROUP + n, tT[:, :, n * P:(n + 1) * P])
                        if n >= 1:
                            table_row(g, n - 1)
                    table_row(g, GROUP - 1)
                    act.wait_ge(xm_ready, GROUP * g + GROUP)
                    act.dma_start(xmid_out[group_rows(g), :].rearrange("(n p) d -> p n d", p=P), xm[:]).then_inc(stored[0], 16)
                    act.wait_ge(ht_ready, GROUP * g + GROUP)
                    act.dma_start(table_out[group_rows(g), :].rearrange("(n p) d -> p n d", p=P), ht[:]).then_inc(stored[1], 16)
                act.wait_ge(stored[0], 16 * GROUPS)
                act.wait_ge(stored[1], 16 * GROUPS)

            @block.gpsimd
            def _(pool):
                row = {s: c["rows"][:, j, :] for j, s in enumerate(("O_b", "ln1_w", "ln1_b", "f2_b", "ln2_w", "ln2_b"))}

                def rstd(g, which, n):
                    pool.wait_ge(var_ready, 3 * GROUP * g + which * GROUP + n + 1)
                    nc.gpsimd.tensor_tensor(rs[:, n:n + 1], ve[:, n:n + 1], c["half"][:], ALU.pow).then_inc(rstd_ready, 1)

                with pool.Fori(0, GROUPS) as g:
                    for n in range(GROUP):
                        pool.wait_ge(x_in, 16 * g + 16)
                        pool.wait_ge(resid, 2 * GROUP * g)
                        nc.gpsimd.tensor_tensor(xb[:, n, :], xt[:, n, :], row["O_b"], ALU.add).then_inc(xb_ready, 1)
                    for n in range(GROUP + 1):
                        if n < GROUP:
                            rstd(g, 0, n)
                        if n >= 1:
                            m = n - 1
                            pool.wait_ge(normed, 2 * GROUP * g + m + 1)
                            nc.gpsimd.tensor_tensor(h1[:, m, :], h[:, m, :], row["ln1_w"], ALU.mult).then_inc(scaled, 1)
                            pool.wait_ge(scaled, 2 * GROUP * g + m + 1)
                            nc.gpsimd.tensor_tensor(h1[:, m, :], h1[:, m, :], row["ln1_b"], ALU.add).then_inc(h1_ready, 1)
                            pool.wait_ge(h1_ready, upto(g, m))
                            nc.gpsimd.tensor_tensor(hb[:, m, :], h1[:, m, :], row["f2_b"], ALU.add).then_inc(hb_ready, 1)
                    for n in range(GROUP + 1):
                        if n < GROUP:
                            rstd(g, 1, n)
                        if n >= 1:
                            m = n - 1
                            pool.wait_ge(normed, 2 * GROUP * g + GROUP + m + 1)
                            nc.gpsimd.tensor_tensor(h[:, m, :], h[:, m, :], row["ln2_w"], ALU.mult).then_inc(scaled, 1)
                            pool.wait_ge(scaled, 2 * GROUP * g + GROUP + m + 1)
                            nc.gpsimd.tensor_tensor(h[:, m, :], h[:, m, :], row["ln2_b"], ALU.add).then_inc(h2_ready, 1)
                    for n in range(GROUP):
                        rstd(g, 2, n)

            @block.vector
            def _(dve):
                def sum_and_stats(g, which, n, dst, in0, in1):
                    if which < 2:
                        nc.vector.tensor_tensor(dst, in0, in1, ALU.add).then_inc(resid, 1)
                        dve.wait_ge(resid, 2 * GROUP * g + which * GROUP + n + 1)
                    else:
                        nc.vector.tensor_tensor(dst, in0, in1, ALU.add).then_inc(y_summed, 1)
                        dve.wait_ge(y_summed, upto(g, n))
                    count = 3 * GROUP * g + which * GROUP + n + 1
                    nc.vector.bn_stats(stats[:], dst).then_inc(stats_ready, 1)
                    hold(dve, stats_ready, count)
                    nc.vector.bn_aggr(mv[:, n, :], stats[:]).then_inc(mean_ready, 1)
                    dve.wait_ge(mean_ready, count)
                    nc.vector.tensor_scalar(ve[:, n:n + 1], mv[:, n, 1:2], EPS, None, ALU.add).then_inc(var_ready, 1)

                def normalise(g, which, n, dst, src):
                    dve.wait_ge(rstd_ready, 3 * GROUP * g + which * GROUP + n + 1)
                    nc.vector.tensor_scalar(dst, src, mv[:, n, 0:1], rs[:, n:n + 1], ALU.subtract,
                                            ALU.mult).then_inc(normed if which < 2 else xm_ready, 1)

                def combine(g, q):
                    half, m = q // KC, q % KC
                    cols = slice(half * HALF, (half + 1) * HALF)
                    done = GQ * g + q + 1
                    dve.wait_ge(new_ready, done)
                    nc.vector.tensor_tensor(rT[:, m, cols], hT[:, m, cols], nT[:, m, cols], ALU.subtract).then_inc(h_less_n, 1)
                    dve.wait_ge(h_less_n, done)
                    nc.vector.tensor_tensor(rT[:, m, cols], rT[:, m, cols], zT[:, m, cols], ALU.mult).then_inc(z_applied, 1)
                    dve.wait_ge(z_applied, done)
                    nc.vector.tensor_tensor(nT[:, m, cols], rT[:, m, cols], nT[:, m, cols], ALU.add).then_inc(o_ready, 1)

                with dve.Fori(0, GROUPS) as g:
                    dve.wait_ge(x1_in, 16 * g + 16)
                    dve.wait_ge(agg_in, 16 * g + 16)
                    for n in range(GROUP):
                        dve.wait_ge(tp_full, TP * g)
                        nc.vector.tensor_tensor(at[:, n, :], x1t[:, n, :], agt[:, n, :], ALU.mult).then_inc(attn_ready, 1)
                    for n in range(GROUP + 1):
                        if n < GROUP:
                            dve.wait_ge(mo_full, MO * g + n + 1)
                            dve.wait_ge(xb_ready, upto(g, n))
                            sum_and_stats(g, 0, n, h[:, n, :], mo[:, n % 2, 0:D], xb[:, n, :])
                        if n >= 1:
                            normalise(g, 0, n - 1, h[:, n - 1, :], h[:, n - 1, :])
                    for n in range(GROUP + 1):
                        if n < GROUP:
                            dve.wait_ge(mo_full, MO * g + GROUP + n + 1)
                            dve.wait_ge(hb_ready, upto(g, n))
                            sum_and_stats(g, 1, n, h[:, n, :], mo[:, (GROUP + n) % 2, 0:D], hb[:, n, :])
                        if n >= 1:
                            normalise(g, 1, n - 1, h[:, n - 1, :], h[:, n - 1, :])
                    for q in range(GQ):
                        half, m = q // KC, q % KC
                        cols = slice(half * HALF, (half + 1) * HALF)
                        dve.wait_ge(hf_full, HF * g + 2 * FC + 4 * q + 4)
                        dve.wait_ge(gates, GAT * g + 2 * q + 1)
                        dve.wait_ge(tp_full, TP * g)
                        nc.vector.scalar_tensor_tensor(out=nT[:, m, cols], in0=hf[:, 3, 0:HALF], scalar=c["bhh"][:, 4 + m:5 + m],
                                                       in1=rT[:, m, cols], op0=ALU.add, op1=ALU.mult).then_inc(reset_applied, 1)
                        dve.wait_ge(reset_applied, GQ * g + q + 1)
                        nc.vector.tensor_tensor(nT[:, m, cols], nT[:, m, cols], hf[:, 2, 0:HALF], ALU.add).then_inc(new_pre, 1)
                        if q >= 1:
                            combine(g, q - 1)
                    combine(g, GQ - 1)
                    for n in range(GROUP + 1):
                        if n < GROUP:
                            dve.wait_ge(tp_out, TP * g + 3 * GROUP + n + 1)
                            sum_and_stats(g, 2, n, bk[:, n, :], bk[:, n, :], xt[:, n, :])
                        if n >= 1:
                            dve.wait_ge(stored[0], 16 * g)
                            normalise(g, 2, n - 1, xm[:, n - 1, :], bk[:, n - 1, :])


class EdgeWalk:

    def __init__(self, kit, tmp, nc, name, weighted, bank):
        def sb(what, shape, dt=F32):
            return tmp.enter_context(nc.sbuf_tensor(f"{name}_{what}", shape, dt))

        self.weighted, self.cols = weighted, HT if weighted else D
        self.seg, self.gat = sb("seg", [P, 1], I32), sb("gat", [P, 1], I32)
        self.seg_row = sb("seg_row", [P, P], I32)
        self.seg_f = sb("seg_f", [P, 1])
        self.rows, self.old, self.recv = sb("rows", [P, self.cols]), sb("old", [P, self.cols]), sb("recv", [P, HT])
        self.w = sb("w", [P, 4])
        self.same, self.earlier = sb("same", [P, P]), sb("earlier", [P, P])
        self.below, self.trash = sb("below", [P, P]), sb("trash", [P, 1])
        self.rank, self.first = sb("rank", [P, 1]), sb("first", [P, 1])
        self.to_f, self.to = sb("to_f", [P, 1]), sb("to", [P, 1], I32)
        self.sums = bank
        self.s_zeroed = kit.sem(name + "_zeroed")
        self.s_cleared = kit.sem(name + "_cleared")
        self.s_consts = kit.sem(name + "_consts")
        self.s_below_set = kit.sem(name + "_below_set")
        self.s_idx_in = kit.sem(name + "_idx_in")
        self.s_rows_in = kit.sem(name + "_rows_in")
        self.s_recv_in = kit.sem(name + "_recv_in")
        self.s_old_in = kit.sem(name + "_old_in")
        self.s_converted = kit.sem(name + "_converted")
        self.s_same_ready = kit.sem(name + "_same_ready")
        self.s_masked = kit.sem(name + "_masked")
        self.s_ranked = kit.sem(name + "_ranked")
        self.s_first_ready = kit.sem(name + "_first_ready")
        self.s_moved = kit.sem(name + "_moved")
        self.s_blended = kit.sem(name + "_blended")
        self.s_to_ready = kit.sem(name + "_to_ready")
        self.s_summed = kit.sem(name + "_summed")
        self.s_weighted = kit.sem(name + "_weighted")
        self.s_w_added = kit.sem(name + "_w_added")
        self.s_w_scaled = kit.sem(name + "_w_scaled")
        self.s_w_leaky = kit.sem(name + "_w_leaky")
        self.s_w_ready = kit.sem(name + "_w_ready")
        self.s_w_applied = kit.sem(name + "_w_applied")
        self.s_added = kit.sem(name + "_added")
        self.s_stored = kit.sem(name + "_stored")


def edge_walk_sync(nc, sp, k, seg, gat, out):
    sp.wait_ge(k.s_zeroed, 1)
    n = (ROWS + P) // P
    with sp.Fori(0, n) as t:
        sp.dma_start(out[bass.ds(t * P, P), :], k.old[:]).then_inc(k.s_cleared, 16)
    sp.wait_ge(k.s_cleared, 16 * n)
    with sp.Fori(0, EDGE_TILES) as t:
        sp.wait_ge(k.s_stored, t * 16)
        with nc.allow_non_contiguous_dma("one index per partition"):
            sp.dma_start(k.seg[:], seg[bass.ds(t * P, P)].unsqueeze(1)).then_inc(k.s_idx_in, 16)
            sp.dma_start(k.gat[:], gat[bass.ds(t * P, P)].unsqueeze(1)).then_inc(k.s_idx_in, 16)
        sp.dma_start(k.seg_row[:], seg[bass.ds(t * P, P)].partition_broadcast(P)).then_inc(k.s_idx_in, 16)


def edge_walk_pool(nc, pool, k, table, out):
    nc.gpsimd.memset(k.old[:], 0.0).then_inc(k.s_zeroed, 1)
    nc.gpsimd.iota(k.trash[:], [[0, 1]], base=TRASH, channel_multiplier=1,
                   allow_small_or_imprecise_dtypes=True).then_inc(k.s_consts, 1)
    nc.gpsimd.memset(k.below[:], 1.0).then_inc(k.s_below_set, 1)
    pool.wait_ge(k.s_below_set, 1)
    nc.gpsimd.affine_select(out=k.below[:], in_=k.below[:], compare_op=ALU.is_gt, fill=0.0, base=0,
                            pattern=[[-1, P]], channel_multiplier=1).then_inc(k.s_consts, 1)
    pool.wait_ge(k.s_cleared, 16 * ((ROWS + P) // P))
    with pool.Fori(0, EDGE_TILES) as t:
        hold(pool, k.s_idx_in, t * 48 + 48)
        nc.gpsimd.indirect_dma_start(k.rows[:], None, table, bass.IndirectOffsetOnAxis(ap=k.gat[:, 0:1], axis=0)) \
            .then_inc(k.s_rows_in, 16)
        if k.weighted:
            nc.gpsimd.indirect_dma_start(k.recv[:], None, table, bass.IndirectOffsetOnAxis(ap=k.seg[:, 0:1], axis=0)) \
                .then_inc(k.s_recv_in, 16)
        hold(pool, k.s_to_ready, t + 1)
        nc.gpsimd.indirect_dma_start(k.old[:], None, out, bass.IndirectOffsetOnAxis(ap=k.to[:, 0:1], axis=0)) \
            .then_inc(k.s_old_in, 16)
        hold(pool, k.s_added, t + 1)
        nc.gpsimd.indirect_dma_start(out, bass.IndirectOffsetOnAxis(ap=k.to[:, 0:1], axis=0), k.old[:], None) \
            .then_inc(k.s_stored, 16)
        hold(pool, k.s_stored, t * 16 + 16)


def edge_walk_vector(nc, dve, k):
    dve.wait_ge(k.s_consts, 2)
    with dve.Fori(0, EDGE_TILES) as t:
        dve.wait_ge(k.s_idx_in, t * 48 + 48)
        nc.vector.tensor_copy(k.seg_f[:], k.seg[:]).then_inc(k.s_converted, 1)
        dve.wait_ge(k.s_converted, t + 1)
        nc.vector.tensor_scalar(k.same[:], k.seg_row[:], k.seg_f[:, 0:1], None, ALU.is_equal).then_inc(k.s_same_ready, 1)
        dve.wait_ge(k.s_same_ready, t + 1)
        nc.vector.tensor_tensor(k.earlier[:], k.same[:], k.below[:], ALU.mult).then_inc(k.s_masked, 1)
        dve.wait_ge(k.s_masked, t + 1)
        nc.vector.tensor_reduce(k.rank[:], k.earlier[:], AX.X, ALU.add).then_inc(k.s_ranked, 1)
        dve.wait_ge(k.s_ranked, t + 1)
        nc.vector.tensor_scalar(k.first[:], k.rank[:], 0.0, None, ALU.is_equal).then_inc(k.s_first_ready, 1)
        nc.vector.tensor_tensor(k.to_f[:], k.seg_f[:], k.trash[:], ALU.subtract).then_inc(k.s_moved, 1)
        dve.wait_ge(k.s_first_ready, t + 1)
        dve.wait_ge(k.s_moved, t + 1)
        nc.vector.scalar_tensor_tensor(out=k.to_f[:], in0=k.to_f[:], scalar=k.first[:, 0:1], in1=k.trash[:],
                                       op0=ALU.mult, op1=ALU.add).then_inc(k.s_blended, 1)
        dve.wait_ge(k.s_blended, t + 1)
        nc.vector.tensor_copy(k.to[:], k.to_f[:]).then_inc(k.s_to_ready, 1)
        if k.weighted:
            dve.wait_ge(k.s_rows_in, t * 16 + 16)
            dve.wait_ge(k.s_recv_in, t * 16 + 16)
            nc.vector.tensor_tensor(k.w[:, 0:1], k.recv[:, D:D + 1], k.rows[:, D + 1:D + 2], ALU.add).then_inc(k.s_w_added, 1)
            dve.wait_ge(k.s_w_added, t + 1)
            nc.vector.tensor_scalar(k.w[:, 1:2], k.w[:, 0:1], ALPHA, None, ALU.mult).then_inc(k.s_w_scaled, 1)
            dve.wait_ge(k.s_w_scaled, t + 1)
            nc.vector.tensor_tensor(k.w[:, 2:3], k.w[:, 0:1], k.w[:, 1:2], ALU.max).then_inc(k.s_w_leaky, 1)
            dve.wait_ge(k.s_w_ready, t + 1)
            nc.vector.tensor_scalar(k.rows[:], k.rows[:], k.w[:, 3:4], None, ALU.mult).then_inc(k.s_w_applied, 1)
            dve.wait_ge(k.s_w_applied, t + 1)
            nc.vector.tensor_copy(k.rows[:, D:D + 1], k.w[:, 3:4]).then_inc(k.s_weighted, 1)
        dve.wait_ge(k.s_old_in, t * 16 + 16)
        dve.wait_ge(k.s_summed, t + 1)
        nc.vector.tensor_tensor(k.old[:], k.old[:], k.sums[:, 0:k.cols], ALU.add).then_inc(k.s_added, 1)


def edge_walk_scalar(nc, act, k):
    if k.weighted:
        with act.Fori(0, EDGE_TILES) as t:
            act.wait_ge(k.s_w_leaky, t + 1)
            nc.scalar.activation(k.w[:, 3:4], k.w[:, 2:3], ACT.Exp, scale=-1.0).then_inc(k.s_w_ready, 1)


def edge_walk_tensor(nc, pe, k):
    with pe.Fori(0, EDGE_TILES) as t:
        pe.wait_ge(k.s_same_ready, t + 1)
        if k.weighted:
            pe.wait_ge(k.s_weighted, t + 1)
        else:
            pe.wait_ge(k.s_rows_in, t * 16 + 16)
        nc.tensor.matmul(k.sums[:, 0:k.cols], k.same[:], k.rows[:], start=True, stop=True).then_inc(k.s_summed, 1)


def final_rows(nc, kit, c, xmid, sums, out):
    with ExitStack() as tmp:
        def sb(name, shape, dt=F32):
            return tmp.enter_context(nc.sbuf_tensor(name, shape, dt))

        xm, sm, y = sb("f_xmid", [P, GROUP, D]), sb("f_sums", [P, GROUP, D + 1]), sb("f_y", [P, GROUP, D])
        rd, rs = sb("f_rweights", [P, GROUP]), sb("f_rstd", [P, GROUP])
        stats, mv, ve = sb("f_stats", [P, nc.vector.BN_STATS_DIM]), sb("f_mv", [P, GROUP, 2]), sb("f_var_eps", [P, GROUP])
        xm_in = [kit.sem(f"f_xmid_loaded{n}") for n in range(GROUP)]
        sm_in = [kit.sem(f"f_sums_loaded{n}") for n in range(GROUP)]
        stored = [kit.sem(f"out_stored{n}") for n in range(GROUP)]
        clamped, inverted, divided, summed, stats_ready, mean_ready, var_ready, rstd_ready, ready = (
            kit.sem("f_" + s) for s in ("clamped", "inverted", "divided", "summed", "stats", "mean", "var", "rstd", "ready"))
        with nc.Block() as block:

            @block.sync
            def _(sp):
                with sp.Fori(0, GROUPS) as g:
                    for n in range(GROUP):
                        sp.wait_ge(ready, before(g, n, GROUP))
                        sp.dma_start(xm[:, n, :], xmid[tile_rows(g, n), :]).then_inc(xm_in[n], 16)
                        sp.dma_start(sm[:, n, :], sums[tile_rows(g, n), 0:D + 1]).then_inc(sm_in[n], 16)

            @block.scalar
            def _(act):
                with act.Fori(0, GROUPS) as g:
                    for n in range(GROUP):
                        act.wait_ge(ready, upto(g, n))
                        act.dma_start(out[tile_rows(g, n), :], y[:, n, :]).then_inc(stored[n], 16)
                for n in range(GROUP):
                    act.wait_ge(stored[n], 16 * GROUPS)

            @block.gpsimd
            def _(pool):
                with pool.Fori(0, GROUPS) as g:
                    for n in range(GROUP):
                        pool.wait_ge(var_ready, upto(g, n))
                        nc.gpsimd.tensor_tensor(rs[:, n:n + 1], ve[:, n:n + 1], c["half"][:], ALU.pow).then_inc(rstd_ready, 1)

            @block.vector
            def _(dve):
                def normalise(g, n):
                    dve.wait_ge(rstd_ready, upto(g, n))
                    nc.vector.tensor_scalar(y[:, n, :], y[:, n, :], mv[:, n, 0:1], rs[:, n:n + 1], ALU.subtract,
                                            ALU.mult).then_inc(ready, 1)

                with dve.Fori(0, GROUPS) as g:
                    for n in range(GROUP):
                        done = upto(g, n)
                        dve.wait_ge(sm_in[n], 16 * g + 16)
                        nc.vector.tensor_scalar(rd[:, n:n + 1], sm[:, n, D:D + 1], TINY, None, ALU.max).then_inc(clamped, 1)
                        dve.wait_ge(clamped, done)
                        nc.vector.reciprocal(rd[:, n:n + 1], rd[:, n:n + 1]).then_inc(inverted, 1)
                        dve.wait_ge(inverted, done)
                        dve.wait_ge(stored[n], 16 * g)
                        nc.vector.tensor_scalar(y[:, n, :], sm[:, n, 0:D], rd[:, n:n + 1], 0.0, ALU.mult,
                                                ALU.max).then_inc(divided, 1)
                        dve.wait_ge(divided, done)
                        dve.wait_ge(xm_in[n], 16 * g + 16)
                        nc.vector.tensor_tensor(y[:, n, :], y[:, n, :], xm[:, n, :], ALU.add).then_inc(summed, 1)
                        dve.wait_ge(summed, done)
                        nc.vector.bn_stats(stats[:], y[:, n, :]).then_inc(stats_ready, 1)
                        hold(dve, stats_ready, done)
                        nc.vector.bn_aggr(mv[:, n, :], stats[:]).then_inc(mean_ready, 1)
                        dve.wait_ge(mean_ready, done)
                        nc.vector.tensor_scalar(ve[:, n:n + 1], mv[:, n, 1:2], EPS, None, ALU.add).then_inc(var_ready, 1)
                        if n >= 1:
                            normalise(g, n - 1)
                    normalise(g, GROUP - 1)


WINDOW = 8
WINDOWS = ROWS // WINDOW
WPT = P // WINDOW
SLOTS = 3
EROW = 32
RPW = SLOTS * P // EROW
WCHUNK = WINDOWS // GROUP
KEYS = TILES * WINDOW
EPP = EDGES // P
LINES = EPP // EROW
NO_KEY = -1.0

assert EPP % EROW == 0 and WCHUNK <= P and KEYS <= 512


def prepare_edges(nc, kit, c, dst, pairs):
    c["lo"], c["key"] = kit.sb("edge_lo", [P, SLOTS, WINDOWS]), kit.sb("edge_key", [P, SLOTS, WINDOWS])
    c["flag"] = kit.sb("edges_irregular", [1, 1], I32)
    with ExitStack() as tmp:
        def sb(name, shape, dt=F32):
            return tmp.enter_context(nc.sbuf_tensor(name, shape, dt))

        cols = GROUP * SLOTS * P
        d0, d1 = sb("e_dst", [P, EPP], I32), sb("e_dst_next", [P, EPP], I32)
        firsts = sb("e_firsts", [P, LINES])
        falls, fall = sb("e_falls", [P, EPP]), sb("e_fall", [P, 1])
        bounds, less = sb("e_bounds", [P, WINDOWS + 1], F16), sb("e_less", [P, 2, WINDOWS + 1], BF16)
        ones, onesb = sb("e_ones", [P, 1]), sb("e_ones_bf", [P, 1], BF16)
        cnt, row0, span = sb("e_count", [1, WINDOWS + 1]), sb("e_row0", [1, WINDOWS]), sb("e_span", [1, WINDOWS])
        bad = sb("e_bad", [1, 4])
        steps, idx_f, idx = sb("e_steps", [P, RPW]), sb("e_idx_f", [P, GROUP, RPW]), sb("e_idx", [P, GROUP, RPW], I32)
        r0 = sb("e_r0", [P, GROUP])
        first_node = sb("e_first_node", [P, GROUP])
        ends = sb("e_ends", [P, GROUP, RPW, 2 * EROW], I32)
        lo_i, hi_i = sb("e_lo_i", [P, cols], I32), sb("e_hi_i", [P, cols], I32)
        lo_f, hi_f = sb("e_lo_f", [P, cols]), sb("e_hi_f", [P, cols])
        rel, inside, below = sb("e_rel", [P, cols]), sb("e_inside", [P, cols]), sb("e_below", [P, cols])
        pc = tmp.enter_context(nc.psum_tensor("e_counts", [P, 2, 512], F32))
        pr = tmp.enter_context(nc.psum_tensor("e_small", [P, 512], F32))
        pf = tmp.enter_context(nc.psum_tensor("e_falls_sum", [P, 512], F32))
        pt = tmp.enter_context(nc.psum_tensor("e_turned", [P, 2, 512], F32))

        loaded, consts = kit.sem("e_loaded"), kit.sem("e_consts")
        firsts_ready, compared, counted = kit.sem("e_firsts_ready"), kit.sem("e_compared"), kit.sem("e_counted")
        step, fall_ready, row0_ready = kit.sem("e_step"), kit.sem("e_fall_ready"), kit.sem("e_row0_ready")
        small, idx_ready, fetched = kit.sem("e_small_ready"), kit.sem("e_idx_ready"), kit.sem("e_fetched")
        keys_ready, turned, kept = kit.sem("e_keys_ready"), kit.sem("e_turned_ready"), kit.sem("e_kept")
        half = (WINDOWS + 1) // 2 + 1
        parts = [(0, half), (half, WINDOWS + 1)]
        with nc.Block() as block:

            @block.sync
            def _(sp):
                sp.dma_start(d0[:], dst[0:EDGES].rearrange("(p e) -> p e", p=P)).then_inc(loaded, 16)
                sp.dma_start(d1[:], dst[1:EDGES + 1].rearrange("(p e) -> p e", p=P)).then_inc(loaded, 16)

            @block.gpsimd
            def _(pool):
                nc.gpsimd.iota(bounds[:], [[WINDOW, WINDOWS + 1]], base=0, channel_multiplier=0,
                               allow_small_or_imprecise_dtypes=True).then_inc(consts, 1)
                nc.gpsimd.iota(steps[:], [[1, RPW]], base=0, channel_multiplier=0,
                               allow_small_or_imprecise_dtypes=True).then_inc(consts, 1)
                nc.gpsimd.iota(first_node[:], [[WINDOW * WCHUNK, GROUP]], base=0, channel_multiplier=WINDOW,
                               allow_small_or_imprecise_dtypes=True).then_inc(consts, 1)
                nc.gpsimd.memset(ones[:], 1.0).then_inc(consts, 1)
                nc.gpsimd.memset(onesb[:], 1.0).then_inc(consts, 1)
                pool.wait_ge(idx_ready, 1)
                for t in range(GROUP):
                    for r in range(RPW):
                        nc.gpsimd.indirect_dma_start(ends[0:WCHUNK, t, r, :], None, pairs,
                                                     bass.IndirectOffsetOnAxis(ap=idx[0:WCHUNK, t, r:r + 1], axis=0)) \
                            .then_inc(fetched, 16)

            @block.vector
            def _(dve):
                n = 0

                def link(ins):
                    nonlocal n
                    n += 1
                    ins.then_inc(step, 1)
                    dve.wait_ge(step, n)

                dve.wait_ge(consts, 5)
                dve.wait_ge(loaded, 32)
                nc.vector.tensor_copy(firsts[:], d0[:].rearrange("p (l e) -> p l e", e=EROW)[:, :, 0]).then_inc(firsts_ready, 1)
                dve.wait_ge(firsts_ready, 1)
                for j in range(LINES):
                    if j >= 2:
                        dve.wait_ge(counted, j - 1)
                    nc.vector.tensor_scalar(less[:, j % 2, :], bounds[:], firsts[:, j:j + 1], None, ALU.is_gt).then_inc(compared, 1)
                link(nc.vector.tensor_tensor(falls[:], d0[:], d1[:], ALU.is_gt))
                nc.vector.tensor_reduce(fall[:], falls[:], AX.X, ALU.add).then_inc(fall_ready, 1)
                dve.wait_ge(counted, LINES + 1)
                for b, (a0, a1) in enumerate(parts):
                    link(nc.vector.tensor_copy(cnt[:, a0:a1], pc[0:1, b, 0:a1 - a0]))
                link(nc.vector.tensor_scalar(row0[:], cnt[:, 0:WINDOWS], 1.0, 0.0, ALU.subtract, ALU.max))
                nc.vector.tensor_tensor(span[:], cnt[:, 1:WINDOWS + 1], row0[:], ALU.subtract).then_inc(row0_ready, 1)
                dve.wait_ge(row0_ready, 1)
                real = -(-N_NODES // WINDOW)
                link(nc.vector.tensor_scalar(span[:, 0:real], span[:, 0:real], float(RPW - 1), None, ALU.is_gt))
                link(nc.vector.tensor_reduce(bad[:, 0:1], span[:, 0:real], AX.X, ALU.add))
                link(nc.vector.tensor_tensor(bad[:, 1:2], bad[:, 0:1], pf[0:1, 0:1], ALU.add))
                link(nc.vector.tensor_scalar(bad[:, 2:3], bad[:, 1:2], 1.0, None, ALU.min))
                nc.vector.tensor_copy(c["flag"][:], bad[:, 2:3])
                dve.wait_ge(small, 1)
                link(nc.vector.tensor_copy(r0[0:WCHUNK, :], pr[0:WCHUNK, 8:8 + GROUP]))
                link(nc.vector.tensor_tensor(idx_f[0:WCHUNK], steps[0:WCHUNK, :].unsqueeze(1).broadcast_to([WCHUNK, GROUP, RPW]),
                                             r0[0:WCHUNK, :].unsqueeze(2).broadcast_to([WCHUNK, GROUP, RPW]), ALU.add))
                link(nc.vector.tensor_scalar(idx_f[0:WCHUNK], idx_f[0:WCHUNK], float(EDGES // EROW - 1), None, ALU.min))
                nc.vector.tensor_copy(idx[0:WCHUNK], idx_f[0:WCHUNK]).then_inc(idx_ready, 1)
                dve.wait_ge(fetched, 16 * GROUP * RPW)
                W = WCHUNK
                flat = ends[0:W].rearrange("p t r (e x) -> p (t r e) x", x=2)
                link(nc.vector.tensor_scalar(lo_i[0:W, :], flat[:, :, 0], P - 1, None, ALU.bitwise_and))
                link(nc.vector.tensor_scalar(hi_i[0:W, :], flat[:, :, 0], 7, None, ALU.logical_shift_right))
                link(nc.vector.tensor_copy(lo_f[0:W, :], lo_i[0:W, :]))
                link(nc.vector.tensor_scalar(hi_f[0:W, :], hi_i[0:W, :], float(WINDOW), 1.0, ALU.mult, ALU.add))
                per = SLOTS * P
                for t in range(GROUP):
                    link(nc.vector.tensor_scalar(rel[0:W, t * per:(t + 1) * per], flat[:, t * per:(t + 1) * per, 1],
                                                 first_node[0:W, t:t + 1], None, ALU.subtract))
                link(nc.vector.tensor_scalar(inside[0:W, :], rel[0:W, :], 0.0, None, ALU.is_ge))
                link(nc.vector.tensor_scalar(below[0:W, :], rel[0:W, :], float(WINDOW), None, ALU.is_lt))
                link(nc.vector.tensor_tensor(inside[0:W, :], inside[0:W, :], below[0:W, :], ALU.mult))
                link(nc.vector.tensor_tensor(hi_f[0:W, :], hi_f[0:W, :], rel[0:W, :], ALU.add))
                link(nc.vector.tensor_tensor(hi_f[0:W, :], hi_f[0:W, :], inside[0:W, :], ALU.mult))
                nc.vector.tensor_scalar(hi_f[0:W, :], hi_f[0:W, :], NO_KEY, None, ALU.add).then_inc(keys_ready, 1)

            @block.tensor
            def _(pe):
                pe.wait_ge(consts, 5)
                for j in range(LINES):
                    pe.wait_ge(compared, j + 1)
                    for b, (a0, a1) in enumerate(parts):
                        last = nc.tensor.matmul(pc[0:1, b, 0:a1 - a0], onesb[:], less[:, j % 2, a0:a1], start=(j == 0),
                                                stop=(j == LINES - 1))
                    last.then_inc(counted, 1)
                pe.wait_ge(fall_ready, 1)
                nc.tensor.matmul(pf[0:1, 0:1], fall[:], ones[:], start=True, stop=True).then_inc(counted, 1)
                pe.wait_ge(row0_ready, 1)
                for t in range(GROUP):
                    last = nc.tensor.matmul(pr[0:WCHUNK, 8 + t:9 + t], row0[:, t * WCHUNK:(t + 1) * WCHUNK], ones[0:1, 0:1],
                                            start=True, stop=True)
                last.then_inc(small, 1)
                pe.wait_ge(keys_ready, 1)
                n = 0
                for src in (lo_f, hi_f):
                    for t in range(GROUP):
                        if n >= 2:
                            pe.wait_ge(kept, n - 1)
                        for k in range(SLOTS):
                            a0 = (t * SLOTS + k) * P
                            last = nc.tensor.transpose(pt[:, n % 2, k * P:k * P + WCHUNK], src[0:WCHUNK, a0:a0 + P],
                                                       c["ident"][0:WCHUNK, 0:WCHUNK])
                        last.then_inc(turned, 1)
                        n += 1

            @block.scalar
            def _(act):
                n = 0
                for dst_t in (c["lo"], c["key"]):
                    for t in range(GROUP):
                        act.wait_ge(turned, n + 1)
                        nc.scalar.copy(dst_t[:, :, t * WCHUNK:(t + 1) * WCHUNK],
                                       pt[:, n % 2, 0:SLOTS * P].rearrange("p (k w) -> p k w", k=SLOTS)[:, :, 0:WCHUNK]) \
                            .then_inc(kept, 1)
                        n += 1


HOT_SLOTS = 4


def count_and_sum(nc, kit, c, x1_parts, dst, src, x1, agg, counts):
    with ExitStack() as tmp:
        def sb(name, shape, dt=F32):
            return tmp.enter_context(nc.sbuf_tensor(name, shape, dt))

        n128, n392 = sb("b_nodes", [P, P], BF16), sb("b_keys", [P, KEYS], F16)
        identh = sb("b_ident", [P, P], F16)
        ends = sb("b_ends", [P, 2, 2, SLOTS, WPT])
        lo1, key1 = sb("b_lo_hot", [P, HOT_SLOTS, SLOTS, P], BF16), sb("b_key_hot", [P, HOT_SLOTS, SLOTS, KEYS], BF16)
        ca = sb("b_counts", [P, 2, TILES, P], F16)
        cb = sb("b_counts_turned", [P, 2, TILES * P], F16)
        sums = sb("b_sums", [P, 2, D])
        pcnt = tmp.enter_context(nc.psum_tensor("b_pcounts", [P, 2, 512], F32))
        pturn = tmp.enter_context(nc.psum_tensor("b_pturned", [P, 2, 1024], F16))
        pagg = tmp.enter_context(nc.psum_tensor("b_pagg", [P, 2, 512], F32))
        walk = EdgeWalk(kit, tmp, nc, "l0", False, pagg[:, 0, :])
        consts, ident_ready = kit.sem("b_consts"), kit.sem("b_ident_ready")
        ends_ready, hot, built, kept = kit.sem("b_ends_ready"), kit.sem("b_hot"), kit.sem("b_built"), kit.sem("b_kept")
        turned, cb_ready, summed, sums_ready = (kit.sem("b_turned"), kit.sem("b_turned_kept"), kit.sem("b_summed"),
                                                kit.sem("b_sums_ready"))
        cb_stored = [kit.sem(f"b_counts_stored{k}") for k in range(2)]
        sums_stored = [kit.sem(f"b_sums_stored{k}") for k in range(2)]

        def steps(eng, step):
            step(0, 0, 0, True, False)
            with eng.Fori(0, (TILES - 1) // 2) as i:
                for k in range(2):
                    step(2 * i + 1 + k, (1 + k) % 2, i, True, True)
            step(TILES, TILES % 2, (TILES - 1) // 2, False, True)

        with nc.Block() as block:

            @block.sync
            def _(sp):
                flag = sp.value_load(c["flag"][0:1, 0:1], min_val=0, max_val=1)
                with sp.If(flag == 0):
                    def step(s, k, i, build, use):
                        if use:
                            o = 1 - k
                            rows = bass.ds((s - 1) * P, P)
                            sp.wait_ge(cb_ready, GROUPS * s)
                            sp.dma_start(counts[rows, :], cb[:, o, :]).then_inc(cb_stored[o], 16)
                            sp.wait_ge(sums_ready, s)
                            sp.dma_start(agg[rows, :], sums[:, o, :]).then_inc(sums_stored[o], 16)

                    steps(sp, step)
                    for o in range(2):
                        sp.wait_ge(cb_stored[o], 16 * ((TILES + 1 - o) // 2))
                        sp.wait_ge(sums_stored[o], 16 * ((TILES + 1 - o) // 2))
                with sp.Else():
                    edge_walk_sync(nc, sp, walk, dst, src, agg)

            @block.gpsimd
            def _(pool):
                flag = pool.value_load(c["flag"][0:1, 0:1], min_val=0, max_val=1)
                with pool.If(flag == 0):
                    nc.gpsimd.iota(n128[:], [[1, P]], base=0, channel_multiplier=0,
                                   allow_small_or_imprecise_dtypes=True).then_inc(consts, 1)
                    nc.gpsimd.iota(n392[:], [[1, KEYS]], base=0, channel_multiplier=0,
                                   allow_small_or_imprecise_dtypes=True).then_inc(consts, 1)

                    def step(s, k, i, build, use):
                        if build:
                            if use:
                                pool.wait_ge(hot, WPT * (s - 1))
                            for j, what in enumerate((c["lo"], c["key"])):
                                last = nc.gpsimd.tensor_copy(ends[:, k, j], what[:, :, bass.ds(WPT * s, WPT)])
                            last.then_inc(ends_ready, 1)

                    steps(pool, step)
                with pool.Else():
                    edge_walk_pool(nc, pool, walk, x1, agg)

            @block.vector
            def _(dve):
                flag = dve.value_load(c["flag"][0:1, 0:1], min_val=0, max_val=1)
                with dve.If(flag == 0):
                    nc.vector.tensor_copy(identh[:], c["ident"][:]).then_inc(ident_ready, 1)
                    dve.wait_ge(consts, 2)

                    def step(s, k, i, build, use):
                        if not build:
                            return
                        dve.wait_ge(ends_ready, s + 1)
                        for j in range(WPT):
                            h = j % HOT_SLOTS
                            if use or j >= HOT_SLOTS:
                                dve.wait_ge(built, WPT * s + j + 1 - HOT_SLOTS)
                            for q in range(SLOTS):
                                nc.vector.tensor_scalar(lo1[:, h, q, :], n128[:], ends[:, k, 0, q, j:j + 1], None, ALU.is_equal)
                                last = nc.vector.tensor_scalar(key1[:, h, q, :], n392[:], ends[:, k, 1, q, j:j + 1], None,
                                                               ALU.is_equal)
                            last.then_inc(hot, 1)

                    steps(dve, step)
                with dve.Else():
                    edge_walk_vector(nc, dve, walk)

            @block.tensor
            def _(pe):
                flag = pe.value_load(c["flag"][0:1, 0:1], min_val=0, max_val=1)
                with pe.If(flag == 0):
                    pe.wait_ge(ident_ready, 1)

                    def step(s, k, i, build, use):
                        o = 1 - k

                        def use_source_tile(hi):
                            bank, at = hi // GROUP, hi % GROUP
                            if hi == 0:
                                pe.wait_ge(kept, WPT * s)
                                pe.wait_ge(sums_ready, s - 1)
                            if at == 0 and (build or bank >= 1):
                                pe.wait_ge(cb_ready, GROUPS * (s - 1) + max(bank - 1, 0))
                            for m in range(3):
                                last = nc.tensor.matmul(pagg[:, o, 0:D], ca[:, o, hi, :], x1_parts[:, m, hi, :],
                                                        start=(hi == 0 and m == 0), stop=(hi == TILES - 1 and m == 2))
                            if hi == TILES - 1:
                                last.then_inc(summed, 1)
                            last = nc.tensor.transpose(pturn[:, bank % 2, at * P:(at + 1) * P], ca[:, o, hi, :], identh[:])
                            if at == GROUP - 1:
                                last.then_inc(turned, 1)

                        for j in range(WPT):
                            if build:
                                h = j % HOT_SLOTS
                                pe.wait_ge(hot, WPT * s + j + 1)
                                if use or j >= 2:
                                    pe.wait_ge(kept, WPT * s + j - 1)
                                for q in range(SLOTS):
                                    last = nc.tensor.matmul(pcnt[:, j % 2, 0:KEYS], lo1[:, h, q, :], key1[:, h, q, :],
                                                            start=(q == 0), stop=(q == SLOTS - 1))
                                last.then_inc(built, 1)
                            if use:
                                for hi in range(TILES * j // WPT, TILES * (j + 1) // WPT):
                                    use_source_tile(hi)

                    steps(pe, step)
                with pe.Else():
                    edge_walk_tensor(nc, pe, walk)

            @block.scalar
            def _(act):
                flag = act.value_load(c["flag"][0:1, 0:1], min_val=0, max_val=1)
                with act.If(flag == 0):
                    def step(s, k, i, build, use):
                        o, banks = 1 - k, 0
                        for j in range(WPT):
                            if build:
                                act.wait_ge(built, WPT * s + j + 1)
                                if j == 0 and use:
                                    act.wait_ge(summed, s - 1)
                                    act.wait_ge(turned, GROUPS * (s - 1))
                                nc.scalar.copy(ca[:, k, :, j * WINDOW:(j + 1) * WINDOW],
                                               pcnt[:, j % 2, 0:KEYS].rearrange("p (t w) -> p t w", w=WINDOW)).then_inc(kept, 1)
                            while use and (banks + 1) * GROUP <= TILES * (j + 1) // WPT:
                                act.wait_ge(turned, GROUPS * (s - 1) + banks + 1)
                                if banks == 0:
                                    act.wait_ge(cb_stored[o], 16 * i)
                                nc.scalar.copy(cb[:, o, banks * GROUP * P:(banks + 1) * GROUP * P],
                                               pturn[:, banks % 2, 0:GROUP * P]).then_inc(cb_ready, 1)
                                banks += 1
                        if use:
                            act.wait_ge(summed, s)
                            act.wait_ge(sums_stored[o], 16 * i)
                            nc.scalar.copy(sums[:, o, :], pagg[:, o, 0:D]).then_inc(sums_ready, 1)

                    steps(act, step)
                with act.Else():
                    edge_walk_scalar(nc, act, walk)


def weigh_and_sum(nc, kit, c, src, dst, table, counts, out):
    with ExitStack() as tmp:
        def sb(name, shape, dt=F32):
            return tmp.enter_context(nc.sbuf_tensor(name, shape, dt))

        cols = GROUP * P
        per_bank = 512 // P
        tab = sb("d_table", [P, TILES, HT])
        t_col, scale_col, ones = sb("d_t", [P, TILES]), sb("d_scale", [P, TILES]), sb("d_ones", [P, P])
        diag, s_all = sb("d_diag", [P, 2, per_bank, P]), sb("d_s", [P, TILES * P])
        cnt, wgt = sb("d_counts", [P, GROUP, cols], F16), sb("d_weights", [P, GROUP, cols])
        st = sb("d_sums", [P, GROUP, D + 1])
        acc = tmp.enter_context(nc.psum_tensor("d_acc", [P, GROUP + 1, 512], F32))
        pbc = acc[:, GROUP, :]
        walk = EdgeWalk(kit, tmp, nc, "l1", True, acc[:, 0, :])
        tab_in, ones_ready, diag_ready, spread, s_ready = (
            kit.sem("d_" + s) for s in ("table_loaded", "ones_ready", "diag_ready", "spread", "s_ready"))
        t_taken, exp_t, table_scaled = kit.sem("d_t_taken"), kit.sem("d_exp_t"), kit.sem("d_table_scaled")
        shifted, exped, weighted = kit.sem("d_shifted"), kit.sem("d_exped"), kit.sem("d_weighted")
        used, summed, kept = kit.sem("d_weights_used"), kit.sem("d_summed"), kit.sem("d_kept")
        cnt_in = [kit.sem(f"d_counts_loaded{n}") for n in range(GROUP)]
        stored = [kit.sem(f"d_sums_stored{n}") for n in range(GROUP)]
        banks = -(-TILES // per_bank)

        def batches(eng, batch):
            with eng.Fori(0, GROUPS) as J:
                batch(J, 0, True, False)
                with eng.Fori(1, GROUPS - 1) as b:
                    batch(J, b, False, False)
                batch(J, GROUPS - 1, False, True)

        with nc.Block() as block:

            @block.sync
            def _(sp):
                flag = sp.value_load(c["flag"][0:1, 0:1], min_val=0, max_val=1)
                with sp.If(flag == 0):
                    for g in range(GROUPS):
                        sp.dma_start(tab[:, g * GROUP:(g + 1) * GROUP, :],
                                     table[g * GROUP * P:(g + 1) * GROUP * P, :].rearrange("(t p) c -> p t c", p=P)) \
                            .then_inc(tab_in, 16)

                    def batch(J, b, first, last):
                        g = J * GROUPS + b
                        for n in range(GROUP):
                            sp.wait_ge(weighted, before(g, n, GROUP))
                            sp.dma_start(cnt[:, n, :], counts[bass.ds((b * GROUP + n) * P, P), bass.ds(J * cols, cols)]) \
                                .then_inc(cnt_in[n], 16)

                    batches(sp, batch)
                with sp.Else():
                    edge_walk_sync(nc, sp, walk, src, dst, out)

            @block.vector
            def _(dve):
                flag = dve.value_load(c["flag"][0:1, 0:1], min_val=0, max_val=1)
                with dve.If(flag == 0):
                    dve.wait_ge(tab_in, 16 * GROUPS)
                    nc.vector.tensor_copy(t_col[:], tab[:, :, D + 1]).then_inc(t_taken, 1)
                    for q in range(banks):
                        if q >= 2:
                            dve.wait_ge(spread, q - 1)
                        for t in range(q * per_bank, min(TILES, (q + 1) * per_bank)):
                            last = nc.vector.tensor_scalar(diag[:, q % 2, t % per_bank, :], c["ident"][:], tab[:, t, D:D + 1],
                                                           None, ALU.mult)
                        last.then_inc(diag_ready, 1)
                    dve.wait_ge(exp_t, 1)
                    dve.wait_ge(diag_ready, banks)
                    for t in range(TILES):
                        nc.vector.tensor_scalar(tab[:, t, 0:D], tab[:, t, 0:D], scale_col[:, t:t + 1], None, ALU.mult)
                    nc.vector.tensor_copy(tab[:, :, D], scale_col[:]).then_inc(table_scaled, 1)
                    dve.wait_ge(s_ready, banks)
                    dve.wait_ge(t_taken, 1)

                    def weigh(g, n):
                        dve.wait_ge(exped, upto(g, n))
                        dve.wait_ge(cnt_in[n], 16 * g + 16)
                        nc.vector.tensor_tensor(wgt[:, n, :], wgt[:, n, :], cnt[:, n, :], ALU.mult).then_inc(weighted, 1)

                    def batch(J, b, first, last):
                        g = J * GROUPS + b
                        for n in range(GROUP):
                            dve.wait_ge(used, before(g, n, GROUP))
                            nc.vector.tensor_scalar(wgt[:, n, :], s_all[:, bass.ds(J * cols, cols)],
                                                    t_col[:, bass.ds(b * GROUP + n, 1)], 0.0, ALU.add, ALU.max).then_inc(shifted, 1)
                            if n >= 2:
                                weigh(g, n - 2)
                        weigh(g, GROUP - 2)
                        weigh(g, GROUP - 1)

                    batches(dve, batch)
                with dve.Else():
                    edge_walk_vector(nc, dve, walk)

            @block.scalar
            def _(act):
                flag = act.value_load(c["flag"][0:1, 0:1], min_val=0, max_val=1)
                with act.If(flag == 0):
                    act.wait_ge(t_taken, 1)
                    nc.scalar.activation(scale_col[:], t_col[:], ACT.Exp, scale=-ALPHA).then_inc(exp_t, 1)
                    for q in range(banks):
                        act.wait_ge(spread, q + 1)
                        m = min(TILES - q * per_bank, per_bank) * P
                        nc.scalar.copy(s_all[:, q * 512:q * 512 + m], pbc[:, 0:m]).then_inc(s_ready, 1)

                    def batch(J, b, first, last):
                        g = J * GROUPS + b
                        for n in range(GROUP):
                            act.wait_ge(shifted, upto(g, n))
                            nc.scalar.activation(wgt[:, n, :], wgt[:, n, :], ACT.Exp, scale=-(1.0 - ALPHA)).then_inc(exped, 1)
                        for r in range(GROUP if last else 0):
                            if r < GROUP - 1:
                                act.wait_ge(summed, J * (GROUP - 1) + r + 1)
                            else:
                                act.wait_ge(used, J * TILES + TILES)
                            act.wait_ge(stored[r], 16 * J)
                            nc.scalar.copy(st[:, r, :], acc[:, r, 0:D + 1]).then_inc(kept, 1)

                    batches(act, batch)
                with act.Else():
                    edge_walk_scalar(nc, act, walk)

            @block.tensor
            def _(pe):
                flag = pe.value_load(c["flag"][0:1, 0:1], min_val=0, max_val=1)
                with pe.If(flag == 0):
                    pe.wait_ge(ones_ready, 1)
                    for q in range(banks):
                        pe.wait_ge(diag_ready, q + 1)
                        if q >= 1:
                            pe.wait_ge(s_ready, q)
                        m = min(TILES - q * per_bank, per_bank) * P
                        nc.tensor.matmul(pbc[:, 0:m], ones[:], diag[:, q % 2].rearrange("p t c -> p (t c)")[:, 0:m], start=True,
                                         stop=True).then_inc(spread, 1)
                    pe.wait_ge(table_scaled, 1)

                    def batch(J, b, first, last):
                        g = J * GROUPS + b
                        if first:
                            pe.wait_ge(kept, J * GROUP)
                        for n in range(GROUP):
                            pe.wait_ge(weighted, upto(g, n))
                            for r in range(GROUP):
                                ins = nc.tensor.matmul(acc[:, r, 0:D + 1], wgt[:, n, r * P:(r + 1) * P],
                                                       tab[:, bass.ds(b * GROUP + n, 1), 0:D + 1],
                                                       start=(first and n == 0), stop=(last and n == GROUP - 1))
                                if last and n == GROUP - 1 and r < GROUP - 1:
                                    ins.then_inc(summed, 1)
                            ins.then_inc(used, 1)

                    batches(pe, batch)
                with pe.Else():
                    edge_walk_tensor(nc, pe, walk)

            @block.gpsimd
            def _(pool):
                flag = pool.value_load(c["flag"][0:1, 0:1], min_val=0, max_val=1)
                with pool.If(flag == 0):
                    nc.gpsimd.memset(ones[:], 1.0).then_inc(ones_ready, 1)
                    with pool.Fori(0, GROUPS) as J:
                        for r in range(GROUP):
                            pool.wait_ge(kept, J * GROUP + r + 1)
                            pool.dma_start(out[bass.ds((J * GROUP + r) * P, P), 0:D + 1], st[:, r, :]).then_inc(stored[r], 16)
                    for r in range(GROUP):
                        pool.wait_ge(stored[r], 16 * GROUPS)
                with pool.Else():
                    edge_walk_pool(nc, pool, walk, table, out)

_WEIGHTS = ["Wq", "Wk", "Wv", "O_w", "O_b", "ln1_w", "ln1_b", "f1_w", "f1_b", "f2_w", "f2_b", "ln2_w", "ln2_b",
            "gru_w_ih", "gru_w_hh", "gru_b_ih", "gru_b_hh"]


def build(nc, a, out):
    w = {n: a["L0_gnn_" + n] for n in _WEIGHTS}
    w["L1_W"], w["L1_a"] = a["L1_gnn_W"], a["L1_gnn_a"]

    def scratch(name, shape):
        return nc.dram_tensor(name, shape, F32, kind="Internal").ap()

    x1, xmid = scratch("x1_table", [ROWS, D]), scratch("xmid", [ROWS, D])
    table = scratch("node_table", [ROWS, HT])
    agg, sums = scratch("agg", [ROWS + P, D]), scratch("sums", [ROWS + P, HT])
    counts = nc.dram_tensor("edge_counts", [ROWS, ROWS], F16, kind="Internal").ap()
    with ExitStack() as ctx:
        kit = Kit(nc, ctx)
        c = load_constants(nc, kit, w)
        prepare_edges(nc, kit, c, a["dst"], a["pairs"])
        with nc.sbuf_tensor("x1_parts", [P, 3, TILES, D], BF16) as parts:
            with kit.stage() as k:
                attention_rows(nc, k, c, a["x"], x1, parts)
            with kit.stage() as k:
                count_and_sum(nc, k, c, parts, a["dst"], a["src"], x1, agg, counts)
        with kit.stage() as k:
            update_rows(nc, k, c, a["x"], x1, agg, xmid, table)
        with kit.stage() as k:
            weigh_and_sum(nc, k, c, a["src"], a["dst"], table, counts, sums)
        final_rows(nc, kit, c, xmid, sums, out)


def _pad(a, n, fill):
    a = np.asarray(a)
    return np.concatenate([a, np.full((n - a.shape[0],) + a.shape[1:], fill, a.dtype)])


def kernel(**inputs):
    import concourse.bacc as _bacc
    from concourse.bass_utils import run_bass_kernel_spmd as _run

    host = dict(inputs)
    host["x"] = _pad(inputs["x"], ROWS, 0)
    host["src"] = _pad(inputs["src"], EDGES + P, ROWS - 1)
    host["dst"] = _pad(inputs["dst"], EDGES + P, ROWS - 1)
    host["pairs"] = np.stack([host["src"][:EDGES], host["dst"][:EDGES]], axis=-1).reshape(EDGES // EROW, 2 * EROW)
    nc = _bacc.Bacc("TRN2", target_bir_lowering=False, num_devices=1)
    arrays, aps = {}, {}
    for name, a in host.items():
        a = np.ascontiguousarray(a)
        arrays[f"in_{name}"] = a
        aps[name] = nc.dram_tensor(f"in_{name}", a.shape, mybir.dt.from_np(a.dtype), kind="ExternalInput").ap()
    out = nc.dram_tensor("out_rows", [ROWS, D], F32, kind="ExternalOutput").ap()
    build(nc, aps, out)
    r = _run(nc, [arrays], core_ids=[0])
    return r.results[0]["out_rows"][:N_NODES]
```

```python
from contextlib import ExitStack, contextmanager

import numpy as np

import concourse.bass as bass
from concourse import mybir

F32 = mybir.dt.float32
F32R = mybir.dt.float32r
BF16 = mybir.dt.bfloat16
F16 = mybir.dt.float16
I32 = mybir.dt.int32
ALU = mybir.AluOpType
ACT = mybir.ActivationFunctionType
AX = mybir.AxisListType

P = 128
N_NODES = 6250
N_EDGES = 206250
D = 256
KC = D // P
N_HEADS = 8
D_HEAD = D // N_HEADS
D_FFN = 2 * D
FC = D_FFN // P
TILES = -(-N_NODES // P)
GROUP = 7
GROUPS = TILES // GROUP
HALF = GROUP * P // 2
ROWS = TILES * P
TRASH = ROWS
EROW = 64
SLOTS = 3
EDGE_TILES = -(-(N_EDGES + SLOTS * P) // (EROW * P)) * EROW
EDGES = EDGE_TILES * P
HT = D + 2
EPS = 1e-5
SCORE_SCALE = float(D_HEAD) ** -0.5
ALPHA = 0.2
TINY = 1.2e-38

assert TILES == GROUPS * GROUP and GROUPS % 2 == 1


def before(g, n, slots):
    return GROUP * g + max(0, n - slots + 1)


def upto(g, n):
    return GROUP * g + n + 1


def tile_rows(g, n):
    return bass.ds(g * (GROUP * P) + n * P, P)


class Kit:

    def __init__(self, nc, ctx, whole=None):
        self.nc, self.ctx, self.sems = nc, ctx, []
        self.whole = whole or self

    def sb(self, name, shape, dt=F32):
        return self.ctx.enter_context(self.nc.sbuf_tensor(name, shape, dt))

    def ps(self, name, shape, dt=F32):
        return self.ctx.enter_context(self.nc.psum_tensor(name, shape, dt))

    def sem(self, name):
        self.sems.append(self.ctx.enter_context(self.nc.semaphore(name)))
        return self.sems[-1]

    def pool_dma_sem(self, name):
        return self.whole.sem(name)

    @contextmanager
    def stage(self):
        with ExitStack() as ctx:
            kit = Kit(self.nc, ctx, self.whole)
            yield kit
            with self.nc.Block() as block:

                @block.gpsimd
                def _(pool):
                    for sem in kit.sems:
                        pool.sem_clear(sem)


def lasting(nc, kit):
    c = {"ident": kit.sb("ident", [P, P]), "half": kit.sb("minus_half", [P, 1]), "flag": kit.sb("edges_irregular", [1, 1], I32),
         "st": kit.sb("s_and_t", [P, TILES, 2])}
    zeroed = kit.sem("ident_zeroed")
    with nc.Block() as block:

        @block.gpsimd
        def _(pool):
            nc.gpsimd.memset(c["ident"][:], 0.0).then_inc(zeroed, 1)
            nc.gpsimd.memset(c["half"][:], -0.5)
            pool.wait_ge(zeroed, 1)
            nc.gpsimd.affine_select(out=c["ident"][:], in_=c["ident"][:], compare_op=ALU.not_equal, fill=1.0,
                                    base=0, pattern=[[-1, P]], channel_multiplier=1)
    return c


def split_rows(ap):
    return ap.rearrange("(k p) n -> p k n", p=P)


class UpdateWeights:

    def __init__(self, kit, w):
        self.w = w
        self.wo, self.f1, self.f2 = kit.sb("wo", [P, KC, D]), kit.sb("f1", [P, KC, D_FFN]), kit.sb("f2", [P, FC, D])
        self.gru = kit.sb("gru", [P, KC, 4 * D])
        self.whh = kit.sb("whh", [P, KC, 3 * D])
        self.w1 = kit.sb("w1", [P, KC, HT])
        self.rows = kit.sb("rows", [P, 6, D])
        self.f1_b, self.bih, self.bhh = kit.sb("f1_bias", [P, FC]), kit.sb("bih", [P, 6]), kit.sb("bhh", [P, 6])
        self.brz, self.a, self.junk = kit.sb("brz", [P, 4]), kit.sb("a_bc", [P, 2, D]), kit.sb("wa_products", [P, D])
        self.first_in, self.rest_in, self.folded = kit.sem("first_weights_in"), kit.sem("rest_weights_in"), kit.sem("weights_folded")
        self.FIRST, self.REST, self.FOLDED = 16 * 7, 16 * 9, 3 + 4 * KC

    def load_first(self, sp):
        sp.dma_start(self.wo[:], split_rows(self.w["O_w"])).then_inc(self.first_in, 16)
        for j, name in enumerate(("O_b", "ln1_w", "ln1_b", "f2_b", "ln2_w", "ln2_b")):
            sp.dma_start(self.rows[:, j, :], self.w[name].partition_broadcast(P)).then_inc(self.first_in, 16)

    def load_rest(self, nc, sp):
        for name, dst in (("f1_w", self.f1[:]), ("f2_w", self.f2[:]), ("gru_w_hh", self.whh[:]), ("L1_W", self.w1[:, :, 0:D]),
                          ("gru_w_ih", self.gru[:, :, 0:3 * D])):
            sp.dma_start(dst, split_rows(self.w[name])).then_inc(self.rest_in, 16)
        sp.dma_start(self.a[:].rearrange("p a b -> p (a b)"), self.w["L1_a"].partition_broadcast(P)).then_inc(self.rest_in, 16)
        for name, dst in (("f1_b", self.f1_b), ("gru_b_ih", self.bih), ("gru_b_hh", self.bhh)):
            with nc.allow_non_contiguous_dma("a few hundred bias values, once"):
                sp.dma_start(dst[:], self.w[name].rearrange("(m p) -> p m", p=P)).then_inc(self.rest_in, 16)

    def fold(self, nc, dve):
        dve.wait_ge(self.rest_in, self.REST)
        g = self.gru
        nc.vector.tensor_copy(g[:, :, 3 * D:4 * D], self.whh[:, :, 2 * D:3 * D]).then_inc(self.folded, 1)
        nc.vector.tensor_tensor(g[:, :, 0:2 * D], g[:, :, 0:2 * D], self.whh[:, :, 0:2 * D], ALU.add).then_inc(self.folded, 1)
        nc.vector.tensor_tensor(self.brz[:], self.bih[:, 0:4], self.bhh[:, 0:4], ALU.add).then_inc(self.folded, 1)
        n = 3
        for k in range(KC):
            for j in range(2):
                nc.vector.tensor_tensor(self.junk[:], self.w1[:, k, 0:D], self.a[:, j, :], ALU.mult).then_inc(self.folded, 1)
                n += 1
                dve.wait_ge(self.folded, n)
                nc.vector.tensor_reduce(self.w1[:, k, D + j:D + j + 1], self.junk[:], AX.X, ALU.add).then_inc(self.folded, 1)
                n += 1
                dve.wait_ge(self.folded, n)


QUAD = 4
PASS = 2 * QUAD
LAST_TILE = (TILES // PASS) * PASS


def tile_steps(eng, step, delay):
    for T in range(PASS):
        step(T, T % QUAD)
    with eng.Fori(1, LAST_TILE // PASS) as i:
        for u in range(PASS):
            step(PASS * i + u, u % QUAD)
    for T in range(LAST_TILE, TILES + delay):
        step(T, T % QUAD)


def attention_rows(nc, kit, c, w, x, x1_out, parts):
    with ExitStack() as tmp:
        def sb(name, shape, dt=F32):
            return tmp.enter_context(nc.sbuf_tensor(name, shape, dt))

        def ps(name, shape):
            return tmp.enter_context(nc.psum_tensor(name, shape, F32))

        wqkv = sb("wqkv", [P, KC, 3 * D])
        xt, xT = sb("qx", [P, QUAD, D]), sb("qxT", [P, 2, D])
        qk, v = sb("qk", [P, 2, 2 * D]), sb("v", [P, QUAD, D])
        prod = sb("qk_products", [P, N_HEADS, N_HEADS, D_HEAD])
        av = sb("av_products", [P, 2, N_HEADS, D_HEAD, N_HEADS])
        sc = sb("scores", [P, QUAD, N_HEADS, N_HEADS])
        mx, sm, rs = (sb(s, [P, 2, N_HEADS]) for s in ("score_max", "prob_sum", "prob_rsum"))
        x1 = sb("x1_tile", [P, QUAD, D])
        tp, pqk, pv = ps("q_tp", [P, 2, 512]), ps("p_qk", [P, 2, 512]), ps("p_v", [P, 2, 512])

        w_loaded = kit.sem("wqkv_loaded")
        x_loaded = [kit.sem(f"q_x_loaded{n}") for n in range(QUAD)]
        xT_in_psum, xT_ready = kit.sem("q_xT_in_psum"), kit.sem("q_xT_ready")
        qkv_in_psum, qk_ready, v_ready = kit.sem("qkv_in_psum"), kit.sem("qk_ready"), kit.sem("v_ready")
        products, reduced, maxed = kit.sem("qk_products_done"), kit.sem("scores_reduced"), kit.sem("scores_maxed")
        shifted, exped = kit.sem("scores_shifted"), kit.sem("scores_exped")
        summed, inverted, probs = kit.sem("probs_summed"), kit.sem("probs_inverted"), kit.sem("probs_ready")
        av_ready, x1_ready = kit.sem("av_products_ready"), kit.sem("x1_ready")
        x1_stored = [kit.sem(f"x1_stored{n}") for n in range(QUAD)]
        high, low = kit.sem("x1_high"), kit.sem("x1_low")

        def is_tile(t):
            return not isinstance(t, int) or 0 <= t < TILES

        def free(eng, sem, t, slots):
            if not isinstance(t, int) or t >= slots:
                eng.wait_ge(sem, t + 1 - slots)

        def stored_before(eng, T, u, t, slot):
            if isinstance(t, int):
                if t >= QUAD:
                    eng.wait_ge(x1_stored[slot], 16 * (t // QUAD))
            else:
                eng.wait_ge(x1_stored[slot], (T - u) * (16 // QUAD) - (0 if u >= 3 else 16))

        def part(k, t):
            return parts[:, k, t:t + 1, :] if isinstance(t, int) else parts[:, k, bass.ds(t, 1), :]

        def rows(t):
            return bass.ds(t * P, P)

        with nc.Block() as block:

            @block.sync
            def _(sp):
                def step(T, u):
                    if is_tile(T):
                        free(sp, xT_in_psum, T, QUAD)
                        sp.dma_start(xt[:, u, :], x[rows(T), :]).then_inc(x_loaded[u], 16)
                    if isinstance(T, int) and T == 0:
                        for j, name in enumerate(("Wq", "Wk", "Wv")):
                            sp.dma_start(wqkv[:, :, j * D:(j + 1) * D], split_rows(w[name])).then_inc(w_loaded, 16)

                tile_steps(sp, step, 0)

            @block.tensor
            def _(pe):
                def step(T, u):
                    if is_tile(T):
                        pe.wait_ge(x_loaded[u], 16 * (T // QUAD) + 16 if isinstance(T, int) else (T - u) * (16 // QUAD) + 16)
                        free(pe, xT_ready, T, 2)
                        for k in range(KC):
                            last = nc.tensor.transpose(tp[:, u % 2, k * P:(k + 1) * P], xt[:, u, k * P:(k + 1) * P],
                                                       c["ident"][:])
                        last.then_inc(xT_in_psum, 1)
                    t, s = T - 1, (u - 1) % 2
                    if is_tile(t):
                        pe.wait_ge(xT_ready, T)
                        if isinstance(T, int) and T == 1:
                            pe.wait_ge(w_loaded, 16 * 3)
                        free(pe, v_ready, t, 2)
                        for k in range(KC):
                            nc.tensor.matmul(pqk[:, s, :], xT[:, s, k * P:(k + 1) * P], wqkv[:, k, 0:2 * D],
                                             start=(k == 0), stop=(k == KC - 1))
                        for k in range(KC):
                            last = nc.tensor.matmul(pv[:, s, 0:D], xT[:, s, k * P:(k + 1) * P], wqkv[:, k, 2 * D:3 * D],
                                                    start=(k == 0), stop=(k == KC - 1))
                        last.then_inc(qkv_in_psum, 1)

                tile_steps(pe, step, 1)

            @block.scalar
            def _(act):
                def step(T, u):
                    if is_tile(T):
                        act.wait_ge(xT_in_psum, T + 1)
                        free(act, qkv_in_psum, T, 2)
                        nc.scalar.copy(xT[:, u % 2, :], tp[:, u % 2, 0:D]).then_inc(xT_ready, 1)
                    if is_tile(T - 2):
                        act.wait_ge(shifted, T - 1)
                        q = (u - 2) % QUAD
                        nc.scalar.activation(sc[:, q], sc[:, q], ACT.Exp, scale=SCORE_SCALE).then_inc(exped, 1)
                    t, q = T - 1, (u - 1) % QUAD
                    if is_tile(t):
                        act.wait_ge(qkv_in_psum, T)
                        free(act, products, t, 2)
                        nc.scalar.copy(qk[:, q % 2, :], pqk[:, q % 2, :]).then_inc(qk_ready, 1)
                        free(act, av_ready, t, QUAD)
                        nc.scalar.copy(v[:, q, :], pv[:, q % 2, 0:D]).then_inc(v_ready, 1)
                    if is_tile(T - 4):
                        act.wait_ge(x1_ready, T - 3)
                        nc.scalar.copy(part(0, T - 4), x1[:, u:u + 1, :]).then_inc(high, 1)
                        act.dma_start(x1_out[rows(T - 4), :], x1[:, u, :]).then_inc(x1_stored[u], 16)

                tile_steps(act, step, 4)
                for n in range(QUAD):
                    act.wait_ge(x1_stored[n], 16 * len(range(n, TILES, QUAD)))

            @block.gpsimd
            def _(pool):
                def step(T, u):
                    if is_tile(T - 4):
                        pool.wait_ge(high, T - 3)
                        nc.gpsimd.tensor_tensor(part(1, T - 4), x1[:, u:u + 1, :], part(0, T - 4), ALU.subtract).then_inc(low, 1)
                    t, q = T - 2, (u - 2) % QUAD
                    if is_tile(t):
                        pool.wait_ge(inverted, T - 1)
                        nc.gpsimd.tensor_tensor(sc[:, q], sc[:, q], rs[:, q % 2].unsqueeze(2).broadcast_to([P, N_HEADS, N_HEADS]),
                                                ALU.mult).then_inc(probs, 1)
                        pool.wait_ge(v_ready, T - 1)
                        pool.wait_ge(probs, T - 1)
                        free(pool, x1_ready, t, 2)
                        p_b = sc[:, q].unsqueeze(2).broadcast_to([P, N_HEADS, D_HEAD, N_HEADS])
                        v_b = v[:, q, :].rearrange("p (g d) -> p d g", g=N_HEADS).unsqueeze(1) \
                            .broadcast_to([P, N_HEADS, D_HEAD, N_HEADS])
                        nc.gpsimd.tensor_tensor(av[:, q % 2], p_b, v_b, ALU.mult).then_inc(av_ready, 1)

                tile_steps(pool, step, 4)

            @block.vector
            def _(dve):
                def step(T, u):
                    a, qa, b, qb = T - 1, (u - 1) % QUAD, T - 2, (u - 2) % QUAD
                    if is_tile(a):
                        dve.wait_ge(qk_ready, T)
                        q_b = qk[:, qa % 2, 0:D].rearrange("p (h d) -> p h d", h=N_HEADS).unsqueeze(2) \
                            .broadcast_to([P, N_HEADS, N_HEADS, D_HEAD])
                        k_b = qk[:, qa % 2, D:2 * D].rearrange("p (h d) -> p h d", h=N_HEADS).unsqueeze(1) \
                            .broadcast_to([P, N_HEADS, N_HEADS, D_HEAD])
                        free(dve, reduced, a, 1)
                        nc.vector.tensor_tensor(prod[:], q_b, k_b, ALU.mult).then_inc(products, 1)
                    if is_tile(b):
                        dve.wait_ge(exped, T - 1)
                        free(dve, probs, b, 2)
                        nc.vector.tensor_reduce(sm[:, qb % 2], sc[:, qb], AX.X, ALU.add).then_inc(summed, 1)
                    if is_tile(a):
                        dve.wait_ge(products, T)
                        free(dve, av_ready, a, QUAD)
                        nc.vector.tensor_reduce(sc[:, qa], prod[:], AX.X, ALU.add).then_inc(reduced, 1)
                    if is_tile(b):
                        dve.wait_ge(summed, T - 1)
                        nc.vector.reciprocal(rs[:, qb % 2], sm[:, qb % 2]).then_inc(inverted, 1)
                    if is_tile(a):
                        dve.wait_ge(reduced, T)
                        free(dve, shifted, a, 2)
                        nc.vector.tensor_reduce(mx[:, qa % 2], sc[:, qa], AX.X, ALU.max).then_inc(maxed, 1)
                    if is_tile(a):
                        dve.wait_ge(maxed, T)
                        nc.vector.tensor_tensor(sc[:, qa], sc[:, qa],
                                                mx[:, qa % 2].unsqueeze(2).broadcast_to([P, N_HEADS, N_HEADS]),
                                                ALU.subtract).then_inc(shifted, 1)
                    t, q = T - 3, (u - 3) % QUAD
                    if is_tile(t):
                        dve.wait_ge(av_ready, T - 2)
                        stored_before(dve, T, u, t, q)
                        free(dve, low, t, QUAD)
                        nc.vector.tensor_reduce(x1[:, q, :], av[:, q % 2].rearrange("p h d g -> p (h d) g"), AX.X,
                                                ALU.add).then_inc(x1_ready, 1)

                tile_steps(dve, step, 3)


def group_steps(eng, body):
    body(0)
    with eng.Fori(0, (GROUPS - 1) // 2) as i:
        for k in range(2):
            body(2 * i + 1 + k)


def hold(eng, sem, value):
    if isinstance(value, int):
        eng.wait_ge(sem, value)
        return
    value = eng.snap(eng.to_reg(value))
    eng.wait_ge(sem, 1)
    eng.wait_ge(sem, value)


def group_rows(g):
    return bass.ds(g * (GROUP * P), GROUP * P)


UPDATE_STEPS = (
    ("attn", 0), ("attn", 1), ("O", 0), ("attn", 2), ("O", 1), ("attn", 3), ("O", 2), ("attn", 4), ("O", 3), ("attn", 5),
    ("O", 4), ("h1", 0), ("attn", 6), ("O", 5), ("h1", 1), ("O", 6), ("h1", 2), ("h1", 3),
    ("f1", 0), ("h1", 4), ("h1", 5), ("h1", 6), ("f1", 1),
    ("f2", 0), ("f2", 1), ("f2", 2), ("f2", 3), ("h2", 0), ("f2", 4), ("h2", 1), ("f2", 5), ("h2", 2), ("f2", 6), ("h2", 3),
    ("gates", 0), ("gates", 1), ("h2", 4), ("h2", 5), ("h2", 6), ("gates", 2), ("gru", 0), ("gru", 1), ("gru", 2), ("gates", 3),
    ("xmid", 0), ("xmid", 1), ("table", 0), ("xmid", 2), ("gru", 3), ("gru", 4), ("gru", 5), ("gru", 6), ("table", 1),
    ("table", 2), ("xmid", 3), ("xmid", 4), ("table", 3), ("xmid", 5), ("table", 4), ("xmid", 6), ("table", 5), ("table", 6))
TURNS = tuple(s for s in UPDATE_STEPS if s[0] in ("attn", "h1", "h2", "gru", "xmid"))


def turned(*step):
    return TURNS.index(step) + 1


def update_rows(nc, kit, c, weights, x, x1, agg, xmid_out, table_out):
    with ExitStack() as tmp:
        def sb(name, shape, dt=F32):
            return tmp.enter_context(nc.sbuf_tensor(name, shape, dt))

        def ps(name, shape):
            return tmp.enter_context(nc.psum_tensor(name, shape, F32))

        xt, x1t, agt = (sb(f"u_{s}", [P, GROUP, D]) for s in ("x", "x1", "agg"))
        at, xb, h, h1, hb = (sb(f"u_{s}", [P, GROUP, D]) for s in ("attn", "x_plus_bias", "h", "h1", "h1_plus_bias"))
        bk, xm = sb("u_gru_rows", [P, GROUP, D]), sb("u_xmid", [P, GROUP, D])
        ht = sb("u_table", [P, GROUP, HT])
        tT = sb("u_attnT", [P, KC, GROUP * P])
        hT = sb("u_hT", [P, KC, GROUP * P])
        gT = sb("u_hiddenT", [P, FC, GROUP * P])
        rT, zT, nT = (sb(f"u_{s}T", [P, KC, GROUP * P]) for s in "rzn")
        stats, mv = sb("u_stats", [P, nc.vector.BN_STATS_DIM]), sb("u_mean_var", [P, GROUP, 2])
        ve, rs = sb("u_var_eps", [P, GROUP]), sb("u_rstd", [P, GROUP])
        tp, mo, hf = ps("u_tp", [P, 2, 512]), ps("u_mo", [P, 2, 512]), ps("u_hf", [P, 4, 512])

        x_in, x1_in, agg_in = kit.sem("u_x_loaded"), kit.sem("u_x1_loaded"), kit.sem("u_agg_loaded")
        stored = [kit.sem("xmid_stored"), kit.sem("table_stored")]
        attn_ready, xb_ready = kit.sem("attn_ready"), kit.sem("x_plus_bias_ready")
        tp_full, tp_out = kit.sem("u_tp_full"), kit.sem("u_tp_evacuated")
        mo_full, resid = kit.sem("u_mo_full"), kit.sem("u_residual_added")
        ht_ready, st_kept = kit.sem("table_row_ready"), kit.sem("s_and_t_kept")
        hf_full, relued = kit.sem("u_hf_full"), kit.sem("u_hidden_relued")
        gates, new_pre, new_ready, o_ready = (kit.sem(s) for s in ("gates_ready", "new_gate_summed", "new_gate_ready",
                                                                    "gru_out_ready"))
        var_ready, rstd_ready, normed = kit.sem("var_ready"), kit.sem("rstd_ready"), kit.sem("rows_normed")
        h1_ready, hb_ready, h2_ready, xm_ready = (kit.sem(s) for s in ("h1_ready", "h1_plus_bias_ready", "h2_ready",
                                                                       "xmid_ready"))
        stats_ready, mean_ready, y_summed = kit.sem("u_stats_ready"), kit.sem("u_mean_ready"), kit.sem("gru_plus_x_summed")
        reset_applied = kit.sem("reset_gate_applied")
        h_less_n, z_applied = kit.sem("h_less_n"), kit.sem("update_gate_applied")
        TP, MO, HF = 5 * GROUP, 3 * GROUP, 24
        REL, GAT, GQ = 2 * FC, 2 * 2 * KC, 2 * KC

        def first_time(eng, g, sem, value):
            if isinstance(g, int):
                eng.wait_ge(sem, value)

        with nc.Block() as block:

            @block.sync
            def _(sp):
                weights.load_first(sp)

                def group(g):
                    for dst, src, sem, free in ((x1t, x1, x1_in, attn_ready), (agt, agg, agg_in, attn_ready),
                                                (xt, x, x_in, xm_ready)):
                        sp.wait_ge(free, GROUP * g)
                        sp.dma_start(dst[:], src[group_rows(g), 0:D].rearrange("(n p) d -> p n d", p=P)).then_inc(sem, 16)
                    if isinstance(g, int):
                        weights.load_rest(nc, sp)

                group_steps(sp, group)

            @block.tensor
            def _(pe):
                def turn(g, use, src):
                    pe.wait_ge(tp_out, TP * g + max(0, use - 1))
                    for k in range(KC):
                        last = nc.tensor.transpose(tp[:, use % 2, k * P:(k + 1) * P], src(k), c["ident"][:])
                    last.then_inc(tp_full, 1)

                def rows_matmul(use, lhsT, rhs, chunks, cols):
                    for k in range(chunks):
                        last = nc.tensor.matmul(mo[:, use % 2, 0:cols], lhsT(k), rhs(k), start=(k == 0),
                                                stop=(k == chunks - 1))
                    last.then_inc(mo_full, 1)

                def half_matmul(slot, w, col, src, half):
                    for k in range(KC):
                        last = nc.tensor.matmul(hf[:, slot, 0:HALF], w[:, k, col:col + P],
                                                src[:, k, half * HALF:(half + 1) * HALF],
                                                start=(k == 0), stop=(k == KC - 1))
                    last.then_inc(hf_full, 1)

                def step(g, what, n):
                    if what == "attn":
                        pe.wait_ge(attn_ready, upto(g, n))
                        turn(g, turned(what, n) - 1, lambda k: at[:, n, k * P:(k + 1) * P])
                    elif what == "O":
                        pe.wait_ge(tp_out, TP * g + turned("attn", n))
                        first_time(pe, g, weights.first_in, weights.FIRST)
                        if n < 2:
                            pe.wait_ge(ht_ready, GROUP * g)
                        else:
                            pe.wait_ge(resid, 2 * GROUP * g + n - 1)
                        rows_matmul(n, lambda k: tT[:, k, n * P:(n + 1) * P], lambda k: weights.wo[:, k, :], KC, D)
                    elif what == "h1":
                        pe.wait_ge(h1_ready, upto(g, n))
                        turn(g, turned(what, n) - 1, lambda k: h1[:, n, k * P:(k + 1) * P])
                    elif what == "f1":
                        pe.wait_ge(tp_out, TP * g + turned("h1", 3 if n == 0 else GROUP - 1))
                        first_time(pe, g, weights.rest_in, weights.REST)
                        for m in range(FC):
                            use = n * FC + m
                            if use < 2:
                                pe.wait_ge(gates, GAT * g)
                            elif use < 4:
                                pe.wait_ge(new_pre, GQ * g)
                            else:
                                pe.wait_ge(relued, REL * g + use - 3)
                            half_matmul(use % 4, weights.f1, m * P, hT, n)
                    elif what == "f2":
                        pe.wait_ge(relued, REL * g + (FC if n < 3 else 2 * FC))
                        pe.wait_ge(resid, 2 * GROUP * g + GROUP + n - 1)
                        rows_matmul(GROUP + n, lambda m: gT[:, m, n * P:(n + 1) * P], lambda m: weights.f2[:, m, :], FC, D)
                    elif what == "h2":
                        pe.wait_ge(h2_ready, upto(g, n))
                        turn(g, turned(what, n) - 1, lambda k: h[:, n, k * P:(k + 1) * P])
                    elif what == "gates":
                        half, m = n // KC, n % KC
                        first_time(pe, g, weights.folded, weights.FOLDED)
                        pe.wait_ge(tp_out, TP * g + turned("h2", 3 if half == 0 else GROUP - 1))
                        for slot in range(4):
                            if n >= 1:
                                if slot < 2:
                                    pe.wait_ge(gates, GAT * g + 2 * (n - 1) + slot + 1)
                                else:
                                    pe.wait_ge(new_pre, GQ * g + n)
                            half_matmul(slot, weights.gru, slot * D + m * P, hT, half)
                    elif what == "gru":
                        pe.wait_ge(o_ready, GQ * g + (KC if n < 3 else 2 * KC))
                        turn(g, turned(what, n) - 1, lambda k: nT[:, k, n * P:(n + 1) * P])
                    elif what == "xmid":
                        pe.wait_ge(xm_ready, upto(g, n))
                        turn(g, turned(what, n) - 1, lambda k: xm[:, n, k * P:(k + 1) * P])
                    else:
                        pe.wait_ge(tp_out, TP * g + turned("xmid", n))
                        if n < 2:
                            pe.wait_ge(resid, 2 * GROUP * g + 2 * GROUP)
                        else:
                            pe.wait_ge(ht_ready, GROUP * g + n - 1)
                        rows_matmul(2 * GROUP + n, lambda k: tT[:, k, n * P:(n + 1) * P], lambda k: weights.w1[:, k, :], KC, HT)

                def group(g):
                    for what, n in UPDATE_STEPS:
                        step(g, what, n)

                group_steps(pe, group)

            @block.scalar
            def _(act):
                def evacuate(g, what, n, dst):
                    use = turned(what, n) - 1
                    act.wait_ge(tp_full, TP * g + use + 1)
                    nc.scalar.copy(dst, tp[:, use % 2, 0:D].rearrange("p (k c) -> p k c", k=KC)).then_inc(tp_out, 1)

                def new_gate(g, q):
                    half, m = q // KC, q % KC
                    act.wait_ge(new_pre, GQ * g + q + 1)
                    s = nT[:, m, half * HALF:(half + 1) * HALF]
                    nc.scalar.activation(s, s, ACT.Tanh, bias=weights.bih[:, 4 + m:5 + m]).then_inc(new_ready, 1)

                def step(g, what, n):
                    if what == "attn":
                        act.wait_ge(mo_full, MO * g)
                        evacuate(g, what, n, tT[:, :, n * P:(n + 1) * P])
                    elif what in ("h1", "h2"):
                        act.wait_ge(o_ready, GQ * g)
                        evacuate(g, what, n, hT[:, :, n * P:(n + 1) * P])
                    elif what == "f1":
                        first_time(act, g, weights.rest_in, weights.REST)
                        for m in range(FC):
                            use = n * FC + m
                            act.wait_ge(hf_full, HF * g + use + 1)
                            nc.scalar.activation(gT[:, m, n * HALF:(n + 1) * HALF], hf[:, use % 4, 0:HALF], ACT.Relu,
                                                 bias=weights.f1_b[:, m:m + 1]).then_inc(relued, 1)
                    elif what == "gates":
                        half, m = n // KC, n % KC
                        first_time(act, g, weights.folded, weights.FOLDED)
                        if n >= 1:
                            new_gate(g, n - 1)
                        for slot, dst in ((0, rT), (1, zT)):
                            act.wait_ge(hf_full, HF * g + 2 * FC + 4 * n + slot + 1)
                            nc.scalar.activation(dst[:, m, half * HALF:(half + 1) * HALF], hf[:, slot, 0:HALF], ACT.Sigmoid,
                                                 bias=weights.brz[:, slot * KC + m:slot * KC + m + 1]).then_inc(gates, 1)
                    elif what == "gru":
                        evacuate(g, what, n, bk[:, n, :].rearrange("p (k c) -> p k c", k=KC))
                    elif what == "xmid":
                        evacuate(g, what, n, tT[:, :, n * P:(n + 1) * P])
                        if n == 1:
                            new_gate(g, GQ - 1)
                    elif what == "table":
                        act.wait_ge(mo_full, MO * g + 2 * GROUP + n + 1)
                        act.wait_ge(stored[1], 16 * g)
                        act.wait_ge(st_kept, g)
                        nc.scalar.copy(ht[:, n, :], mo[:, (2 * GROUP + n) % 2, 0:HT]).then_inc(ht_ready, 1)

                def group(g):
                    for what, n in UPDATE_STEPS:
                        step(g, what, n)
                    act.wait_ge(xm_ready, GROUP * g + GROUP)
                    act.dma_start(xmid_out[group_rows(g), :].rearrange("(n p) d -> p n d", p=P), xm[:]).then_inc(stored[0], 16)
                    act.wait_ge(ht_ready, GROUP * g + GROUP)
                    act.dma_start(table_out[group_rows(g), :].rearrange("(n p) d -> p n d", p=P), ht[:]).then_inc(stored[1], 16)
                    nc.scalar.copy(c["st"][:, bass.ds(g * GROUP, GROUP), :], ht[:, :, D:D + 2]).then_inc(st_kept, 1)

                group_steps(act, group)
                act.wait_ge(stored[0], 16 * GROUPS)
                act.wait_ge(stored[1], 16 * GROUPS)

            @block.gpsimd
            def _(pool):
                def rstd(g, which, n):
                    pool.wait_ge(var_ready, 3 * GROUP * g + which * GROUP + n + 1)
                    nc.gpsimd.tensor_tensor(rs[:, n:n + 1], ve[:, n:n + 1], c["half"][:], ALU.pow).then_inc(rstd_ready, 1)

                def group(g):
                    first_time(pool, g, weights.first_in, weights.FIRST)
                    for n in range(GROUP):
                        pool.wait_ge(x_in, 16 * g + 16)
                        pool.wait_ge(resid, 2 * GROUP * g)
                        nc.gpsimd.tensor_tensor(xb[:, n, :], xt[:, n, :], weights.rows[:, 0, :], ALU.add).then_inc(xb_ready, 1)
                    for which in range(2):
                        for n in range(GROUP):
                            rstd(g, which, n)
                    for n in range(GROUP):
                        rstd(g, 2, n)

                group_steps(pool, group)

            @block.vector
            def _(dve):
                def sum_and_stats(g, which, n, dst, in0, in1):
                    if which < 2:
                        nc.vector.tensor_tensor(dst, in0, in1, ALU.add).then_inc(resid, 1)
                        dve.wait_ge(resid, 2 * GROUP * g + which * GROUP + n + 1)
                    else:
                        nc.vector.tensor_tensor(dst, in0, in1, ALU.add).then_inc(y_summed, 1)
                        dve.wait_ge(y_summed, upto(g, n))
                    count = 3 * GROUP * g + which * GROUP + n + 1
                    nc.vector.bn_stats(stats[:], dst).then_inc(stats_ready, 1)
                    hold(dve, stats_ready, count)
                    nc.vector.bn_aggr(mv[:, n, :], stats[:]).then_inc(mean_ready, 1)
                    dve.wait_ge(mean_ready, count)
                    nc.vector.tensor_scalar(ve[:, n:n + 1], mv[:, n, 1:2], EPS, None, ALU.add).then_inc(var_ready, 1)

                def weigh_centred(g, which, n):
                    nc.vector.scalar_tensor_tensor(out=h[:, n, :], in0=h[:, n, :], scalar=mv[:, n, 0:1],
                                                   in1=weights.rows[:, 1 + 3 * which, :], op0=ALU.subtract,
                                                   op1=ALU.mult).then_inc(normed, 1)

                def scale_and_shift(g, which, n, dst, ready):
                    dve.wait_ge(normed, 2 * GROUP * g + which * GROUP + n + 1)
                    dve.wait_ge(rstd_ready, 3 * GROUP * g + which * GROUP + n + 1)
                    nc.vector.scalar_tensor_tensor(out=dst[:, n, :], in0=h[:, n, :], scalar=rs[:, n:n + 1],
                                                   in1=weights.rows[:, 2 + 3 * which, :], op0=ALU.mult,
                                                   op1=ALU.add).then_inc(ready, 1)

                def normalise(g, n, dst, src):
                    dve.wait_ge(rstd_ready, 3 * GROUP * g + 2 * GROUP + n + 1)
                    nc.vector.tensor_scalar(dst, src, mv[:, n, 0:1], rs[:, n:n + 1], ALU.subtract, ALU.mult).then_inc(xm_ready, 1)

                def combine(g, q):
                    half, m = q // KC, q % KC
                    cols = slice(half * HALF, (half + 1) * HALF)
                    done = GQ * g + q + 1
                    dve.wait_ge(new_ready, done)
                    nc.vector.tensor_tensor(rT[:, m, cols], hT[:, m, cols], nT[:, m, cols], ALU.subtract).then_inc(h_less_n, 1)
                    dve.wait_ge(h_less_n, done)
                    nc.vector.tensor_tensor(rT[:, m, cols], rT[:, m, cols], zT[:, m, cols], ALU.mult).then_inc(z_applied, 1)
                    dve.wait_ge(z_applied, done)
                    nc.vector.tensor_tensor(nT[:, m, cols], rT[:, m, cols], nT[:, m, cols], ALU.add).then_inc(o_ready, 1)

                def last_norm(g, first, end):
                    for n in range(first, end + 1):
                        if n < end:
                            dve.wait_ge(tp_out, TP * g + turned("gru", n))
                            sum_and_stats(g, 2, n, bk[:, n, :], bk[:, n, :], xt[:, n, :])
                        if n > first:
                            dve.wait_ge(stored[0], 16 * g)
                            normalise(g, n - 1, xm[:, n - 1, :], bk[:, n - 1, :])

                def group(g):
                    first_time(dve, g, weights.first_in, weights.FIRST)
                    dve.wait_ge(x1_in, 16 * g + 16)
                    dve.wait_ge(agg_in, 16 * g + 16)
                    for n in range(GROUP):
                        dve.wait_ge(tp_full, TP * g)
                        nc.vector.tensor_tensor(at[:, n, :], x1t[:, n, :], agt[:, n, :], ALU.mult).then_inc(attn_ready, 1)
                    for n in range(GROUP + 1):
                        if n < GROUP:
                            dve.wait_ge(mo_full, MO * g + n + 1)
                            dve.wait_ge(xb_ready, upto(g, n))
                            sum_and_stats(g, 0, n, h[:, n, :], mo[:, n % 2, 0:D], xb[:, n, :])
                            weigh_centred(g, 0, n)
                        if n >= 1:
                            scale_and_shift(g, 0, n - 1, h1, h1_ready)
                    for n in range(GROUP):
                        dve.wait_ge(h1_ready, upto(g, n))
                        nc.vector.tensor_tensor(hb[:, n, :], h1[:, n, :], weights.rows[:, 3, :], ALU.add).then_inc(hb_ready, 1)
                    if isinstance(g, int):
                        weights.fold(nc, dve)
                    for n in range(GROUP + 1):
                        if n < GROUP:
                            dve.wait_ge(mo_full, MO * g + GROUP + n + 1)
                            dve.wait_ge(hb_ready, upto(g, n))
                            sum_and_stats(g, 1, n, h[:, n, :], mo[:, (GROUP + n) % 2, 0:D], hb[:, n, :])
                            weigh_centred(g, 1, n)
                        if n >= 1:
                            scale_and_shift(g, 1, n - 1, h, h2_ready)
                    for q in range(GQ):
                        half, m = q // KC, q % KC
                        cols = slice(half * HALF, (half + 1) * HALF)
                        if q >= 1:
                            combine(g, q - 1)
                        if q == GQ - 1:
                            last_norm(g, 0, 3)
                        dve.wait_ge(hf_full, HF * g + 2 * FC + 4 * q + 4)
                        dve.wait_ge(gates, GAT * g + 2 * q + 1)
                        dve.wait_ge(tp_full, TP * g)
                        nc.vector.scalar_tensor_tensor(out=nT[:, m, cols], in0=hf[:, 3, 0:HALF], scalar=weights.bhh[:, 4 + m:5 + m],
                                                       in1=rT[:, m, cols], op0=ALU.add, op1=ALU.mult).then_inc(reset_applied, 1)
                        dve.wait_ge(reset_applied, GQ * g + q + 1)
                        nc.vector.tensor_tensor(nT[:, m, cols], nT[:, m, cols], hf[:, 2, 0:HALF], ALU.add).then_inc(new_pre, 1)
                    combine(g, GQ - 1)
                    last_norm(g, 3, GROUP)

                group_steps(dve, group)


class EdgeWalk:

    def __init__(self, kit, tmp, nc, name, weighted, bank):
        def sb(what, shape, dt=F32):
            return tmp.enter_context(nc.sbuf_tensor(f"{name}_{what}", shape, dt))

        self.weighted, self.cols = weighted, HT if weighted else D
        self.seg, self.gat = sb("seg", [P, 1], I32), sb("gat", [P, 1], I32)
        self.seg_row = sb("seg_row", [P, P], I32)
        self.seg_f = sb("seg_f", [P, 1])
        self.rows, self.old, self.recv = sb("rows", [P, self.cols]), sb("old", [P, self.cols]), sb("recv", [P, HT])
        self.w = sb("w", [P, 4])
        self.same, self.earlier = sb("same", [P, P]), sb("earlier", [P, P])
        self.below, self.trash = sb("below", [P, P]), sb("trash", [P, 1])
        self.rank, self.first = sb("rank", [P, 1]), sb("first", [P, 1])
        self.to_f, self.to = sb("to_f", [P, 1]), sb("to", [P, 1], I32)
        self.sums = bank
        self.s_zeroed = kit.sem(name + "_zeroed")
        self.s_cleared = kit.sem(name + "_cleared")
        self.s_consts = kit.sem(name + "_consts")
        self.s_below_set = kit.sem(name + "_below_set")
        self.s_idx_in = kit.sem(name + "_idx_in")
        self.s_rows_in = kit.pool_dma_sem(name + "_rows_in")
        self.s_recv_in = kit.pool_dma_sem(name + "_recv_in")
        self.s_old_in = kit.pool_dma_sem(name + "_old_in")
        self.s_converted = kit.sem(name + "_converted")
        self.s_same_ready = kit.sem(name + "_same_ready")
        self.s_masked = kit.sem(name + "_masked")
        self.s_ranked = kit.sem(name + "_ranked")
        self.s_first_ready = kit.sem(name + "_first_ready")
        self.s_moved = kit.sem(name + "_moved")
        self.s_blended = kit.sem(name + "_blended")
        self.s_to_ready = kit.sem(name + "_to_ready")
        self.s_summed = kit.sem(name + "_summed")
        self.s_weighted = kit.sem(name + "_weighted")
        self.s_w_added = kit.sem(name + "_w_added")
        self.s_w_scaled = kit.sem(name + "_w_scaled")
        self.s_w_leaky = kit.sem(name + "_w_leaky")
        self.s_w_ready = kit.sem(name + "_w_ready")
        self.s_w_applied = kit.sem(name + "_w_applied")
        self.s_added = kit.sem(name + "_added")
        self.s_stored = kit.pool_dma_sem(name + "_stored")


def edge_walk_sync(nc, sp, k, seg, gat, out):
    sp.wait_ge(k.s_zeroed, 1)
    n = (ROWS + P) // P
    with sp.Fori(0, n) as t:
        sp.dma_start(out[bass.ds(t * P, P), :], k.old[:]).then_inc(k.s_cleared, 16)
    sp.wait_ge(k.s_cleared, 16 * n)
    with sp.Fori(0, EDGE_TILES) as t:
        sp.wait_ge(k.s_stored, t * 16)
        with nc.allow_non_contiguous_dma("one index per partition"):
            sp.dma_start(k.seg[:], seg[bass.ds(t * P, P)].unsqueeze(1)).then_inc(k.s_idx_in, 16)
            sp.dma_start(k.gat[:], gat[bass.ds(t * P, P)].unsqueeze(1)).then_inc(k.s_idx_in, 16)
        sp.dma_start(k.seg_row[:], seg[bass.ds(t * P, P)].partition_broadcast(P)).then_inc(k.s_idx_in, 16)


def edge_walk_pool(nc, pool, k, table, out):
    nc.gpsimd.memset(k.old[:], 0.0).then_inc(k.s_zeroed, 1)
    nc.gpsimd.iota(k.trash[:], [[0, 1]], base=TRASH, channel_multiplier=1,
                   allow_small_or_imprecise_dtypes=True).then_inc(k.s_consts, 1)
    nc.gpsimd.memset(k.below[:], 1.0).then_inc(k.s_below_set, 1)
    pool.wait_ge(k.s_below_set, 1)
    nc.gpsimd.affine_select(out=k.below[:], in_=k.below[:], compare_op=ALU.is_gt, fill=0.0, base=0,
                            pattern=[[-1, P]], channel_multiplier=1).then_inc(k.s_consts, 1)
    pool.wait_ge(k.s_cleared, 16 * ((ROWS + P) // P))
    with pool.Fori(0, EDGE_TILES) as t:
        hold(pool, k.s_idx_in, t * 48 + 48)
        nc.gpsimd.indirect_dma_start(k.rows[:], None, table, bass.IndirectOffsetOnAxis(ap=k.gat[:, 0:1], axis=0)) \
            .then_inc(k.s_rows_in, 16)
        if k.weighted:
            nc.gpsimd.indirect_dma_start(k.recv[:], None, table, bass.IndirectOffsetOnAxis(ap=k.seg[:, 0:1], axis=0)) \
                .then_inc(k.s_recv_in, 16)
        hold(pool, k.s_to_ready, t + 1)
        nc.gpsimd.indirect_dma_start(k.old[:], None, out, bass.IndirectOffsetOnAxis(ap=k.to[:, 0:1], axis=0)) \
            .then_inc(k.s_old_in, 16)
        hold(pool, k.s_added, t + 1)
        nc.gpsimd.indirect_dma_start(out, bass.IndirectOffsetOnAxis(ap=k.to[:, 0:1], axis=0), k.old[:], None) \
            .then_inc(k.s_stored, 16)
        hold(pool, k.s_stored, t * 16 + 16)


def edge_walk_vector(nc, dve, k):
    dve.wait_ge(k.s_consts, 2)
    with dve.Fori(0, EDGE_TILES) as t:
        dve.wait_ge(k.s_idx_in, t * 48 + 48)
        nc.vector.tensor_copy(k.seg_f[:], k.seg[:]).then_inc(k.s_converted, 1)
        dve.wait_ge(k.s_converted, t + 1)
        nc.vector.tensor_scalar(k.same[:], k.seg_row[:], k.seg_f[:, 0:1], None, ALU.is_equal).then_inc(k.s_same_ready, 1)
        dve.wait_ge(k.s_same_ready, t + 1)
        nc.vector.tensor_tensor(k.earlier[:], k.same[:], k.below[:], ALU.mult).then_inc(k.s_masked, 1)
        dve.wait_ge(k.s_masked, t + 1)
        nc.vector.tensor_reduce(k.rank[:], k.earlier[:], AX.X, ALU.add).then_inc(k.s_ranked, 1)
        dve.wait_ge(k.s_ranked, t + 1)
        nc.vector.tensor_scalar(k.first[:], k.rank[:], 0.0, None, ALU.is_equal).then_inc(k.s_first_ready, 1)
        nc.vector.tensor_tensor(k.to_f[:], k.seg_f[:], k.trash[:], ALU.subtract).then_inc(k.s_moved, 1)
        dve.wait_ge(k.s_first_ready, t + 1)
        dve.wait_ge(k.s_moved, t + 1)
        nc.vector.scalar_tensor_tensor(out=k.to_f[:], in0=k.to_f[:], scalar=k.first[:, 0:1], in1=k.trash[:],
                                       op0=ALU.mult, op1=ALU.add).then_inc(k.s_blended, 1)
        dve.wait_ge(k.s_blended, t + 1)
        nc.vector.tensor_copy(k.to[:], k.to_f[:]).then_inc(k.s_to_ready, 1)
        if k.weighted:
            dve.wait_ge(k.s_rows_in, t * 16 + 16)
            dve.wait_ge(k.s_recv_in, t * 16 + 16)
            nc.vector.tensor_tensor(k.w[:, 0:1], k.recv[:, D:D + 1], k.rows[:, D + 1:D + 2], ALU.add).then_inc(k.s_w_added, 1)
            dve.wait_ge(k.s_w_added, t + 1)
            nc.vector.tensor_scalar(k.w[:, 1:2], k.w[:, 0:1], ALPHA, None, ALU.mult).then_inc(k.s_w_scaled, 1)
            dve.wait_ge(k.s_w_scaled, t + 1)
            nc.vector.tensor_tensor(k.w[:, 2:3], k.w[:, 0:1], k.w[:, 1:2], ALU.max).then_inc(k.s_w_leaky, 1)
            dve.wait_ge(k.s_w_ready, t + 1)
            nc.vector.tensor_scalar(k.rows[:], k.rows[:], k.w[:, 3:4], None, ALU.mult).then_inc(k.s_w_applied, 1)
            dve.wait_ge(k.s_w_applied, t + 1)
            nc.vector.tensor_copy(k.rows[:, D:D + 1], k.w[:, 3:4]).then_inc(k.s_weighted, 1)
        dve.wait_ge(k.s_old_in, t * 16 + 16)
        dve.wait_ge(k.s_summed, t + 1)
        nc.vector.tensor_tensor(k.old[:], k.old[:], k.sums[:, 0:k.cols], ALU.add).then_inc(k.s_added, 1)


def edge_walk_scalar(nc, act, k):
    if k.weighted:
        with act.Fori(0, EDGE_TILES) as t:
            act.wait_ge(k.s_w_leaky, t + 1)
            nc.scalar.activation(k.w[:, 3:4], k.w[:, 2:3], ACT.Exp, scale=-1.0).then_inc(k.s_w_ready, 1)


def edge_walk_tensor(nc, pe, k):
    with pe.Fori(0, EDGE_TILES) as t:
        pe.wait_ge(k.s_same_ready, t + 1)
        if k.weighted:
            pe.wait_ge(k.s_weighted, t + 1)
        else:
            pe.wait_ge(k.s_rows_in, t * 16 + 16)
        nc.tensor.matmul(k.sums[:, 0:k.cols], k.same[:], k.rows[:], start=True, stop=True).then_inc(k.s_summed, 1)


def final_rows(nc, kit, c, xmid, sums, out):
    with ExitStack() as tmp:
        def sb(name, shape, dt=F32):
            return tmp.enter_context(nc.sbuf_tensor(name, shape, dt))

        xm, sm, y = sb("f_xmid", [P, GROUP, D]), sb("f_sums", [P, GROUP, D + 1]), sb("f_y", [P, GROUP, D])
        rd, rs = sb("f_rweights", [P, GROUP]), sb("f_rstd", [P, GROUP])
        stats, mv, ve = sb("f_stats", [P, nc.vector.BN_STATS_DIM]), sb("f_mv", [P, GROUP, 2]), sb("f_var_eps", [P, GROUP])
        xm_in = [kit.sem(f"f_xmid_loaded{n}") for n in range(GROUP)]
        sm_in = [kit.sem(f"f_sums_loaded{n}") for n in range(GROUP)]
        stored = [kit.sem(f"out_stored{n}") for n in range(GROUP)]
        clamped, inverted, divided, summed, stats_ready, mean_ready, var_ready, rstd_ready, ready = (
            kit.sem("f_" + s) for s in ("clamped", "inverted", "divided", "summed", "stats", "mean", "var", "rstd", "ready"))
        with nc.Block() as block:

            @block.sync
            def _(sp):
                flag = sp.value_load(c["flag"][0:1, 0:1], min_val=0, max_val=1)
                with sp.If(flag == 1):
                    with sp.Fori(0, GROUPS) as g:
                        for n in range(GROUP):
                            sp.wait_ge(ready, before(g, n, GROUP))
                            sp.dma_start(xm[:, n, :], xmid[tile_rows(g, n), :]).then_inc(xm_in[n], 16)
                            sp.dma_start(sm[:, n, :], sums[tile_rows(g, n), 0:D + 1]).then_inc(sm_in[n], 16)

            @block.scalar
            def _(act):
                flag = act.value_load(c["flag"][0:1, 0:1], min_val=0, max_val=1)
                with act.If(flag == 1):
                    with act.Fori(0, GROUPS) as g:
                        for n in range(GROUP):
                            act.wait_ge(ready, upto(g, n))
                            act.dma_start(out[tile_rows(g, n), :], y[:, n, :]).then_inc(stored[n], 16)
                    for n in range(GROUP):
                        act.wait_ge(stored[n], 16 * GROUPS)

            @block.gpsimd
            def _(pool):
                flag = pool.value_load(c["flag"][0:1, 0:1], min_val=0, max_val=1)
                with pool.If(flag == 1):
                    with pool.Fori(0, GROUPS) as g:
                        for n in range(GROUP):
                            pool.wait_ge(var_ready, upto(g, n))
                            nc.gpsimd.tensor_tensor(rs[:, n:n + 1], ve[:, n:n + 1], c["half"][:], ALU.pow).then_inc(rstd_ready, 1)

            @block.vector
            def _(dve):
                flag = dve.value_load(c["flag"][0:1, 0:1], min_val=0, max_val=1)
                with dve.If(flag == 1):
                    def normalise(g, n):
                        dve.wait_ge(rstd_ready, upto(g, n))
                        nc.vector.tensor_scalar(y[:, n, :], y[:, n, :], mv[:, n, 0:1], rs[:, n:n + 1], ALU.subtract,
                                                ALU.mult).then_inc(ready, 1)

                    with dve.Fori(0, GROUPS) as g:
                        for n in range(GROUP):
                            done = upto(g, n)
                            dve.wait_ge(sm_in[n], 16 * g + 16)
                            nc.vector.tensor_scalar(rd[:, n:n + 1], sm[:, n, D:D + 1], TINY, None, ALU.max).then_inc(clamped, 1)
                            dve.wait_ge(clamped, done)
                            nc.vector.reciprocal(rd[:, n:n + 1], rd[:, n:n + 1]).then_inc(inverted, 1)
                            dve.wait_ge(inverted, done)
                            dve.wait_ge(stored[n], 16 * g)
                            nc.vector.tensor_scalar(y[:, n, :], sm[:, n, 0:D], rd[:, n:n + 1], 0.0, ALU.mult,
                                                    ALU.max).then_inc(divided, 1)
                            dve.wait_ge(divided, done)
                            dve.wait_ge(xm_in[n], 16 * g + 16)
                            nc.vector.tensor_tensor(y[:, n, :], y[:, n, :], xm[:, n, :], ALU.add).then_inc(summed, 1)
                            dve.wait_ge(summed, done)
                            nc.vector.bn_stats(stats[:], y[:, n, :]).then_inc(stats_ready, 1)
                            hold(dve, stats_ready, done)
                            nc.vector.bn_aggr(mv[:, n, :], stats[:]).then_inc(mean_ready, 1)
                            dve.wait_ge(mean_ready, done)
                            nc.vector.tensor_scalar(ve[:, n:n + 1], mv[:, n, 1:2], EPS, None, ALU.add).then_inc(var_ready, 1)
                            if n >= 1:
                                normalise(g, n - 1)
                        normalise(g, GROUP - 1)


WINDOW = 8
WINDOWS = ROWS // WINDOW
WPT = P // WINDOW
RPW = SLOTS * P // EROW
WCHUNK = WINDOWS // GROUP
KEYS = TILES * WINDOW
EPP = EDGES // P
LINES = EPP // EROW
NO_KEY = -1.0

assert EPP % EROW == 0 and WCHUNK <= P and KEYS <= 512


def prepare_edges(nc, kit, c, dst, pairs):
    c["lo"], c["key"] = kit.sb("edge_lo", [P, SLOTS, WINDOWS], F16), kit.sb("edge_key", [P, SLOTS, WINDOWS], F16)
    with ExitStack() as tmp:
        def sb(name, shape, dt=F32):
            return tmp.enter_context(nc.sbuf_tensor(name, shape, dt))

        cols = GROUP * SLOTS * P
        d0, d1 = sb("e_dst", [P, EPP], I32), sb("e_dst_next", [P, EPP], I32)
        firsts = sb("e_firsts", [P, LINES])
        falls, fall = sb("e_falls", [P, EPP]), sb("e_fall", [P, 1])
        bounds, less = sb("e_bounds", [P, WINDOWS + 1], F16), sb("e_less", [P, 2, WINDOWS + 1], BF16)
        ones, onesb = sb("e_ones", [P, 1]), sb("e_ones_bf", [P, 1], BF16)
        cnt, row0, span = sb("e_count", [1, WINDOWS + 1]), sb("e_row0", [1, WINDOWS]), sb("e_span", [1, WINDOWS])
        bad = sb("e_bad", [1, 4])
        steps, idx_f, idx = sb("e_steps", [P, RPW]), sb("e_idx_f", [P, GROUP, RPW]), sb("e_idx", [P, GROUP, RPW], I32)
        r0 = sb("e_r0", [P, GROUP])
        first_node = sb("e_first_node", [P, GROUP])
        ends = sb("e_ends", [P, GROUP, RPW, 2 * EROW], I32)
        lo_i, hi_i = sb("e_lo_i", [P, cols], I32), sb("e_hi_i", [P, cols], I32)
        lo_f, hi_f = sb("e_lo_f", [P, cols]), sb("e_hi_f", [P, cols])
        rel, inside, below = sb("e_rel", [P, cols]), sb("e_inside", [P, cols]), sb("e_below", [P, cols])
        pc = tmp.enter_context(nc.psum_tensor("e_counts", [P, 2, 512], F32))
        pr = tmp.enter_context(nc.psum_tensor("e_small", [P, 512], F32))
        pf = tmp.enter_context(nc.psum_tensor("e_falls_sum", [P, 512], F32))
        pt = tmp.enter_context(nc.psum_tensor("e_turned", [P, 2, 512], F32))

        loaded, consts = kit.sem("e_loaded"), kit.sem("e_consts")
        firsts_ready, compared, counted = kit.sem("e_firsts_ready"), kit.sem("e_compared"), kit.sem("e_counted")
        step, fall_ready, row0_ready = kit.sem("e_step"), kit.sem("e_fall_ready"), kit.sem("e_row0_ready")
        small, idx_ready = kit.sem("e_small_ready"), kit.sem("e_idx_ready")
        fetched = [kit.pool_dma_sem(f"e_fetched{t}") for t in range(GROUP)]
        keys_ready, turned, kept = kit.sem("e_keys_ready"), kit.sem("e_turned_ready"), kit.sem("e_kept")
        half = (WINDOWS + 1) // 2 + 1
        parts = [(0, half), (half, WINDOWS + 1)]
        with nc.Block() as block:

            @block.sync
            def _(sp):
                sp.dma_start(d0[:], dst[0:EDGES].rearrange("(p e) -> p e", p=P)).then_inc(loaded, 16)
                sp.dma_start(d1[:], dst[1:EDGES + 1].rearrange("(p e) -> p e", p=P)).then_inc(loaded, 16)

            @block.gpsimd
            def _(pool):
                nc.gpsimd.iota(bounds[:], [[WINDOW, WINDOWS + 1]], base=0, channel_multiplier=0,
                               allow_small_or_imprecise_dtypes=True).then_inc(consts, 1)
                nc.gpsimd.iota(steps[:], [[1, RPW]], base=0, channel_multiplier=0,
                               allow_small_or_imprecise_dtypes=True).then_inc(consts, 1)
                nc.gpsimd.iota(first_node[:], [[WINDOW * WCHUNK, GROUP]], base=0, channel_multiplier=WINDOW,
                               allow_small_or_imprecise_dtypes=True).then_inc(consts, 1)
                nc.gpsimd.memset(ones[:], 1.0).then_inc(consts, 1)
                nc.gpsimd.memset(onesb[:], 1.0).then_inc(consts, 1)
                pool.wait_ge(idx_ready, 1)
                for t in range(GROUP):
                    for r in range(RPW):
                        nc.gpsimd.indirect_dma_start(ends[0:WCHUNK, t, r, :], None, pairs,
                                                     bass.IndirectOffsetOnAxis(ap=idx[0:WCHUNK, t, r:r + 1], axis=0)) \
                            .then_inc(fetched[t], 16)

            @block.vector
            def _(dve):
                n = 0

                def link(ins):
                    nonlocal n
                    n += 1
                    ins.then_inc(step, 1)
                    dve.wait_ge(step, n)

                dve.wait_ge(consts, 5)
                dve.wait_ge(loaded, 32)
                nc.vector.tensor_copy(firsts[:], d0[:].rearrange("p (l e) -> p l e", e=EROW)[:, :, 0]).then_inc(firsts_ready, 1)
                dve.wait_ge(firsts_ready, 1)
                for j in range(LINES):
                    if j >= 2:
                        dve.wait_ge(counted, j - 1)
                    nc.vector.tensor_scalar(less[:, j % 2, :], bounds[:], firsts[:, j:j + 1], None, ALU.is_gt).then_inc(compared, 1)
                dve.wait_ge(counted, LINES)
                for b, (a0, a1) in enumerate(parts):
                    link(nc.vector.tensor_copy(cnt[:, a0:a1], pc[0:1, b, 0:a1 - a0]))
                nc.vector.tensor_scalar(row0[:], cnt[:, 0:WINDOWS], 1.0, 0.0, ALU.subtract, ALU.max).then_inc(row0_ready, 1)
                dve.wait_ge(row0_ready, 1)
                dve.wait_ge(small, 1)
                link(nc.vector.tensor_copy(r0[0:WCHUNK, :], pr[0:WCHUNK, 8:8 + GROUP]))
                link(nc.vector.tensor_tensor(idx_f[0:WCHUNK], steps[0:WCHUNK, :].unsqueeze(1).broadcast_to([WCHUNK, GROUP, RPW]),
                                             r0[0:WCHUNK, :].unsqueeze(2).broadcast_to([WCHUNK, GROUP, RPW]), ALU.add))
                link(nc.vector.tensor_scalar(idx_f[0:WCHUNK], idx_f[0:WCHUNK], float(EDGES // EROW - 1), None, ALU.min))
                nc.vector.tensor_copy(idx[0:WCHUNK], idx_f[0:WCHUNK]).then_inc(idx_ready, 1)
                link(nc.vector.tensor_tensor(falls[:], d0[:], d1[:], ALU.is_gt))
                nc.vector.tensor_reduce(fall[:], falls[:], AX.X, ALU.add).then_inc(fall_ready, 1)
                link(nc.vector.tensor_tensor(span[:], cnt[:, 1:WINDOWS + 1], row0[:], ALU.subtract))
                dve.wait_ge(counted, LINES + 1)
                real = -(-N_NODES // WINDOW)
                link(nc.vector.tensor_scalar(span[:, 0:real], span[:, 0:real], float(RPW), None, ALU.is_gt))
                link(nc.vector.tensor_reduce(bad[:, 0:1], span[:, 0:real], AX.X, ALU.add))
                link(nc.vector.tensor_tensor(bad[:, 1:2], bad[:, 0:1], pf[0:1, 0:1], ALU.add))
                link(nc.vector.tensor_scalar(bad[:, 2:3], bad[:, 1:2], 1.0, None, ALU.min))
                nc.vector.tensor_copy(c["flag"][:], bad[:, 2:3])
                per, W = SLOTS * P, WCHUNK
                flat = ends[0:W].rearrange("p t r (e x) -> p (t r e) x", x=2)
                for t in range(GROUP):
                    dve.wait_ge(fetched[t], 16 * RPW)
                    e = slice(t * per, (t + 1) * per)
                    link(nc.vector.tensor_scalar(lo_i[0:W, e], flat[:, e, 0], P - 1, None, ALU.bitwise_and))
                    link(nc.vector.tensor_scalar(hi_i[0:W, e], flat[:, e, 0], 7, None, ALU.logical_shift_right))
                    link(nc.vector.tensor_copy(lo_f[0:W, e], lo_i[0:W, e]))
                    link(nc.vector.tensor_scalar(hi_f[0:W, e], hi_i[0:W, e], float(WINDOW), 1.0, ALU.mult, ALU.add))
                    link(nc.vector.tensor_scalar(rel[0:W, e], flat[:, e, 1], first_node[0:W, t:t + 1], None, ALU.subtract))
                    link(nc.vector.tensor_scalar(inside[0:W, e], rel[0:W, e], 0.0, None, ALU.is_ge))
                    link(nc.vector.tensor_scalar(below[0:W, e], rel[0:W, e], float(WINDOW), None, ALU.is_lt))
                    link(nc.vector.tensor_tensor(inside[0:W, e], inside[0:W, e], below[0:W, e], ALU.mult))
                    link(nc.vector.tensor_tensor(hi_f[0:W, e], hi_f[0:W, e], rel[0:W, e], ALU.add))
                    link(nc.vector.tensor_tensor(hi_f[0:W, e], hi_f[0:W, e], inside[0:W, e], ALU.mult))
                    nc.vector.tensor_scalar(hi_f[0:W, e], hi_f[0:W, e], NO_KEY, None, ALU.add).then_inc(keys_ready, 1)

            @block.tensor
            def _(pe):
                pe.wait_ge(consts, 5)
                for j in range(LINES):
                    pe.wait_ge(compared, j + 1)
                    for b, (a0, a1) in enumerate(parts):
                        last = nc.tensor.matmul(pc[0:1, b, 0:a1 - a0], onesb[:], less[:, j % 2, a0:a1], start=(j == 0),
                                                stop=(j == LINES - 1))
                    last.then_inc(counted, 1)
                pe.wait_ge(row0_ready, 1)
                for t in range(GROUP):
                    last = nc.tensor.matmul(pr[0:WCHUNK, 8 + t:9 + t], row0[:, t * WCHUNK:(t + 1) * WCHUNK], ones[0:1, 0:1],
                                            start=True, stop=True)
                last.then_inc(small, 1)
                pe.wait_ge(fall_ready, 1)
                nc.tensor.matmul(pf[0:1, 0:1], fall[:], ones[:], start=True, stop=True).then_inc(counted, 1)
                n = 0
                for t in range(GROUP):
                    pe.wait_ge(keys_ready, t + 1)
                    for src in (lo_f, hi_f):
                        if n >= 2:
                            pe.wait_ge(kept, n - 1)
                        for k in range(SLOTS):
                            a0 = (t * SLOTS + k) * P
                            last = nc.tensor.transpose(pt[:, n % 2, k * P:k * P + WCHUNK], src[0:WCHUNK, a0:a0 + P],
                                                       c["ident"][0:WCHUNK, 0:WCHUNK])
                        last.then_inc(turned, 1)
                        n += 1

            @block.scalar
            def _(act):
                n = 0
                for t in range(GROUP):
                    for dst_t in (c["lo"], c["key"]):
                        act.wait_ge(turned, n + 1)
                        nc.scalar.copy(dst_t[:, :, t * WCHUNK:(t + 1) * WCHUNK],
                                       pt[:, n % 2, 0:SLOTS * P].rearrange("p (k w) -> p k w", k=SLOTS)[:, :, 0:WCHUNK]) \
                            .then_inc(kept, 1)
                        n += 1


assert SLOTS * WPT < TILES
HOT_SLOTS = 4
TURNED = 512 // P
BANKS = -(-TILES // TURNED)


def count_and_sum(nc, kit, c, x1_parts, dst, src, x1, agg, counts):
    with ExitStack() as tmp:
        def sb(name, shape, dt=F32):
            return tmp.enter_context(nc.sbuf_tensor(name, shape, dt))

        n128, n392 = sb("b_nodes", [P, P], BF16), sb("b_keys", [P, KEYS], F16)
        identr = sb("b_ident", [P, P], F32R)
        ends = sb("b_ends", [P, 2, 2, SLOTS, WPT])
        lo1, key1 = sb("b_lo_hot", [P, HOT_SLOTS, SLOTS, P], BF16), sb("b_key_hot", [P, HOT_SLOTS, SLOTS, KEYS], BF16)
        ca = sb("b_counts", [P, 2, TILES, P], F32R)
        cb = sb("b_counts_turned", [P, 2, TILES * P], F16)
        sums = sb("b_sums", [P, 2, D])
        pcnt = tmp.enter_context(nc.psum_tensor("b_pcounts", [P, 4, 512], F32))
        pturn = tmp.enter_context(nc.psum_tensor("b_pturned", [P, 2, 512], F32))
        pagg = tmp.enter_context(nc.psum_tensor("b_pagg", [P, 2, 512], F32))
        walk = EdgeWalk(kit, tmp, nc, "l0", False, pagg[:, 0, :])
        consts, ident_ready = kit.sem("b_consts"), kit.sem("b_ident_ready")
        ends_ready, hot, built, kept = kit.sem("b_ends_ready"), kit.sem("b_hot"), kit.sem("b_built"), kit.sem("b_kept")
        turned, cb_ready, summed = kit.sem("b_turned"), kit.sem("b_turned_kept"), kit.sem("b_summed")
        sums_ready = [kit.sem(f"b_sums_ready{k}") for k in range(2)]
        cb_stored = [kit.sem(f"b_counts_stored{k}") for k in range(2)]
        sums_stored = [kit.sem(f"b_sums_stored{k}") for k in range(2)]

        def steps(eng, step):
            step(0, 0, 0, True, False)
            with eng.Fori(0, (TILES - 1) // 4) as i:
                for k in range(4):
                    step(4 * i + 1 + k, (1 + k) % 2, 2 * i + k // 2, True, True)
            step(TILES, TILES % 2, (TILES - 1) // 2, False, True)

        with nc.Block() as block:

            @block.sync
            def _(sp):
                flag = sp.value_load(c["flag"][0:1, 0:1], min_val=0, max_val=1)
                with sp.If(flag == 0):
                    def step(s, k, i, build, use):
                        if use:
                            o = 1 - k
                            rows = bass.ds((s - 1) * P, P)
                            sp.wait_ge(cb_ready, BANKS * s)
                            sp.dma_start(counts[rows, :], cb[:, o, :]).then_inc(cb_stored[o], 16)
                            sp.wait_ge(sums_ready[o], i + 1)
                            sp.dma_start(agg[rows, :], sums[:, o, :]).then_inc(sums_stored[o], 16)

                    steps(sp, step)
                    for o in range(2):
                        sp.wait_ge(cb_stored[o], 16 * ((TILES + 1 - o) // 2))
                        sp.wait_ge(sums_stored[o], 16 * ((TILES + 1 - o) // 2))
                with sp.Else():
                    edge_walk_sync(nc, sp, walk, dst, src, agg)

            @block.gpsimd
            def _(pool):
                flag = pool.value_load(c["flag"][0:1, 0:1], min_val=0, max_val=1)
                with pool.If(flag == 0):
                    nc.gpsimd.iota(n128[:], [[1, P]], base=0, channel_multiplier=0,
                                   allow_small_or_imprecise_dtypes=True).then_inc(consts, 1)
                    nc.gpsimd.iota(n392[:], [[1, KEYS]], base=0, channel_multiplier=0,
                                   allow_small_or_imprecise_dtypes=True).then_inc(consts, 1)

                    def step(s, k, i, build, use):
                        if build:
                            if use:
                                pool.wait_ge(hot, WPT * (s - 1))
                            for j, what in enumerate((c["lo"], c["key"])):
                                last = nc.gpsimd.tensor_copy(ends[:, k, j], what[:, :, bass.ds(WPT * s, WPT)])
                            last.then_inc(ends_ready, 1)

                    steps(pool, step)
                with pool.Else():
                    edge_walk_pool(nc, pool, walk, x1, agg)

            @block.vector
            def _(dve):
                flag = dve.value_load(c["flag"][0:1, 0:1], min_val=0, max_val=1)
                with dve.If(flag == 0):
                    nc.vector.tensor_copy(identr[:], c["ident"][:]).then_inc(ident_ready, 1)
                    dve.wait_ge(consts, 2)

                    def step(s, k, i, build, use):
                        if not build:
                            return
                        dve.wait_ge(ends_ready, s + 1)
                        for j in range(WPT):
                            h = j % HOT_SLOTS
                            if use or j >= HOT_SLOTS:
                                dve.wait_ge(built, WPT * s + j + 1 - HOT_SLOTS)
                            for q in range(SLOTS):
                                nc.vector.tensor_scalar(lo1[:, h, q, :], n128[:], ends[:, k, 0, q, j:j + 1], None, ALU.is_equal)
                                last = nc.vector.tensor_scalar(key1[:, h, q, :], n392[:], ends[:, k, 1, q, j:j + 1], None,
                                                               ALU.is_equal)
                            last.then_inc(hot, 1)

                    steps(dve, step)
                with dve.Else():
                    edge_walk_vector(nc, dve, walk)

            @block.tensor
            def _(pe):
                flag = pe.value_load(c["flag"][0:1, 0:1], min_val=0, max_val=1)
                with pe.If(flag == 0):
                    pe.wait_ge(ident_ready, 1)

                    def step(s, k, i, build, use):
                        o = 1 - k

                        def use_source_tile(hi):
                            bank, at = hi // TURNED, hi % TURNED
                            if hi == 0:
                                pe.wait_ge(kept, WPT * s)
                                pe.wait_ge(sums_ready[o], i)
                            for m in range(2):
                                last = nc.tensor.matmul(pagg[:, o, 0:D], ca[:, o, hi, :], x1_parts[:, m, hi, :],
                                                        start=(hi == 0 and m == 0), stop=(hi == TILES - 1 and m == 1))
                            if hi == TILES - 1:
                                last.then_inc(summed, 1)
                            if at == 0:
                                pe.wait_ge(cb_ready, BANKS * (s - 1) + max(bank - 1, 0))
                            last = nc.tensor.matmul(pturn[:, bank % 2, at * P:(at + 1) * P], ca[:, o, hi, :], identr[:],
                                                    start=True, stop=True)
                            if at == TURNED - 1 or hi == TILES - 1:
                                last.then_inc(turned, 1)

                        for n in range(TILES):
                            j, q = n // SLOTS, n % SLOTS
                            if build and j < WPT:
                                if q == 0 and j % 2 == 0:
                                    pe.wait_ge(hot, WPT * s + j + 2)
                                    if use or j >= 4:
                                        pe.wait_ge(kept, WPT * s + j - 2)
                                h = j % HOT_SLOTS
                                ins = nc.tensor.matmul(pcnt[:, j % 4, 0:KEYS], lo1[:, h, q, :], key1[:, h, q, :],
                                                       start=(q == 0), stop=(q == SLOTS - 1))
                                if q == SLOTS - 1:
                                    ins.then_inc(built, 1)
                            if use:
                                use_source_tile(n)

                    steps(pe, step)
                with pe.Else():
                    edge_walk_tensor(nc, pe, walk)

            @block.scalar
            def _(act):
                flag = act.value_load(c["flag"][0:1, 0:1], min_val=0, max_val=1)
                with act.If(flag == 0):
                    def step(s, k, i, build, use):
                        o = 1 - k
                        for n in range(TILES):
                            j, q = n // SLOTS, n % SLOTS
                            if build and j < WPT and q == SLOTS - 1:
                                act.wait_ge(built, WPT * s + j + 1)
                                if j == 0 and use:
                                    act.wait_ge(summed, s - 1)
                                    act.wait_ge(turned, BANKS * (s - 1))
                                nc.scalar.copy(ca[:, k, :, j * WINDOW:(j + 1) * WINDOW],
                                               pcnt[:, j % 4, 0:KEYS].rearrange("p (t w) -> p t w", w=WINDOW)).then_inc(kept, 1)
                            if use and (n % TURNED == TURNED - 1 or n == TILES - 1):
                                bank = n // TURNED
                                act.wait_ge(turned, BANKS * (s - 1) + bank + 1)
                                if bank == 0:
                                    act.wait_ge(cb_stored[o], 16 * i)
                                at, m = bank * TURNED * P, min(TURNED, TILES - bank * TURNED) * P
                                nc.scalar.copy(cb[:, o, at:at + m], pturn[:, bank % 2, 0:m]).then_inc(cb_ready, 1)
                        if use:
                            act.wait_ge(summed, s)
                            act.wait_ge(sums_stored[o], 16 * i)
                            nc.scalar.copy(sums[:, o, :], pagg[:, o, 0:D]).then_inc(sums_ready[o], 1)

                    steps(act, step)
                with act.Else():
                    edge_walk_scalar(nc, act, walk)


def weigh_and_sum(nc, kit, c, src, dst, table, counts, sums, xmid, out):
    cols = GROUP * P
    slots = 4
    with ExitStack() as tmp:
        def sb(name, shape, dt=F32):
            return tmp.enter_context(nc.sbuf_tensor(name, shape, dt))

        high, low = sb("d_rows_high", [P, TILES, HT], F32R), sb("d_rows_low", [P, TILES, HT], F32R)
        s_all, scale_col = sb("d_s", [P, TILES * P]), sb("d_scale", [P, TILES])
        diag, ones = sb("d_diag", [P, 2, 512]), sb("d_ones", [P, P])
        cnt = sb("d_counts", [P, GROUP, cols], F16)
        wgt, wh, wl = sb("d_weights", [P, slots, cols]), sb("d_weights_high", [P, slots, cols], F32R), \
            sb("d_weights_low", [P, slots, cols], F32R)
        y, xm = sb("d_y", [P, GROUP, HT]), sb("d_xmid", [P, GROUP, HT])
        staged = (y, xm)
        rd, rs = sb("d_rweights", [P, GROUP]), sb("d_rstd", [P, GROUP])
        stats, mv, ve = sb("d_stats", [P, nc.vector.BN_STATS_DIM]), sb("d_mv", [P, GROUP, 2]), sb("d_var_eps", [P, GROUP])
        acc = tmp.enter_context(nc.psum_tensor("d_acc", [P, GROUP + 1, 512], F32))
        walk = EdgeWalk(kit, tmp, nc, "l1", True, acc[:, 0, :])
        shifted, exped, weighted = kit.sem("d_shifted"), kit.sem("d_exped"), kit.sem("d_weighted")
        rounded, split, used = kit.sem("d_rounded"), kit.sem("d_split"), kit.sem("d_used")
        kept = [kit.sem(f"d_kept{r}") for r in range(GROUP)]
        cnt_in = [kit.sem(f"d_counts_loaded{n}") for n in range(GROUP)]
        clamped, inverted, xm_in, stored = (kit.sem("d_" + s) for s in ("clamped", "inverted", "xmid_loaded", "out_stored"))
        added, stats_ready, mean_ready, var_ready, rstd_ready, ready = (
            kit.sem("d_" + s) for s in ("added", "stats", "mean", "var", "rstd", "ready"))
        ones_ready, diag_ready, spread, s_ready, exp_t = (
            kit.sem("d_" + s) for s in ("ones_ready", "diag_ready", "s_spread", "s_ready", "exp_t"))
        one_set, scaled, high_ready, low_ready = (kit.sem("d_" + s) for s in ("one_set", "rows_scaled", "rows_high", "rows_low"))
        tab_in = [kit.sem(f"d_table_loaded{k}") for k in range(2)]
        per = 512 // P
        spreads = -(-TILES // per)
        ROWS_AHEAD = 4
        FINISH = 3

        def groups(eng, body):
            body(0, False)
            with eng.Fori(0, (GROUPS - 1) // 2) as i:
                for k in range(2):
                    body(2 * i + 1 + k, True)

        def free_block(eng, sem, J, t):
            back = {0: 3, 1: 3, 2: 3, 3: GROUP}.get(t % GROUP, slots)
            if not isinstance(J, int) or J * TILES + t >= back:
                eng.wait_ge(sem, J * TILES + t + 1 - back)

        def slot(t):
            return t % GROUP % slots

        def spread_cols(q):
            return slice(q * per * P, min((q + 1) * per, TILES) * P)

        def late_spreads(t):
            return range(min(GROUP + 2 * t, spreads), min(GROUP + 2 * t + 2, spreads))

        with nc.Block() as block:

            @block.sync
            def _(sp):
                flag = sp.value_load(c["flag"][0:1, 0:1], min_val=0, max_val=1)
                with sp.If(flag == 0):
                    def load_rows(g):
                        if g >= 2:
                            sp.wait_ge(low_ready, GROUP * (g - 1))
                        sp.dma_start(staged[g % 2][:], table[g * cols:(g + 1) * cols, :].rearrange("(r p) c -> p r c", p=P)) \
                            .then_inc(tab_in[g % 2], 16)

                    def store(J):
                        sp.wait_ge(ready, J * GROUP + GROUP)
                        sp.dma_start(out[bass.ds(J * cols, cols), :].rearrange("(r p) c -> p r c", p=P),
                                     y[:, :, 0:D]).then_inc(stored, 16)

                    def body(J, finish):
                        for t in range(TILES):
                            g, at = divmod(t + ROWS_AHEAD, GROUP)
                            if not finish and at == 0 and 2 <= g < GROUPS:
                                load_rows(g)
                            if not isinstance(J, int) or t >= GROUP:
                                sp.wait_ge(weighted, J * TILES + t + 1 - GROUP)
                            sp.dma_start(cnt[:, t % GROUP, :], counts[t * P:(t + 1) * P, bass.ds(J * cols, cols)]) \
                                .then_inc(cnt_in[t % GROUP], 16)
                            if t == TILES - GROUP:
                                if finish:
                                    store(J - 1)
                                else:
                                    sp.wait_ge(low_ready, GROUP * (GROUPS - 1))
                                sp.dma_start(xm[:, :, 0:D], xmid[bass.ds(J * cols, cols), :].rearrange("(r p) c -> p r c", p=P)) \
                                    .then_inc(xm_in, 16)

                    load_rows(0)
                    load_rows(1)
                    groups(sp, body)
                    for r in range(GROUP):
                        row = ((GROUPS - 1) * GROUP + r) * P
                        sp.wait_ge(ready, (GROUPS - 1) * GROUP + r + 1)
                        sp.dma_start(out[row:row + P, :], y[:, r, 0:D]).then_inc(stored, 16)
                    sp.wait_ge(stored, 16 * (GROUPS - 1 + GROUP))
                with sp.Else():
                    edge_walk_sync(nc, sp, walk, src, dst, sums)

            @block.vector
            def _(dve):
                flag = dve.value_load(c["flag"][0:1, 0:1], min_val=0, max_val=1)
                with dve.If(flag == 0):
                    def scale_rows(m):
                        g, r = divmod(m, GROUP)
                        if r == 0:
                            dve.wait_ge(tab_in[g % 2], 16 * (g // 2) + 16)
                            nc.vector.tensor_copy(staged[g % 2][:, :, D], ones[:, 0:GROUP]).then_inc(one_set, 1)
                            dve.wait_ge(one_set, g + 1)
                            dve.wait_ge(exp_t, 1)
                        nc.vector.tensor_scalar(staged[g % 2][:, r, :], staged[g % 2][:, r, :], scale_col[:, m:m + 1], None,
                                                ALU.mult).then_inc(scaled, 1)

                    def rows_low(m):
                        dve.wait_ge(high_ready, m + 1)
                        nc.vector.tensor_tensor(low[:, m, :], staged[m // GROUP % 2][:, m % GROUP, :], high[:, m, :],
                                                ALU.subtract).then_inc(low_ready, 1)

                    def diagonals(q):
                        if q >= 2:
                            dve.wait_ge(spread, q - 1)
                        for t in range(q * per, min(TILES, (q + 1) * per)):
                            last = nc.vector.tensor_scalar(diag[:, q % 2, t % per * P:(t % per + 1) * P], c["ident"][:],
                                                           c["st"][:, t, 0:1], None, ALU.mult)
                        last.then_inc(diag_ready, 1)

                    dve.wait_ge(ones_ready, 1)
                    for q in range(GROUP):
                        diagonals(q)
                    for m in range(ROWS_AHEAD):
                        scale_rows(m)
                    for m in range(ROWS_AHEAD - 1):
                        rows_low(m)

                    def invert(J):
                        dve.wait_ge(used, J * TILES + TILES)
                        nc.vector.tensor_scalar(rd[:], acc[:, 0:GROUP, D], TINY, None, ALU.max).then_inc(clamped, 1)
                        dve.wait_ge(clamped, J + 1)
                        nc.vector.reciprocal(rd[:], rd[:]).then_inc(inverted, 1)

                    def add_and_stats(J, r):
                        n = J * GROUP + r + 1
                        dve.wait_ge(kept[r], J + 1)
                        dve.wait_ge(xm_in, 16 * J + 16)
                        nc.vector.tensor_tensor(y[:, r, 0:D], y[:, r, 0:D], xm[:, r, 0:D], ALU.add).then_inc(added, 1)
                        dve.wait_ge(added, n)
                        nc.vector.bn_stats(stats[:], y[:, r, 0:D]).then_inc(stats_ready, 1)
                        hold(dve, stats_ready, n)
                        nc.vector.bn_aggr(mv[:, r, :], stats[:]).then_inc(mean_ready, 1)
                        dve.wait_ge(mean_ready, n)
                        nc.vector.tensor_scalar(ve[:, r:r + 1], mv[:, r, 1:2], EPS, None, ALU.add).then_inc(var_ready, 1)

                    def normalise(J, r):
                        dve.wait_ge(rstd_ready, J * GROUP + r + 1)
                        nc.vector.tensor_scalar(y[:, r, 0:D], y[:, r, 0:D], mv[:, r, 0:1], rs[:, r:r + 1], ALU.subtract,
                                                ALU.mult).then_inc(ready, 1)

                    def weigh(J, t):
                        dve.wait_ge(exped, J * TILES + t + 1)
                        dve.wait_ge(cnt_in[t % GROUP], J * (GROUPS * 16) + (t // GROUP) * 16 + 16)
                        nc.vector.tensor_tensor(wgt[:, slot(t), :], wgt[:, slot(t), :], cnt[:, t % GROUP, :],
                                                ALU.mult).then_inc(weighted, 1)

                    def body(J, finish):
                        dve.wait_ge(s_ready, spreads if finish else -(-GROUP // per))
                        for t in range(TILES):
                            if finish and t == FINISH:
                                invert(J - 1)
                            free_block(dve, split, J, t)
                            nc.vector.tensor_scalar(wgt[:, slot(t), :], s_all[:, bass.ds(J * cols, cols)], c["st"][:, t, 1:2], 0.0,
                                                    ALU.add, ALU.max).then_inc(shifted, 1)
                            if t >= 1:
                                weigh(J, t - 1)
                            if not finish:
                                for q in late_spreads(t):
                                    diagonals(q)
                                if t + ROWS_AHEAD < TILES:
                                    scale_rows(t + ROWS_AHEAD)
                                if t + ROWS_AHEAD - 1 < TILES:
                                    rows_low(t + ROWS_AHEAD - 1)
                            r, odd = divmod(t - FINISH - 2, 2)
                            if finish and not odd and 0 <= r < GROUP:
                                add_and_stats(J - 1, r)
                            if finish and not odd and 0 <= r - 2 < GROUP:
                                normalise(J - 1, r - 2)
                        weigh(J, TILES - 1)

                    groups(dve, body)
                    invert(GROUPS - 1)
                    for r in range(GROUP):
                        add_and_stats(GROUPS - 1, r)
                        if r >= 1:
                            normalise(GROUPS - 1, r - 1)
                    normalise(GROUPS - 1, GROUP - 1)
                with dve.Else():
                    edge_walk_vector(nc, dve, walk)

            @block.scalar
            def _(act):
                flag = act.value_load(c["flag"][0:1, 0:1], min_val=0, max_val=1)
                with act.If(flag == 0):
                    def round_rows(m):
                        act.wait_ge(scaled, m + 1)
                        nc.scalar.copy(high[:, m, :], staged[m // GROUP % 2][:, m % GROUP, :]).then_inc(high_ready, 1)

                    def keep_spread(q):
                        act.wait_ge(spread, q + 1)
                        at = spread_cols(q)
                        nc.scalar.copy(s_all[:, at], acc[:, q % GROUP, 0:at.stop - at.start]).then_inc(s_ready, 1)

                    nc.scalar.activation(scale_col[:], c["st"][:, :, 1], ACT.Exp, scale=-ALPHA).then_inc(exp_t, 1)
                    for q in range(GROUP):
                        keep_spread(q)
                    for m in range(ROWS_AHEAD):
                        round_rows(m)

                    def keep(J):
                        act.wait_ge(inverted, J + 1)
                        act.wait_ge(stored, 16 * J)
                        for r in range(GROUP):
                            nc.scalar.activation(y[:, r, 0:D], acc[:, r, 0:D], ACT.Relu, scale=rd[:, r:r + 1]).then_inc(kept[r], 1)

                    def round_high(J, t):
                        act.wait_ge(weighted, J * TILES + t + 1)
                        free_block(act, used, J, t)
                        nc.scalar.copy(wh[:, slot(t), :], wgt[:, slot(t), :]).then_inc(rounded, 1)

                    def body(J, finish):
                        for t in range(TILES):
                            if finish and t == FINISH:
                                keep(J - 1)
                            act.wait_ge(shifted, J * TILES + t + 1)
                            nc.scalar.activation(wgt[:, slot(t), :], wgt[:, slot(t), :], ACT.Exp,
                                                 scale=-(1.0 - ALPHA)).then_inc(exped, 1)
                            if not finish:
                                for q in late_spreads(t):
                                    keep_spread(q)
                                if t + ROWS_AHEAD < TILES:
                                    round_rows(t + ROWS_AHEAD)
                            if t >= 1:
                                round_high(J, t - 1)
                        round_high(J, TILES - 1)

                    groups(act, body)
                    keep(GROUPS - 1)
                with act.Else():
                    edge_walk_scalar(nc, act, walk)

            @block.gpsimd
            def _(pool):
                flag = pool.value_load(c["flag"][0:1, 0:1], min_val=0, max_val=1)
                with pool.If(flag == 0):
                    nc.gpsimd.memset(ones[:], 1.0).then_inc(ones_ready, 1)
                    def root(J, r):
                        pool.wait_ge(var_ready, J * GROUP + r + 1)
                        nc.gpsimd.tensor_tensor(rs[:, r:r + 1], ve[:, r:r + 1], c["half"][:], ALU.pow).then_inc(rstd_ready, 1)

                    def body(J, finish):
                        for t in range(TILES):
                            pool.wait_ge(rounded, J * TILES + t + 1)
                            free_block(pool, used, J, t)
                            nc.gpsimd.tensor_tensor(wl[:, slot(t), :], wgt[:, slot(t), :], wh[:, slot(t), :],
                                                    ALU.subtract).then_inc(split, 1)
                            r, odd = divmod(t - FINISH - 2, 2)
                            if finish and not odd and 0 <= r < GROUP:
                                root(J - 1, r)

                    groups(pool, body)
                    for r in range(GROUP):
                        root(GROUPS - 1, r)
                with pool.Else():
                    edge_walk_pool(nc, pool, walk, table, sums)

            @block.tensor
            def _(pe):
                flag = pe.value_load(c["flag"][0:1, 0:1], min_val=0, max_val=1)
                with pe.If(flag == 0):
                    pe.wait_ge(ones_ready, 1)
                    for q in range(spreads):
                        pe.wait_ge(diag_ready, q + 1)
                        if q >= GROUP:
                            pe.wait_ge(s_ready, q - GROUP + 1)
                        at = spread_cols(q)
                        nc.tensor.matmul(acc[:, q % GROUP, 0:at.stop - at.start], ones[:], diag[:, q % 2, 0:at.stop - at.start],
                                         start=True, stop=True).then_inc(spread, 1)
                    pe.wait_ge(s_ready, spreads)

                    def body(J):
                        for t in range(TILES):
                            pe.wait_ge(low_ready, t + 1)
                            pe.wait_ge(split, J * TILES + t + 1)
                            for r in range(GROUP):
                                if t == 0:
                                    pe.wait_ge(kept[r], J)
                                a, b = wh[:, slot(t), r * P:(r + 1) * P], wl[:, slot(t), r * P:(r + 1) * P]
                                nc.tensor.matmul(acc[:, r, 0:HT], a, high[:, t, :], start=(t == 0), stop=False)
                                nc.tensor.matmul(acc[:, r, 0:HT], a, low[:, t, :], start=False, stop=False)
                                last = nc.tensor.matmul(acc[:, r, 0:HT], b, high[:, t, :], start=False, stop=(t == TILES - 1))
                            last.then_inc(used, 1)

                    group_steps(pe, body)
                with pe.Else():
                    edge_walk_tensor(nc, pe, walk)

_WEIGHTS = ["Wq", "Wk", "Wv", "O_w", "O_b", "ln1_w", "ln1_b", "f1_w", "f1_b", "f2_w", "f2_b", "ln2_w", "ln2_b",
            "gru_w_ih", "gru_w_hh", "gru_b_ih", "gru_b_hh"]


def build(nc, a, out):
    w = {n: a["L0_gnn_" + n] for n in _WEIGHTS}
    w["L1_W"], w["L1_a"] = a["L1_gnn_W"], a["L1_gnn_a"]

    def scratch(name, shape):
        return nc.dram_tensor(name, shape, F32, kind="Internal").ap()

    x1, xmid = scratch("x1_table", [ROWS, D]), scratch("xmid", [ROWS, D])
    table = scratch("node_table", [ROWS, HT])
    agg, sums = scratch("agg", [ROWS + P, D]), scratch("sums", [ROWS + P, HT])
    counts = nc.dram_tensor("edge_counts", [ROWS, ROWS], F16, kind="Internal").ap()
    with ExitStack() as ctx:
        kit = Kit(nc, ctx)
        c = lasting(nc, kit)
        with kit.stage() as edges:
            prepare_edges(nc, edges, c, a["dst"], a["pairs"])
            parts = edges.sb("x1_parts", [P, 2, TILES, D], F32R)
            with edges.stage() as k:
                attention_rows(nc, k, c, w, a["x"], x1, parts)
            with edges.stage() as k:
                count_and_sum(nc, k, c, parts, a["dst"], a["src"], x1, agg, counts)
        with kit.stage() as k:
            update_rows(nc, k, c, UpdateWeights(k, w), a["x"], x1, agg, xmid, table)
        with kit.stage() as k:
            weigh_and_sum(nc, k, c, a["src"], a["dst"], table, counts, sums, xmid, out)
        with kit.stage() as k:
            final_rows(nc, k, c, xmid, sums, out)


def _pad(a, n, fill):
    a = np.asarray(a)
    return np.concatenate([a, np.full((n - a.shape[0],) + a.shape[1:], fill, a.dtype)])


def kernel(**inputs):
    import concourse.bacc as _bacc
    from concourse.bass_utils import run_bass_kernel_spmd as _run

    host = dict(inputs)
    host["x"] = _pad(inputs["x"], ROWS, 0)
    host["src"] = _pad(inputs["src"], EDGES + P, ROWS - 1)
    host["dst"] = _pad(inputs["dst"], EDGES + P, ROWS - 1)
    host["pairs"] = np.stack([host["src"][:EDGES], host["dst"][:EDGES]], axis=-1).reshape(EDGES // EROW, 2 * EROW)
    nc = _bacc.Bacc("TRN2", target_bir_lowering=False, num_devices=1)
    arrays, aps = {}, {}
    for name, a in host.items():
        a = np.ascontiguousarray(a)
        arrays[f"in_{name}"] = a
        aps[name] = nc.dram_tensor(f"in_{name}", a.shape, mybir.dt.from_np(a.dtype), kind="ExternalInput").ap()
    out = nc.dram_tensor("out_rows", [ROWS, D], F32, kind="ExternalOutput").ap()
    build(nc, aps, out)
    r = _run(nc, [arrays], core_ids=[0])
    return r.results[0]["out_rows"][:N_NODES]
```
